# Optimizing a Trainium2 kernel written in Bass

```python
import numpy as np
import jax
import jax.numpy as jnp

def _softmax(x, axis=-1):
    return jax.nn.softmax(x, axis=axis)

def _gelu(x):
    return jax.nn.gelu(x, approximate=True)

def _silu(x):
    return jax.nn.silu(x)

def _sigmoid(x):
    return jax.nn.sigmoid(x)

def _layernorm(x, axis=-1, eps=1e-05):
    m = jnp.mean(x, axis=axis, keepdims=True)
    v = jnp.var(x, axis=axis, keepdims=True)
    return (x - m) / jnp.sqrt(v + eps)

def _scatter_add(tgt, idx, src, axis=0):
    return tgt.at[idx].add(src)

def _segment_sum(src, seg, n):
    return jax.ops.segment_sum(src, seg, n)
kernel_name = 'mk_gnn_resnorm_d4_gnn_r32_2d9e6f'

def setup_inputs(seed: int=0):
    np.random.seed(seed)
    _w = jnp.asarray

    def _rec_inputs():
        import jax
        import jax.numpy as jnp
        _gk = jax.random.key(seed)
        x = -0.0001006 + 1 * jax.random.normal(jax.random.fold_in(_gk, 1), (50000, 48), jnp.float32)
        src = jax.random.randint(jax.random.fold_in(_gk, 2), (50000,), 0, 50000, jnp.int32)
        dst = jnp.minimum((50000 * jax.random.uniform(jax.random.fold_in(_gk, 3), (50000,)) ** 2.0).astype(jnp.int32), 49999)
        _o = jnp.argsort(dst, stable=True)
        src = src[_o]
        dst = dst[_o]
        edge_attr_40 = jax.random.uniform(jax.random.fold_in(_gk, 13), (50000, 40), jnp.float32, 0.0, 1)
        edge_weight = jax.random.uniform(jax.random.fold_in(_gk, 15), (50000,), jnp.float32, 0.0, 6.99999)
        edge_weight1 = -0.000414295 + 0.999828 * jax.random.normal(jax.random.fold_in(_gk, 16), (50000, 1), jnp.float32)
        node_type_119 = jax.random.randint(jax.random.fold_in(_gk, 17), (50000,), 0, 119, jnp.int32)
        node_vec = jax.random.uniform(jax.random.fold_in(_gk, 18), (50000,), jnp.float32, 0.0, 1.49999)
        return (x, src, dst, edge_attr_40, edge_weight, edge_weight1, node_type_119, node_vec)
    x, src, dst, edge_attr_40, edge_weight, edge_weight1, node_type_119, node_vec = _rec_inputs()

    def _L0_gnn_setup():
        import jax, jax.numpy as jnp
        import numpy as np
        N_NODES = 3125
        N_EDGES = 50000
        N_CLASSES = 48
        key = jax.random.key(seed)
        k1, k2, k3, k4 = jax.random.split(key, 4)
        soft_label = jax.random.normal(k1, (N_NODES, N_CLASSES), dtype=jnp.float32)
        e = jax.random.normal(k2, (N_EDGES, 1), dtype=jnp.float32)
        src = jax.random.randint(k3, (N_EDGES,), 0, N_NODES)
        dst = jax.random.randint(k4, (N_EDGES,), 0, N_NODES)
        return {'soft_label': soft_label, 'e': e, 'src': src, 'dst': dst}
    _L0_gnn_all = _L0_gnn_setup()
    _L0_gnn_in = {k: v for k, v in _L0_gnn_all.items() if k in ()}
    del _L0_gnn_all

    def _L1_gnn_setup():
        import jax, jax.numpy as jnp
        import numpy as np
        CUTOFF = 6.0
        LN_EPS = 1e-05
        key = jax.random.key(seed)
        ks = jax.random.split(key, 16)
        N, E, H, R, NEL, G = (50000, 25000, 48, 40, 119, 32)
        inp = {'h': jax.random.normal(ks[0], (N, H), jnp.float32), 'edge_index': jax.random.randint(ks[1], (2, E), 0, N, jnp.int64), 'edge_attr': jax.random.uniform(ks[2], (E, R), jnp.float32), 'distances': jax.random.uniform(ks[3], (E,), jnp.float32) * 7.0, 'atom_z': jax.random.randint(ks[4], (N,), 0, NEL, jnp.int64), 'node_mult': jax.random.uniform(ks[5], (N,), jnp.float32) + 0.5, 'batch': jnp.zeros((N,), jnp.int64), 'W1': jax.random.normal(ks[6], (H, R), jnp.float32) / np.sqrt(R), 'b1': jax.random.normal(ks[7], (H,), jnp.float32) * 0.01, 'W2': jax.random.normal(ks[8], (H, H), jnp.float32) / np.sqrt(H), 'b2': jax.random.normal(ks[9], (H,), jnp.float32) * 0.01, 'emb': jax.random.normal(ks[10], (NEL, G), jnp.float32) * 0.01, 'adaptW': jax.random.normal(ks[11], (G, G), jnp.float32) * 0.01, 'gamma': jnp.ones((H,), jnp.float32), 'beta': jnp.zeros((H,), jnp.float32)}
        return inp
    _L1_gnn_all = _L1_gnn_setup()
    _L1_gnn_in = {k: v for k, v in _L1_gnn_all.items() if k in ('W1', 'b1', 'W2', 'b2', 'emb', 'adaptW', 'gamma', 'beta')}
    del _L1_gnn_all

    def _L2_gnn_setup():
        import jax, jax.numpy as jnp
        import numpy as np
        N_NODES = 50000
        N_EDGES = 50000
        D_IN = 48
        D_OUT = 48
        key = jax.random.key(seed)
        k1, k2, k3, k4 = jax.random.split(key, 4)
        features = jax.random.normal(k1, (N_NODES, D_IN), dtype=jnp.float32)
        src = jax.random.randint(k2, (N_EDGES,), 0, N_NODES, dtype=jnp.int64)
        dst = jax.random.randint(k3, (N_EDGES,), 0, N_NODES, dtype=jnp.int64)
        std = np.sqrt(2.0 / (D_IN + D_OUT))
        W = jax.random.normal(k4, (D_OUT, D_IN), dtype=jnp.float32) * std
        b = jnp.zeros((D_OUT,), dtype=jnp.float32)
        return {'features': features, 'src': src, 'dst': dst, 'W': W, 'b': b}
    _L2_gnn_all = _L2_gnn_setup()
    _L2_gnn_in = {k: v for k, v in _L2_gnn_all.items() if k in ('W', 'b')}
    del _L2_gnn_all

    def _L3_gnn_setup():
        import jax, jax.numpy as jnp
        import numpy as np
        N_NODES = 3125
        N_EDGES = 50000
        IN_CH = 48
        OUT_CH = 48
        BN_EPS = 1e-05
        key = jax.random.key(seed)
        k1, k2, k3, k4 = jax.random.split(key, 4)
        x = jax.random.normal(k1, (N_NODES, IN_CH), dtype=jnp.float32)
        edge_index = jax.random.randint(k2, (2, N_EDGES), 0, N_NODES, dtype=jnp.int32)
        W = jax.random.normal(k3, (IN_CH, OUT_CH), dtype=jnp.float32) * (1.0 / np.sqrt(IN_CH))
        b = jnp.zeros((OUT_CH,), dtype=jnp.float32)
        gamma = jnp.ones((OUT_CH,), dtype=jnp.float32)
        beta = jnp.zeros((OUT_CH,), dtype=jnp.float32)
        return {'x': x, 'edge_index': edge_index, 'W': W, 'b': b, 'gamma': gamma, 'beta': beta}
    _L3_gnn_all = _L3_gnn_setup()
    _L3_gnn_in = {k: v for k, v in _L3_gnn_all.items() if k in ('W', 'b', 'gamma', 'beta')}
    del _L3_gnn_all
    return {'x': x, 'src': src, 'dst': dst, 'edge_attr_40': edge_attr_40, 'edge_weight': edge_weight, 'edge_weight1': edge_weight1, 'node_type_119': node_type_119, 'node_vec': node_vec, 'L1_gnn_W1': _L1_gnn_in['W1'], 'L1_gnn_b1': _L1_gnn_in['b1'], 'L1_gnn_W2': _L1_gnn_in['W2'], 'L1_gnn_b2': _L1_gnn_in['b2'], 'L1_gnn_emb': _L1_gnn_in['emb'], 'L1_gnn_adaptW': _L1_gnn_in['adaptW'], 'L1_gnn_gamma': _L1_gnn_in['gamma'], 'L1_gnn_beta': _L1_gnn_in['beta'], 'L2_gnn_W': _L2_gnn_in['W'], 'L2_gnn_b': _L2_gnn_in['b'], 'L3_gnn_W': _L3_gnn_in['W'], 'L3_gnn_b': _L3_gnn_in['b'], 'L3_gnn_gamma': _L3_gnn_in['gamma'], 'L3_gnn_beta': _L3_gnn_in['beta']}

def reference(x, src, dst, edge_attr_40, edge_weight, edge_weight1, node_type_119, node_vec, L1_gnn_W1, L1_gnn_b1, L1_gnn_W2, L1_gnn_b2, L1_gnn_emb, L1_gnn_adaptW, L1_gnn_gamma, L1_gnn_beta, L2_gnn_W, L2_gnn_b, L3_gnn_W, L3_gnn_b, L3_gnn_gamma, L3_gnn_beta):
    import jax
    import jax.numpy as jnp

    def _L0_gnn_ref(soft_label, e, src, dst):
        import jax, jax.numpy as jnp
        import numpy as np
        N_NODES = 3125
        N_EDGES = 50000
        N_CLASSES = 48
        N = soft_label.shape[0]
        logits = e[:, 0]
        seg_max = jax.ops.segment_max(logits, dst, num_segments=N)
        seg_max = jnp.where(jnp.isfinite(seg_max), seg_max, 0.0)
        ex = jnp.exp(logits - seg_max[dst])
        seg_sum = jax.ops.segment_sum(ex, dst, num_segments=N)
        a = ex / seg_sum[dst]
        msg = soft_label[src] * a[:, None]
        rst = jax.ops.segment_sum(msg, dst, num_segments=N)
        return jax.nn.elu(rst)

    def _L1_gnn_ref(h, edge_index, edge_attr, distances, atom_z, node_mult, batch, W1, b1, W2, b2, emb, adaptW, gamma, beta):
        import jax, jax.numpy as jnp
        import numpy as np
        CUTOFF = 6.0
        LN_EPS = 1e-05
        src, dst = (edge_index[0], edge_index[1])
        N = h.shape[0]
        gate = jax.nn.silu(edge_attr @ W1.T + b1) @ W2.T + b2
        ei = emb[atom_z[src]]
        ej = emb[atom_z[dst]]
        adapt_logit = jnp.sum(ei * (ej @ adaptW.T), axis=-1, keepdims=True)
        gate = gate + adapt_logit
        cw = jnp.where(distances < CUTOFF, 0.5 * (jnp.cos(jnp.pi * distances / CUTOFF) + 1.0), 0.0)
        mj = node_mult[dst]
        msg = gate * h[dst] * (cw * mj)[:, None]
        agg = jax.ops.segment_sum(msg, src, num_segments=N)
        tot = jax.ops.segment_sum(mj, src, num_segments=N)
        agg = agg / jnp.clip(tot, 1e-08, None)[:, None]
        x = h + agg
        mu = jnp.mean(x, axis=-1, keepdims=True)
        var = jnp.mean(jnp.square(x - mu), axis=-1, keepdims=True)
        return (x - mu) / jnp.sqrt(var + LN_EPS) * gamma + beta

    def _L2_gnn_ref(features, src, dst, W, b):
        import jax, jax.numpy as jnp
        import numpy as np
        N_NODES = 50000
        N_EDGES = 50000
        D_IN = 48
        D_OUT = 48
        n = features.shape[0]
        ones = jnp.ones(src.shape[0], dtype=features.dtype)
        out_deg = jax.ops.segment_sum(ones, src, num_segments=n)
        in_deg = jax.ops.segment_sum(ones, dst, num_segments=n)
        ci = jax.lax.rsqrt(jnp.maximum(out_deg, 1.0))
        cj = jax.lax.rsqrt(jnp.maximum(in_deg, 1.0))
        msg = features[src] * ci[src][:, None]
        agg = jax.ops.segment_sum(msg, dst, num_segments=n) * cj[:, None]
        h = jnp.where(in_deg[:, None] > 0, agg, features)
        out = jax.nn.relu(h @ W.T + b)
        return out

    def _L3_gnn_ref(x, edge_index, W, b, gamma, beta):
        import jax, jax.numpy as jnp
        import numpy as np
        N_NODES = 3125
        N_EDGES = 50000
        IN_CH = 48
        OUT_CH = 48
        BN_EPS = 1e-05
        N = x.shape[0]
        loops = jnp.arange(N, dtype=edge_index.dtype)
        src = jnp.concatenate([edge_index[0], loops])
        dst = jnp.concatenate([edge_index[1], loops])
        deg = jax.ops.segment_sum(jnp.ones_like(dst, dtype=x.dtype), dst, num_segments=N)
        dinv = jax.lax.rsqrt(deg)
        norm = dinv[src] * dinv[dst]
        h = x @ W
        msg = h[src] * norm[:, None]
        agg = jax.ops.segment_sum(msg, dst, num_segments=N) + b
        mean = jnp.mean(agg, axis=0)
        var = jnp.mean(jnp.square(agg - mean), axis=0)
        y = (agg - mean) * jax.lax.rsqrt(var + BN_EPS) * gamma + beta
        return jax.nn.relu(y)
    edge_index = jnp.stack([src, dst])
    batch0 = jnp.zeros((50000,), jnp.int32)
    x = _layernorm(x + _L0_gnn_ref(x, edge_weight1, src, dst), axis=-1)
    x = _layernorm(x + _L1_gnn_ref(x, edge_index, edge_attr_40, edge_weight, node_type_119, node_vec, batch0, L1_gnn_W1, L1_gnn_b1, L1_gnn_W2, L1_gnn_b2, L1_gnn_emb, L1_gnn_adaptW, L1_gnn_gamma, L1_gnn_beta), axis=-1)
    x = _layernorm(x + _L2_gnn_ref(x, src, dst, L2_gnn_W, L2_gnn_b), axis=-1)
    x = _layernorm(x + _L3_gnn_ref(x, edge_index, L3_gnn_W, L3_gnn_b, L3_gnn_gamma, L3_gnn_beta), axis=-1)
    return x

_drawn_inputs = setup_inputs


def setup_inputs(seed=0):
    import zlib

    import numpy as np

    out = dict(_drawn_inputs(seed))
    spreads = {'L1_gnn_gamma': (1.0, 0.2),
     'L1_gnn_beta': (0.0, 0.1),
     'L2_gnn_b': (0.0, 0.1),
     'L3_gnn_b': (0.0, 2.0),
     'L3_gnn_gamma': (1.0, 0.2),
     'L3_gnn_beta': (0.0, 0.1)}
    factors = {'node_vec': 11.54,
     'L1_gnn_b1': 38.997,
     'L1_gnn_b2': 24.399,
     'L1_gnn_emb': 64.0,
     'L1_gnn_adaptW': 64.0,
     'edge_attr_40': 2.685}
    for name, (base, spread) in spreads.items():
        noise = np.random.default_rng([zlib.crc32(name.encode()), seed]).standard_normal(out[name].shape)
        drawn = base * np.exp(spread * noise) if base else spread * noise
        out[name] = jnp.asarray(drawn.astype(out[name].dtype))
    for name, factor in factors.items():
        out[name] = (out[name] * factor).astype(out[name].dtype)
    return out
```

```python
import concourse.bass as bass
from concourse import mybir
from contextlib import ExitStack

F32 = mybir.dt.float32
I32 = mybir.dt.int32
ALU = mybir.AluOpType
ACT = mybir.ActivationFunctionType
AX = mybir.AxisListType

P = 128
N = 50000
H = 48
GE = 32
R = 40
NEL = 119
T = 392
FULL = N // P
REST = N - FULL * P
U = 8
IT = T // U
Q = 4
W = 4
SEGS = [(0, 17, 2), (17, 34, 3), (34, IT, 4)]
TA = T + W
C0 = H + 1
C1 = H + 2
K0 = H + GE
K1 = H + GE + 1
TABLES = 4
CH = 14
NC = T // CH
BIG = 2.0 ** 120
EPS = 1e-5
AW = 4536
PI = 3.141592653589793


class Tally:

    def __init__(self, sem):
        self.sem, self.base, self.per, self.it, self.k = sem, 0, 0, 0, 0

    def value(self):
        return self.base + self.k + (self.it * self.per if self.per else 0)

    def add(self, ins, n=1):
        ins.then_inc(self.sem, n)
        self.k += n
        return self.value()

    def turn(self, it, per):
        if not self.per:
            self.base += self.k
        self.it, self.per, self.k = it, per, 0

    def close(self, turns):
        self.base += turns * self.per
        self.per, self.it, self.k = 0, 0, 0


def is_reg(v):
    return not isinstance(v, int)


def wait(eng, sem, v):
    if is_reg(v) or v > 0:
        eng.wait_ge(sem, v)


def turns(eng, n, body):
    body(0)
    with eng.Fori(1, n - 1) as i:
        body(i)
    body(n - 1)


def segments(eng, body):
    for n, (a, b, w) in enumerate(SEGS):
        if a == 0:
            body(0, w, w)
        with eng.Fori(max(a, 1), b - 1) as i:
            body(i, w, w)
        body(b - 1, w, SEGS[n + 1][2] if n + 1 < len(SEGS) else None)


def build(nc, x, src, dst, attr, ew, ew1, ntype, nvec, W1, b1, W2, b2, emb, adaptW, gamma, beta,
          L2W, L2b, L3W, L3b, L3g, L3be, out):
    ctx = ExitStack()
    with ctx:
        def sb(name, shape, dt=F32):
            return ctx.enter_context(nc.sbuf_tensor(name, shape, dt))

        def sem(name):
            return ctx.enter_context(nc.semaphore(name))

        def dram(name, shape):
            return nc.dram_tensor(name, shape, F32, kind="Internal").ap()

        tab0 = dram("tab0", (P * T, K0))
        tab1 = dram("tab1", (P * T, K1))
        tab2 = dram("tab2", (P * T, H))
        tab3 = dram("tab3", (P * T, H))
        aggs = [dram(f"agg{k}", (P * T + P, C1)) for k in range(TABLES)]
        rows_d = [dram(f"rows{a}", (T * P,)) for a in range(3)]
        srcemb = dram("srcemb", (P, T * GE))
        tab0v = tab0.rearrange("(p j) c -> p j c", p=P)
        tab1v = tab1.rearrange("(p j) c -> p j c", p=P)
        tab2v = tab2.rearrange("(p j) c -> p j c", p=P)
        tab3v = tab3.rearrange("(p j) c -> p j c", p=P)
        aggv = [a[0:P * T, :].rearrange("(p j) c -> p (j c)", p=P) for a in aggs]

        X = sb("X", [P, T, H])
        ACC = sb("ACC", [P, TA * C0])
        acc0 = ACC[:, :].rearrange("p (j c) -> p j c", c=C0)
        acc = ACC[:, 0:TA * H].rearrange("p (j c) -> p j c", c=H)
        cols = sb("cols", [P, 5, T])
        dcol, scol, lcol, ecol, mcol = (cols[:, a, :] for a in range(5))
        relc = sb("relc", [P, T])
        gsrc = sb("gsrc", [P, T], I32)
        gdst = sb("gdst", [P, T], I32)
        base = sb("base", [1, T], I32)
        indeg = sb("indeg", [P, TA])
        smax = sb("smax", [P, TA])
        ident = sb("ident", [P, P])
        tril = sb("tril", [P, P])
        ones = sb("ones", [P, P])
        iota = sb("iota", [P, W * P])
        pcol = sb("pcol", [P, 8])
        trash, firstv, halfpi, epsc, valid = (pcol[:, a:a + 1] for a in range(5))
        idx = sb("idx", [P, 2, Q], I32)
        flag = sb("flag", [1, 1], I32)
        flagr = sb("flagr", [P, 1])
        flagf = sb("flagf", [1, P])
        wsm = sb("wsm", [P, 864])
        W1T = wsm[0:R, 0:H]
        W2T = wsm[0:H + 1, 48:96]
        L2WT = wsm[0:H + 1, 96:144]
        L3Ws = wsm[0:H, 144:192]
        EU = wsm[0:NEL, 192:256]
        b1c = wsm[0:H, 256:257]
        embT = wsm[0:GE, 257:257 + NEL]
        adT = wsm[0:GE, 376:408]
        w1raw = wsm[0:H, 408:448]
        w2raw = wsm[0:H, 448:496]
        l2raw = wsm[0:H, 496:544]
        adraw = wsm[0:GE, 544:576]
        b1raw = wsm[0:1, 576:624]
        vecs = [wsm[:, 624 + 48 * a:672 + 48 * a] for a in range(5)]

        A1 = sb("A1", [P, AW])
        idxs = sb("idxs", [P, 2, Q], I32)

        RI = ACC[:, 0:1024].bitcast(I32).rearrange("p (a b e) -> p a b e", a=2, b=4)
        RF = ACC[:, 1024:3584].rearrange("p (a b e) -> p a b e", a=5, b=4)
        zb = [ACC[0:NEL, 4096 + 1024 * s:5120 + 1024 * s].bitcast(I32) for s in range(2)]
        zoh = [ACC[0:NEL, 6144 + 1024 * s:7168 + 1024 * s] for s in range(2)]
        st0 = [ACC[:, 8192 + 640 * s:8832 + 640 * s].rearrange("p (t c) -> p t c", t=U) for s in range(2)]
        stu = [ACC[:, 9600 + 264 * s:9864 + 264 * s].rearrange("p (t c) -> p t c", t=U) for s in range(2)]

        o = 0

        def cut(n):
            nonlocal o
            o += n
            assert o <= AW, o
            return A1[:, o - n:o]

        gat = cut(U * K1).rearrange("p (k c) -> p k c", k=U)
        oneh = sb("oneh", [P, U, W * P])
        wrow = cut(U * 52).rearrange("p (k c) -> p k c", k=U)
        drow = [cut(Q * P) for _ in range(2)]
        lrow = [cut(Q * P) for _ in range(2)]
        tmpc, tmpd, tmpi = drow[0][:, 0:T], drow[1][:, 0:T], lrow[0][:, 0:T].bitcast(I32)
        dtra = lcol
        tmpr = lrow[1][:, 0:T]
        cj = lcol
        resc = mcol
        t1 = cut(Q * P).rearrange("p (k c) -> p k c", k=Q)
        mloc = cut(2 * Q).rearrange("p (g k) -> p g k", g=2)
        fsum = cut(2 * Q).rearrange("p (g k) -> p g k", g=2)
        lm = cut(2 * Q).rearrange("p (g k) -> p g k", g=2)
        cand = cut(W * Q)
        dif = cut(2 * 2 * W * Q).rearrange("p (g h k) -> p g h k", g=2, h=2)
        prod = cut(2 * W * C0)
        junk = prod[:, 0:P]
        zero = cut(U * C1)
        att = [ACC[:, 160 * s:160 * s + 160].rearrange("p (k c) -> p k c", k=Q) for s in range(2)]
        vse = [ACC[:, 320 + 128 * s:448 + 128 * s].rearrange("p (k c) -> p k c", k=Q) for s in range(2)]
        attT = [ACC[0:R, 600 + 512 * s:1112 + 512 * s] for s in range(2)]
        hid = [ACC[0:H + 1, 1700 + 512 * s:2212 + 512 * s] for s in range(2)]
        msg = [ACC[:, 2800 + 200 * s:3000 + 200 * s].rearrange("p (k c) -> p k c", k=Q) for s in range(2)]
        osum = [ACC[:, 3200 + 200 * s:3400 + 200 * s].rearrange("p (k c) -> p k c", k=Q) for s in range(2)]
        eqm = [ACC[:, 3600 + 512 * s:4112 + 512 * s].rearrange("p (k c) -> p k c", k=Q) for s in range(2)]
        uv = ACC[:, 4700:4828].rearrange("p (k c) -> p k c", k=Q)
        m1 = ACC[:, 4900:5092].rearrange("p (k c) -> p k c", k=Q)
        m2 = ACC[:, 5100:5292].rearrange("p (k c) -> p k c", k=Q)
        adp = ACC[:, 5300:5304]
        qmu = ACC[:, 5304:5308]
        rank = ACC[:, 5308:5316].rearrange("p (g k) -> p g k", g=2)
        idf = ACC[:, 5316:5320]
        aload = [[ACC[:, 5400 + 700 * (4 * s + k):6100 + 700 * (4 * s + k)] for k in range(TABLES)] for s in range(2)]
        NCOL = CH * H
        ybuf, sbuf_, tbuf, ubuf = (A1[:, NCOL * a:NCOL * (a + 1)] for a in range(4))
        stg = [A1[:, NCOL * (4 + s):NCOL * (5 + s)] for s in range(2)]
        small = [A1[:, NCOL * 6 + 16 * a:NCOL * 6 + 16 * a + CH] for a in range(8)]
        hT = oneh[0:H + 1, :, :].rearrange("p k c -> p (k c)")[:, 0:1024]
        hT2 = oneh[0:H + 1, :, :].rearrange("p k c -> p (k c)")[:, 1024:2048]

        psum = ctx.enter_context(nc.psum_tensor("psum", [P, 8, 512], F32))

        CR = 52
        states = dram("states", (P * T + P, CR))
        statev = states[0:P * T, :].rearrange("(p j) c -> p (j c)", p=P)
        RA = oneh[:, :, :].rearrange("p k c -> p (k c)")
        req, rt1, rjunk, rdk, rdl = (RA[:, a * P:(a + 1) * P] for a in range(5))
        rw, rst, rnew, rs_ = (RA[:, 640 + CR * a:640 + CR * (a + 1)] for a in range(4))
        rc = [RA[:, 848 + a:849 + a] for a in range(16)]
        rd2 = RA[:, 864:866]
        rdf = RA[:, 868:868 + 2 * CH]
        rchunk = RA[:, 1024:1024 + CH * CR]
        rzero = RA[:, 2048:2048 + CH * CR]

        r_go, r_zero, r_init, r_ld, r_use, r_pl, r_x, r_ix, r_st, r_q, r_bk, r_lm, r_ex, r_w, r_mm, r_df, r_dx, \
            r_new, r_sc, r_dv, r_mf, r_mx = (sem("r_" + n) for n in (
                "go", "zero", "init", "ld", "use", "pl", "x", "ix", "st", "q", "bk", "lm", "ex", "w", "mm", "df",
                "dx", "new", "sc", "dv", "mf", "mx"))
        s_const = sem("s_const")
        s_pad = sem("s_pad")
        s_rows = sem("s_rows")
        s_w = sem("s_w")
        s_rowf = sem("s_rowf")
        s_rowd = sem("s_rowd")
        s_tp = sem("s_tp")
        s_cp = sem("s_cp")
        s_bb = sem("s_bb")
        s_flag = sem("s_flag")
        s_zl = [sem(f"s_zl{s}") for s in range(2)]
        s_zo, s_zm, s_ze, s_zx = sem("s_zo"), sem("s_zm"), sem("s_ze"), sem("s_zx")
        s_zs = [sem(f"s_zs{s}") for s in range(2)]
        s_prep = sem("s_prep")
        s_dv = sem("s_dv")
        s_pl = sem("s_pl")
        s_tick = sem("s_tick")
        s_ask, s_ans = sem("s_ask"), sem("s_ans")
        s_ga = [sem(f"s_ga{k}") for k in range(U)]
        s_rl = [sem(f"s_rl{g}") for g in range(2)]
        s_vs = [sem(f"s_vs{g}") for g in range(2)]
        s_edge, s_oh, s_wr, s_sc0, s_st, s_mm, s_df, s_dx, s_cmb, s_rdone = (sem(n) for n in (
            "s_edge", "s_oh", "s_wr", "s_scl", "s_st", "s_mm", "s_df", "s_dx", "s_cmb", "s_rdone"))
        s_zero = sem("s_zero")
        s_n0 = sem("s_n0")
        s_t1 = sem("s_t1")
        s_al = [sem(f"s_al{g}") for g in range(2)]
        s_at, s_ac, s_hd, s_si, s_gt, s_ms, s_eq, s_os, s_oc, s_sx, s_rs = (sem(n) for n in (
            "s_at", "s_ac", "s_hd", "s_si", "s_gt", "s_ms", "s_eq", "s_os", "s_oc", "s_sx", "s_rs"))
        s_sc = [sem(f"s_sc{k}") for k in range(U)]
        s_ld = [sem(f"s_ld{g}") for g in range(2)]
        s_sum, s_n1 = sem("s_sum"), sem("s_n1")
        s_t2 = [sem(f"s_t2{g}") for g in range(2)]
        s_acz = sem("s_acz")
        s_oh2, s_mm2, s_cm2, s_gu2 = [sem("s_oh2"), sem("s_oh3")], [sem("s_mm2"), sem("s_mm3")], \
            [sem("s_cm2"), sem("s_cm3")], sem("s_gu2")
        s_na, s_ntp, s_ncp, s_nmm = sem("s_na"), sem("s_ntp"), sem("s_ncp"), sem("s_nmm")
        s_n2 = sem("s_n2")
        s_t3 = sem("s_t3")
        s_bn, s_bm = sem("s_bn"), sem("s_bm")
        s_n3 = sem("s_n3")
        s_out = sem("s_out")

        block = ctx.enter_context(nc.Block())

        @block.sync
        def _(sp):
            def residual(r):
                sp.wait_ge(s_flag, 3)
                more = sp.value_load(flag[0:1, 0:1], min_val=0, max_val=T * P)
                with sp.If(more > 0):
                    sp.wait_ge(r_zero, r + 1)
                    with sp.Fori(0, NC) as c:
                        sp.dma_start(statev[:, bass.ds(c * (CH * CR), CH * CR)], rzero).then_inc(r_init, 16)
                    sp.dma_start(states[P * T:P * T + P, :], rzero[:, 0:CR]).then_inc(r_init, 16)
                    sp.wait_ge(r_sc, 16 * T * (r + 1))
                    sp.dma_start(rchunk, statev[:, 0:CH * CR]).then_inc(r_ld, 16)
                    with sp.Fori(1, NC) as c:
                        sp.wait_ge(r_use, c * 1 + NC * r)
                        sp.dma_start(rchunk, statev[:, bass.ds(c * (CH * CR), CH * CR)]).then_inc(r_ld, 16)

            sp.wait_ge(s_pad, 1)
            sp.dma_start(RI[0:6, 0, 3, :], dst[384 * P:FULL * P].rearrange("(p e) -> p e", e=P)).then_inc(s_rows, 16)
            for a, arr in enumerate((dst, src, ew1.rearrange("e a -> (e a)"), ew, nvec)):
                to = RI[:, a] if a < 2 else RF[:, a]
                sp.dma_start(to[:, 0:3, :], arr[0:384 * P].rearrange("(b p e) -> p b e", b=3, e=P)).then_inc(s_rows, 16)
                if a:
                    sp.dma_start(to[0:6, 3, :], arr[384 * P:FULL * P].rearrange("(p e) -> p e", e=P)).then_inc(s_rows, 16)
                sp.dma_start(to[6:7, 3, 0:REST], arr[FULL * P:N].rearrange("(a e) -> a e", a=1)).then_inc(s_rows, 16)
            for to, of in ((w1raw, W1), (w2raw, W2), (l2raw, L2W), (adraw, adaptW),
                           (EU[:, 0:GE], emb), (L3Ws, L3W),
                           (W2T[H:H + 1, :], b2.rearrange("(a n) -> a n", a=1)),
                           (L2WT[H:H + 1, :], L2b.rearrange("(a n) -> a n", a=1)),
                           (b1raw, b1.rearrange("(a n) -> a n", a=1))):
                sp.dma_start(to, of).then_inc(s_w, 16)
            for a, v in enumerate((gamma, beta, L3b, L3g, L3be)):
                sp.dma_start(vecs[a], v.partition_broadcast(P)).then_inc(s_w, 16)
            sp.dma_start(X[:, 0:FULL, :], x[0:FULL * P, :].rearrange("(j p) c -> p j c", p=P)).then_inc(s_rows, 16)
            sp.dma_start(X[0:REST, FULL, :], x[FULL * P:N, :]).then_inc(s_rows, 16)
            sp.wait_ge(s_rowf, 1)
            for a in range(3):
                v = rows_d[a].rearrange("(t e) -> t e", e=P)
                sp.dma_start(v[0:384, :].rearrange("(b p) e -> p b e", b=3), RF[:, a, 0:3, :]).then_inc(s_rowd, 16)
                sp.dma_start(v[384:T, :], RF[0:U, a, 3, :]).then_inc(s_rowd, 16)

            def load_z(m, s):
                n = min(U * P, N - U * P * (IT - 1)) if (not is_reg(m) and m == IT - 1) else U * P
                wait(sp, s_zo, m - 1)
                sp.dma_start(zb[s][:, 0:n], ntype[bass.ds(m * (U * P), n)].partition_broadcast(NEL)).then_inc(s_zl[s], 16)

            def store_z(m, s):
                sp.wait_ge(s_ze, m * 1 + 1)
                sp.wait_ge(s_zx, m * 1 + 1)
                sp.dma_start(tab0v[:, bass.ds(m * U, U), :], st0[s]).then_inc(s_zs[s], 16)
                sp.dma_start(tab1v[:, bass.ds(m * U, U), H:K1], stu[s]).then_inc(s_zs[s], 16)

            sp.wait_ge(s_pad, 2)
            load_z(0, 0)
            load_z(1, 1)
            store_z(0, 0)
            load_z(2, 0)
            store_z(1, 1)
            with sp.Fori(1, IT // 2 - 1) as q:
                load_z(q * 2 + 1, 1)
                store_z(q * 2, 0)
                load_z(q * 2 + 2, 0)
                store_z(q * 2 + 1, 1)
            load_z(IT - 2, 1)
            store_z(IT - 3, 0)
            load_z(IT - 1, 0)
            store_z(IT - 2, 1)
            store_z(IT - 1, 0)

            def rows0(it):
                for g in range(2):
                    n = it * 2 + g
                    wait(sp, s_rdone, n - 1)
                    for to, a in ((drow[g], 0), (lrow[g], 2)):
                        sp.dma_start(to, rows_d[a][bass.ds(n * (Q * P), Q * P)].partition_broadcast(P)).then_inc(s_rl[g], 16)

            def side0(it):
                for g in range(2):
                    for k in range(Q):
                        sp.wait_ge(s_ga[g * Q + k], it * 16 + 16)
                    sp.dma_start(srcemb[:, bass.ds(it * (U * GE) + g * Q * GE, Q * GE)].rearrange("p (k c) -> p k c", k=Q),
                                 gat[:, g * Q:(g + 1) * Q, H:K0]).then_inc(s_vs[g], 16)
                for k in range(TABLES):
                    sp.dma_start(aggv[k][:, bass.ds(it * (U * C1), U * C1)], zero[:, :]).then_inc(s_zero, 16)

            sp.wait_ge(s_rowd, 96)
            sp.wait_ge(s_acz, 1)
            for k in range(TABLES):
                sp.dma_start(aggs[k][P * T:P * T + P, :], zero[:, 0:C1]).then_inc(s_zero, 16)
            rows0(0)
            with sp.Fori(0, IT - 1) as it:
                rows0(it + 1)
                side0(it)
            side0(IT - 1)

            residual(0)

            def out0(c):
                sp.wait_ge(s_n0, c * 1 + 1)
                sp.dma_start(tab1v[:, bass.ds(c * CH, CH), 0:H], X[:, bass.ds(c * CH, CH), :]).then_inc(s_t1, 16)
            turns(sp, NC, out0)

            def load1(it, last=False):
                for g in range(2):
                    n = it * 2 + g
                    tail = last and g == 1
                    wait(sp, s_at, n - 1)
                    wait(sp, s_rs, n - 1)
                    if tail:
                        r = FULL - (T - Q)
                        sp.dma_start(att[g][:, 0:r, :], attr[(T - Q) * P:FULL * P, :].rearrange("(k p) c -> p k c", p=P)).then_inc(s_al[g], 16)
                        sp.dma_start(att[g][0:REST, r, :], attr[FULL * P:N, :]).then_inc(s_al[g], 16)
                    else:
                        sp.dma_start(att[g], attr[bass.ds(n * (Q * P), Q * P), :].rearrange("(k p) c -> p k c", p=P)).then_inc(s_al[g], 16)
                    sp.dma_start(vse[g], srcemb[:, bass.ds(n * (Q * GE), Q * GE)].rearrange("p (k c) -> p k c", k=Q)).then_inc(s_al[g], 16)
                    sp.dma_start(drow[g], rows_d[1][bass.ds(n * (Q * P), Q * P)].partition_broadcast(P)).then_inc(s_al[g], 16)
            for g in range(2):
                sp.wait_ge(s_vs[g], 16 * IT)
            load1(0)
            with sp.Fori(1, IT - 1) as it:
                load1(it)
            load1(IT - 1, True)

            for k in range(U):
                sp.wait_ge(s_sc[k], 16 * IT)

            def load_a(c, s):
                wait(sp, s_sum, c - 1)
                for k in range(TABLES):
                    sp.dma_start(aload[s][k], aggv[k][:, bass.ds(c * (CH * C1), CH * C1)]).then_inc(s_ld[s], 16)

            def store_a(c, s):
                sp.wait_ge(s_n1, c * 1 + 1)
                sp.dma_start(tab2v[:, bass.ds(c * CH, CH), :], stg[s].rearrange("p (j c) -> p j c", c=H)).then_inc(s_t2[s], 16)
            load_a(0, 0)
            load_a(1, 1)
            store_a(0, 0)
            load_a(2, 0)
            store_a(1, 1)
            with sp.Fori(1, NC // 2 - 1) as q:
                load_a(q * 2 + 1, 1)
                store_a(q * 2, 0)
                load_a(q * 2 + 2, 0)
                store_a(q * 2 + 1, 1)
            load_a(NC - 1, 1)
            store_a(NC - 2, 0)
            store_a(NC - 1, 1)

            residual(1)

            def out2(it):
                sp.wait_ge(s_n2, it * 1 + 1)
                sp.dma_start(tab3v[:, bass.ds(it * U, U), :], acc[:, bass.ds(it * U, U), :]).then_inc(s_t3, 16)
            turns(sp, IT, out2)

            residual(2)

            def out3(c):
                sp.wait_ge(s_n3, c * 1 + 1)
                sp.dma_start(out[bass.ds(c * (CH * P), CH * P), :].rearrange("(j p) c -> p j c", p=P),
                             X[:, bass.ds(c * CH, CH), :]).then_inc(s_out, 16)
            with sp.Fori(0, NC - 1) as c:
                out3(c)
            sp.wait_ge(s_n3, NC)
            j = (NC - 1) * CH
            sp.dma_start(out[j * P:FULL * P, :].rearrange("(j p) c -> p j c", p=P), X[:, j:FULL, :]).then_inc(s_out, 16)
            sp.dma_start(out[FULL * P:N, :], X[0:REST, FULL, :]).then_inc(s_out, 16)
            sp.wait_ge(s_out, 16 * (NC + 1))
            sp.wait_ge(s_t3, 16 * IT)

        @block.gpsimd
        def _(pool):
            own = Tally(s_pl)

            def link(ins):
                pool.wait_ge(s_pl, own.add(ins))

            def tick(v):
                if is_reg(v):
                    pool.sem_inc(s_tick)

            link(pool.memset(ident[:, :], 0.0))
            link(pool.affine_select(out=ident[:, :], in_=ident[:, :], compare_op=ALU.not_equal, fill=1.0,
                                    base=0, pattern=[[-1, P]], channel_multiplier=1))
            link(pool.memset(tril[:, :], 1.0))
            link(pool.affine_select(out=tril[:, :], in_=tril[:, :], compare_op=ALU.is_gt, fill=0.0,
                                    base=0, pattern=[[-1, P]], channel_multiplier=1))
            link(pool.iota(iota[:, :], [[1, W * P]], base=0, channel_multiplier=0, allow_small_or_imprecise_dtypes=True))
            link(pool.iota(pcol[:, 6:7], [[1, 1]], base=0, channel_multiplier=1, allow_small_or_imprecise_dtypes=True))
            link(pool.iota(trash, [[1, 1]], base=P * T, channel_multiplier=1, allow_small_or_imprecise_dtypes=True))
            pool.memset(ones[:, :], 1.0).then_inc(s_const, 1)

            def gathers(table, width, index, it, g, free):
                free()
                pool.tensor_copy(idx[:, g, :], index[:, bass.ds(it * U + g * Q, Q)]).then_inc(s_pl, 1)
                own.k += 1
                pool.wait_ge(s_pl, own.value())
                tick(it)
                for k in range(Q):
                    pool.indirect_dma_start(gat[:, g * Q + k, 0:width], None, table[:, :],
                                            bass.IndirectOffsetOnAxis(ap=idx[:, g, k:k + 1], axis=0)).then_inc(s_ga[g * Q + k], 16)

            def residual(r, table):
                pool.wait_ge(s_flag, 3)
                more = pool.value_load(flag[0:1, 0:1], min_val=0, max_val=T * P)
                with pool.If(more > 0):
                    pool.wait_ge(r_go, r + 1)
                    pool.wait_ge(r_init, 16 * (NC + 1) * (r + 1))

                    def body(i):
                        n = i + T * r
                        wait(pool, r_sc, n * 16)
                        pool.tensor_copy(idx[:, 0, 0:1], gsrc[:, bass.ds(i, 1)]).then_inc(r_pl, 1)
                        pool.wait_ge(r_pl, n + 1)
                        tick(i)
                        width = K0 if r == 0 else H
                        pool.indirect_dma_start(gat[:, 0, 0:width], None, table[:, :],
                                                bass.IndirectOffsetOnAxis(ap=idx[:, 0, 0:1], axis=0)).then_inc(r_x, 16)
                        pool.wait_ge(r_ix, n + 1)
                        tick(i)
                        pool.indirect_dma_start(rst, None, states[:, :],
                                                bass.IndirectOffsetOnAxis(ap=idx[:, 1, 0:1], axis=0)).then_inc(r_st, 16)
                        pool.wait_ge(r_new, n + 1)
                        tick(i)
                        pool.indirect_dma_start(states[:, :], bass.IndirectOffsetOnAxis(ap=idxs[:, 0, 0:1], axis=0),
                                                rnew, None).then_inc(r_sc, 16)
                    turns(pool, T, body)

            pool.wait_ge(s_prep, 1)
            pool.wait_ge(s_zs[0], 32 * (IT // 2 + 1))
            pool.wait_ge(s_zs[1], 32 * (IT // 2))

            def free0(it, g):
                n = it * 2 + g
                if is_reg(it) or it > 0:
                    pool.wait_ge(s_vs[g], it * 16)
                    pool.wait_ge(s_sc0, n * 4 - 4)
                    for k in range(Q):
                        pool.wait_ge(s_ga[g * Q + k], it * 16)
                    tick(it)

            def body0(it):
                own.turn(it, 2)
                for g in range(2):
                    gathers(tab0, K0, gsrc, it, g, lambda: free0(it, g))
            turns(pool, IT, body0)
            own.close(IT)
            residual(0, tab0)

            pool.wait_ge(s_t1, 16 * NC)
            pool.wait_ge(s_zero, 16 * TABLES * (IT + 1))

            def free1(it, g):
                n = it * 2 + g
                if is_reg(it) or it > 0:
                    pool.wait_ge(s_ms, n * 1 - 1)
                    for k in range(Q):
                        pool.wait_ge(s_ga[g * Q + k], it * 16 + 16 * IT)
                    tick(it)

            def scatter(it, g):
                n = it * 2 + g
                pool.wait_ge(s_oc, n * 1 + 1)
                pool.wait_ge(s_sx, n * 1 + 1)
                for k in range(Q):
                    wait(pool, s_sc[(1 - g) * Q + k], it * 16 + 16 * g)
                tick(it)
                for k in range(Q):
                    pool.indirect_dma_start(aggs[k][:, :], bass.IndirectOffsetOnAxis(ap=idxs[:, g, k:k + 1], axis=0),
                                            osum[g][:, k, :], None, compute_op=ALU.add).then_inc(s_sc[g * Q + k], 16)

            def body1(it, last=False):
                own.turn(it, 2)
                own.k = 1
                gathers(tab1, K1, gdst, it, 1, lambda: free1(it, 1))
                scatter(it, 0)
                if not last:
                    own.turn(it + 1, 2)
                    gathers(tab1, K1, gdst, it + 1, 0, lambda: free1(it + 1, 0))
                scatter(it, 1)
            own.turn(0, 2)
            gathers(tab1, K1, gdst, 0, 0, lambda: None)
            body1(0)
            with pool.Fori(1, IT - 1) as it:
                body1(it)
            body1(IT - 1, True)
            own.close(IT)

            for layer in range(2):
                if layer == 0:
                    pool.wait_ge(s_t2[0], 16 * (NC // 2))
                    pool.wait_ge(s_t2[1], 16 * (NC // 2))
                else:
                    pool.wait_ge(s_t3, 16 * IT)

                def free2(it, g):
                    n = it * 2 + g
                    if is_reg(it) or it > 0:
                        pool.wait_ge(s_mm2[layer], n * 1 - 1)
                        for k in range(Q):
                            pool.wait_ge(s_ga[g * Q + k], it * 16 + 16 * IT * (2 + layer))
                        tick(it)

                def body2(it):
                    own.turn(it, 2)
                    for g in range(2):
                        gathers((tab2, tab3)[layer], H, gsrc, it, g, lambda: free2(it, g))
                turns(pool, IT, body2)
                own.close(IT)
                residual(1 + layer, (tab2, tab3)[layer])

        @block.scalar
        def _(act):
            def tick(v):
                if is_reg(v):
                    act.sem_inc(s_tick)

            def emb_out(m, s):
                act.wait_ge(s_zm, m * 1 + 1)
                if is_reg(m) or m > 1:
                    act.wait_ge(s_zs[s], 16 * (m - s))
                ps = psum[:, s, :].rearrange("p (t c) -> p t c", c=2 * GE)
                act.copy(st0[s][:, :, H:K0], ps[:, :, 0:GE])
                act.copy(stu[s][:, :, 0:GE], ps[:, :, GE:2 * GE]).then_inc(s_ze, 1)
            emb_out(0, 0)
            emb_out(1, 1)
            with act.Fori(1, IT // 2) as q:
                emb_out(q * 2, 0)
                emb_out(q * 2 + 1, 1)
            emb_out(IT - 1, 0)
            act.wait_ge(s_ask, 1)
            act.activation(tmpc[:, :], tmpd[:, :], ACT.Sin, bias=halfpi, scale=-PI / 6.0).then_inc(s_ans, 1)

            def residual(r):
                act.wait_ge(s_flag, 3)
                more = act.value_load(flag[0:1, 0:1], min_val=0, max_val=T * P)
                if r:
                    return
                with act.If(more > 0):
                    def body(i):
                        act.wait_ge(r_lm, i + 1)
                        act.activation(rw[:, H:H + 1], rc[6], ACT.Exp).then_inc(r_ex, 1)
                        act.wait_ge(r_df, i + 1)
                        act.activation(rd2, rd2, ACT.Exp).then_inc(r_dx, 1)
                    turns(act, T, body)

                    def merge(c):
                        act.wait_ge(r_mf, c + 1)
                        act.activation(rdf, rdf, ACT.Exp).then_inc(r_mx, 1)
                    turns(act, NC, merge)

            def group0(it, g, W):
                n = it * 2 + g
                act.wait_ge(s_edge, n * 1 + 1)
                act.activation(wrow[:, g * Q:(g + 1) * Q, H], lm[:, g, :], ACT.Exp).then_inc(s_wr, 1)
                act.wait_ge(s_wr, n * 1 + 1)
                for k in range(g * Q, (g + 1) * Q):
                    act.wait_ge(s_ga[k], it * 16 + 16)
                    act.mul(wrow[:, k, 0:H], gat[:, k, 0:H], wrow[:, k, H:H + 1]).then_inc(s_sc0, 1)
                act.wait_ge(s_df, n * 1 + 1)
                d = dif[:, g, :, 0:Q * W]
                act.activation(d, d, ACT.Exp).then_inc(s_dx, 1)

            def body0(it, w, _):
                group0(it, 0, w)
                group0(it, 1, w)
            segments(act, body0)
            residual(0)

            asked = Tally(s_ask)
            asked.base = 1
            said = Tally(s_ans)
            said.base = 1

            def answer(o_, i_, f, **kw):
                asked.k += 1
                act.wait_ge(s_ask, asked.value())
                act.activation(o_, i_, f, **kw).then_inc(s_ans, 1)

            def nodes0(c):
                asked.turn(c, 2)
                answer(ubuf, tbuf, ACT.Exp)
                answer(small[2], small[1], ACT.Sqrt, bias=epsc, scale=1.0 / H)
            turns(act, NC, nodes0)
            asked.close(NC)

            def group1(it, g):
                n = it * 2 + g
                act.wait_ge(s_at, n * 1 + 1)
                act.copy(attT[g], psum[0:R, g, :]).then_inc(s_ac, 1)
                act.wait_ge(s_hd, n * 1 + 1)
                act.activation(hid[g][0:H, :], psum[0:H, 2 + g, :], ACT.Silu, bias=b1c).then_inc(s_si, 1)
                act.wait_ge(s_os, n * 1 + 1)
                if is_reg(it) or it > 0:
                    for k in range(Q):
                        act.wait_ge(s_sc[g * Q + k], it * 16)
                act.copy(osum[g], psum[:, 6 + g, 0:Q * C1].rearrange("p (k c) -> p k c", k=Q)).then_inc(s_oc, 1)

            def body1(it):
                group1(it, 0)
                group1(it, 1)
            act.wait_ge(s_acz, 2)
            turns(act, IT, body1)

            def nodes1(q):
                asked.turn(q, 6)
                for s in range(2):
                    answer(small[2], small[1], ACT.Sqrt, bias=epsc, scale=1.0 / H)
                    answer(small[2], small[1], ACT.Sqrt, bias=epsc, scale=1.0 / H)
                    answer(small[5], small[4], ACT.Sqrt)
            turns(act, NC // 2, nodes1)
            asked.close(NC // 2)
            answer(cj, tbuf[:, 0:T], ACT.Sqrt)
            answer(smax[:, 0:T], tbuf[:, 0:T], ACT.Sqrt)
            asked.base, asked.k = asked.base + asked.k, 0

            def nodes2(it):
                asked.turn(it, 1)
                act.wait_ge(s_ntp, it * 2 + 1)
                act.copy(hT[0:H, :].rearrange("p (b c) -> p b c", b=2), psum[0:H, 0:2, :]).then_inc(s_ncp, 1)
                answer(small[2][:, 0:U], small[1][:, 0:U], ACT.Sqrt, bias=epsc, scale=1.0 / H)
                act.wait_ge(s_ntp, it * 2 + 2)
                act.copy(hT2[0:H, :].rearrange("p (b c) -> p b c", b=2), psum[0:H, 0:2, :]).then_inc(s_ncp, 1)
            turns(act, IT, nodes2)
            asked.close(IT)

            answer(small[2][:, 0:1], small[1][:, 0:1], ACT.Copy)
            asked.base, asked.k = asked.base + asked.k, 0
            answer(ybuf[:, 0:H], tbuf[:, 0:H], ACT.Sqrt, bias=epsc, scale=1.0 / N)
            asked.base, asked.k = asked.base + asked.k, 0

            def nodes3(c):
                asked.turn(c, 1)
                answer(small[2], small[1], ACT.Sqrt, bias=epsc, scale=1.0 / H)
            turns(act, NC, nodes3)

        @block.tensor
        def _(pe):
            tile = [slice(k * P, (k + 1) * P) for k in range(U)]

            def tick(v):
                if is_reg(v):
                    pe.sem_inc(s_tick)

            def residual(r):
                pe.wait_ge(s_flag, 3)
                more = pe.value_load(flag[0:1, 0:1], min_val=0, max_val=T * P)
                with pe.If(more > 0):
                    def body(i):
                        n = i + T * r
                        pe.wait_ge(r_q, n + 1)
                        tick(i)
                        mm = pe.matmul(psum[:, 0, 0:P], ones[:, :], rdk, start=True, stop=True)
                        if r == 0:
                            mm = pe.matmul(psum[:, 0, P:2 * P], ones[:, :], rdl, start=True, stop=True)
                        mm.then_inc(r_bk, 1)
                        pe.wait_ge(r_w, n + 1)
                        tick(i)
                        pe.matmul(psum[:, 1, 0:CR - 2], req, rw[:, 0:CR - 2], start=True, stop=True).then_inc(r_mm, 1)
                    turns(pe, T, body)

            pe.wait_ge(s_const, 1)
            pe.wait_ge(s_w, 16 * 14)
            pe.transpose(psum[0:R, 0, 0:H], w1raw, ident[0:H, 0:H])
            pe.transpose(psum[0:H, 0, 64:64 + H], w2raw, ident[0:H, 0:H])
            pe.transpose(psum[0:H, 0, 128:128 + H], l2raw, ident[0:H, 0:H])
            pe.transpose(psum[0:GE, 0, 192:192 + GE], adraw, ident[0:GE, 0:GE])
            pe.transpose(psum[0:GE, 0, 256:256 + NEL], EU[:, 0:GE], ident[0:NEL, 0:NEL])
            pe.transpose(psum[0:H, 0, 400:401], b1raw, ident[0:1, 0:1]).then_inc(s_tp, 1)
            pe.wait_ge(s_cp, 1)
            pe.matmul(psum[0:NEL, 0, 0:GE], embT, adT, start=True, stop=True).then_inc(s_tp, 1)
            pe.wait_ge(s_rowf, 1)
            for a in range(5):
                for b in range(4):
                    n = P if b < 3 else U
                    t = pe.transpose(psum[:, 1 + a, b * P:b * P + n], RF[0:n, a, b, :], ident[0:n, 0:n])
                t.then_inc(s_tp, 1)
            pe.wait_ge(s_cp, 7)
            pe.wait_ge(s_flag, 1)
            pe.matmul(psum[:, 6, 0:T], ones[0:1, :], tmpc[0:1, :], start=True, stop=True).then_inc(s_bb, 1)
            pe.wait_ge(s_flag, 2)
            pe.transpose(psum[0:1, 7, 0:P], flagr[:, :], ident[:, :]).then_inc(s_bb, 1)

            def emb_mm(m, s):
                pe.wait_ge(s_zo, m * 1 + 1)
                wait(pe, s_ze, m - 1)
                for k in range(U):
                    mm = pe.matmul(psum[:, s, k * 2 * GE:(k + 1) * 2 * GE], zoh[s][:, tile[k]], EU, start=True, stop=True)
                mm.then_inc(s_zm, 1)
            emb_mm(0, 0)
            emb_mm(1, 1)
            with pe.Fori(1, IT // 2) as q:
                emb_mm(q * 2, 0)
                emb_mm(q * 2 + 1, 1)
            emb_mm(IT - 1, 0)

            def group0(it, g, W):
                n = it * 2 + g
                wait(pe, s_cmb, n - 1)
                for k in range(Q):
                    pe.wait_ge(s_oh, it * U + g * Q + k + 1)
                    for w in range(W):
                        mm = pe.matmul(psum[:, 4 + g, (k * W + w) * 3:(k * W + w) * 3 + 3], oneh[:, g * Q + k, tile[w]],
                                       wrow[:, g * Q + k, C0:C0 + 3], start=True, stop=True)
                mm.then_inc(s_st, 1)
                for k in range(Q):
                    pe.wait_ge(s_sc0, it * U + g * Q + k + 1)
                    at = (k % 2) * W * C0
                    for w in range(W):
                        mm = pe.matmul(psum[:, 2 * g + k // 2, at + w * C0:at + (w + 1) * C0], oneh[:, g * Q + k, tile[w]],
                                       wrow[:, g * Q + k, 0:C0], start=True, stop=True)
                mm.then_inc(s_mm, 1)

            def body0(it, w, _):
                group0(it, 0, w)
                group0(it, 1, w)
            segments(pe, body0)
            residual(0)

            def group1(it, g):
                n = it * 2 + g
                pe.wait_ge(s_al[g], it * 48 + 48 if is_reg(it) or it < IT - 1 or g == 0 else it * 48 + 64)
                wait(pe, s_ac, n - 1)
                tick(it)
                for k in range(Q):
                    t = pe.transpose(psum[0:R, g, tile[k]], att[g][:, k, :], ident[:, :])
                t.then_inc(s_at, 1)
                pe.wait_ge(s_ac, n * 1 + 1)
                wait(pe, s_si, n - 1)
                tick(it)
                pe.matmul(psum[0:H, 2 + g, :], W1T, attT[g], start=True, stop=True).then_inc(s_hd, 1)
                pe.wait_ge(s_si, n * 1 + 1)
                wait(pe, s_ms, n - 1)
                for k in range(Q):
                    mm = pe.matmul(psum[:, 4 + g, k * H:(k + 1) * H], hid[g][:, tile[k]], W2T, start=True, stop=True)
                mm.then_inc(s_gt, 1)
                pe.wait_ge(s_ms, n * 1 + 1)
                pe.wait_ge(s_eq, n * 1 + 1)
                wait(pe, s_oc, n - 1)
                for k in range(Q):
                    mm = pe.matmul(psum[:, 6 + g, k * C1:(k + 1) * C1], eqm[g][:, k, :], msg[g][:, k, :], start=True, stop=True)
                mm.then_inc(s_os, 1)

            def body1(it):
                group1(it, 0)
                group1(it, 1)
            pe.wait_ge(s_acz, 2)
            turns(pe, IT, body1)

            for layer in range(2):
                def group2(it, g, W):
                    n = it * 2 + g
                    wait(pe, s_cm2[layer], n - 1)
                    for k in range(Q):
                        pe.wait_ge(s_oh2[layer], it * U + g * Q + k + 1)
                        pe.wait_ge(s_ga[g * Q + k], it * 16 + 16 + 16 * IT * (2 + layer))
                        at = (k % 2) * W * H
                        for w in range(W):
                            mm = pe.matmul(psum[:, 2 * g + k // 2, at + w * H:at + (w + 1) * H],
                                           oneh[:, g * Q + k, tile[w]], gat[:, g * Q + k, 0:H], start=True, stop=True)
                    mm.then_inc(s_mm2[layer], 1)

                def body2(it, w, _):
                    group2(it, 0, w)
                    group2(it, 1, w)
                segments(pe, body2)
                residual(1 + layer)
                if layer:
                    break

                def nodes2(it):
                    for h, (to, wgt) in enumerate(((hT, L2WT), (hT2[0:H, :], L3Ws))):
                        pe.wait_ge(s_na, it * 2 + h + 1)
                        tick(it)
                        for k in range(U):
                            t = pe.transpose(psum[0:H, k // 4, (k % 4) * P:(k % 4 + 1) * P],
                                             ybuf[:, k * H:(k + 1) * H], ident[:, :])
                        t.then_inc(s_ntp, 1)
                        pe.wait_ge(s_ncp, it * 2 + h + 1)
                        for k in range(U):
                            mm = pe.matmul(psum[:, 2 + h, k * H:(k + 1) * H], to[:, tile[k]], wgt, start=True, stop=True)
                        mm.then_inc(s_nmm, 1)
                turns(pe, IT, nodes2)

            for h in range(2):
                pe.wait_ge(s_bn, h + 1)
                pe.matmul(psum[:, h, 0:H], ones[:, :], sbuf_[:, 0:H], start=True, stop=True).then_inc(s_bm, 1)

        @block.vector
        def _(dve):
            own = Tally(s_dv)
            V = nc.vector

            def link(ins):
                dve.wait_ge(s_dv, own.add(ins))

            def note(ins):
                own.add(ins)

            def tick(v):
                if is_reg(v):
                    dve.sem_inc(s_tick)

            def sync():
                dve.wait_ge(s_dv, own.value())

            note(V.memset(RI[:, :, 3, :], -1))
            note(V.memset(RF[:, 2:5, 3, :], 0.0))
            note(V.memset(W2T, 0.0))
            link(V.memset(L2WT, 0.0))
            V.memset(X[:, FULL:T, :], 0.0).then_inc(s_pad, 1)
            note(V.memset(zb[0], 0))
            note(V.memset(zb[1], 0))
            note(V.memset(zero[:, :], 0.0))
            note(V.memset(indeg[:, :], 0.0))
            note(V.memset(smax[:, :], -BIG))
            note(V.memset(halfpi, PI / 2.0))
            note(V.memset(epsc, EPS))
            note(V.memset(wrow[:, :, C0 + 2], 1.0))
            link(V.memset(valid, 0.0))
            V.memset(pcol[0:64, 4:5], 1.0).then_inc(s_pad, 1)
            note(V.memset(pcol[64:64 + REST - 64, 4:5], 1.0))
            dve.wait_ge(s_rows, 16 * (15 + 2))
            link(V.tensor_copy(RF[:, 0:2], RI))
            V.tensor_copy(flagf[:, 0:1], RF[0:1, 0, 0, 0:1]).then_inc(s_rowf, 1)
            dve.wait_ge(s_tp, 1)
            note(V.tensor_copy(W1T, psum[0:R, 0, 0:H]))
            note(V.tensor_copy(W2T[0:H, :], psum[0:H, 0, 64:64 + H]))
            note(V.tensor_copy(L2WT[0:H, :], psum[0:H, 0, 128:128 + H]))
            note(V.tensor_copy(adT, psum[0:GE, 0, 192:192 + GE]))
            note(V.tensor_copy(b1c, psum[0:H, 0, 400:401]))
            V.tensor_copy(embT, psum[0:GE, 0, 256:256 + NEL]).then_inc(s_cp, 1)
            sync()
            dve.wait_ge(s_tp, 2)
            V.tensor_copy(EU[:, GE:2 * GE], psum[0:NEL, 0, 0:GE]).then_inc(s_cp, 1)
            for a in range(5):
                dve.wait_ge(s_tp, 3 + a)
                V.tensor_copy(cols[:, a, :], psum[:, 1 + a, 0:T]).then_inc(s_cp, 1)
            dve.wait_ge(s_cp, 7)
            link(V.tensor_scalar(tmpc[0:1, :], dcol[0:1, :], 0.0, None, ALU.max))
            link(V.tensor_copy(tmpi[0:1, :], tmpc[0:1, :]))
            link(V.tensor_scalar(base[:, :], tmpi[0:1, :], 7, None, ALU.arith_shift_right))
            V.tensor_scalar(tmpc[0:1, :], base[:, :], float(P), None, ALU.mult).then_inc(s_flag, 1)
            dve.wait_ge(s_bb, 1)
            link(V.tensor_tensor(relc[:, :], dcol, psum[:, 6, 0:T], ALU.subtract))
            link(V.tensor_scalar(tmpc[:, :], relc[:, :], 0.0, None, ALU.is_ge))
            for a, b, w in SEGS:
                js = slice(a * U, b * U)
                note(V.scalar_tensor_tensor(tmpd[:, js], relc[:, js], float(w * P), tmpc[:, js], ALU.is_lt, ALU.mult))
            sync()
            link(V.tensor_scalar(tmpd[:, :], tmpd[:, :], -1.0, 1.0, ALU.mult, ALU.add))
            link(V.scalar_tensor_tensor(tmpc[:, :], dcol, 1.0, tmpd[:, :], ALU.add, ALU.mult))
            link(V.tensor_scalar(tmpr, tmpc[:, :], -1.0, None, ALU.add))
            V.tensor_reduce(flagr[:, :], tmpc[:, :], AX.X, ALU.max).then_inc(s_flag, 1)
            dve.wait_ge(s_bb, 2)
            link(V.tensor_reduce(flagf[:, 0:1], psum[0:1, 7, 0:P], AX.X, ALU.max))
            V.tensor_copy(flag[:, :], flagf[:, 0:1]).then_inc(s_flag, 1)
            for c_, to in ((scol, gsrc), (dcol, gdst)):
                link(V.tensor_scalar(tmpi[:, :], c_, 0.0, None, ALU.max))
                link(V.tensor_scalar(to[:, :], tmpi[:, :], 7, None, ALU.arith_shift_right))
                link(V.tensor_scalar(tmpi[:, :], tmpi[:, :], P - 1, None, ALU.bitwise_and))
                link(V.scalar_tensor_tensor(to[:, :], tmpi[:, :], float(T), to[:, :], ALU.mult, ALU.add))
            link(V.tensor_scalar(firstv, pcol[:, 6:7], -BIG, None, ALU.mult))
            V.tensor_copy(tmpc[:, 0:1], firstv).then_inc(s_prep, 1)
            link(V.scalar_tensor_tensor(tmpd[:, :], ecol, -1.0, ecol, ALU.mult, ALU.max))
            V.tensor_scalar(tmpd[:, :], tmpd[:, :], 6.0, None, ALU.min).then_inc(s_ask, 1)

            def emb_oh(m, s):
                last = not is_reg(m) and m == IT - 1
                q = (m - s) // 2 if not is_reg(m) else None
                dve.wait_ge(s_zl[s], 8 * (m - s) + 16)
                wait(dve, s_zm, m - 1)
                V.tensor_scalar(zoh[s], zb[s], pcol[0:NEL, 6:7], None, ALU.is_equal).then_inc(s_zo, 1)
                if is_reg(m) or m > 1:
                    dve.wait_ge(s_zs[s], 16 * (m - s))
                    if is_reg(m):
                        dve.sem_inc(s_tick)
                note(V.tensor_copy(st0[s][:, :, 0:H], X[:, bass.ds(m * U, U), :]))
                link(V.tensor_copy(stu[s][:, :, GE], mcol[:, bass.ds(m * U, U)]))
                dve.sem_inc(s_zx)
            own.turn(0, 2)
            emb_oh(0, 0)
            own.turn(1, 2)
            emb_oh(1, 1)
            with dve.Fori(1, IT // 2) as q:
                own.turn(q * 2, 2)
                emb_oh(q * 2, 0)
                own.turn(q * 2 + 1, 2)
                emb_oh(q * 2 + 1, 1)
            own.turn(IT - 1, 2)
            emb_oh(IT - 1, 0)
            own.close(IT)
            dve.wait_ge(s_ans, 1)
            link(V.tensor_scalar(tmpc[:, :], tmpc[:, :], 0.5, 0.5, ALU.mult, ALU.add))
            link(V.scalar_tensor_tensor(ecol, ecol, 6.0, tmpc[:, :], ALU.is_lt, ALU.mult))
            link(V.tensor_copy(resc, tmpr))
            dve.wait_ge(s_rowd, 96)
            dve.wait_ge(s_zs[0], 32 * (IT // 2 + 1))
            dve.wait_ge(s_zs[1], 32 * (IT // 2))
            note(V.memset(ACC[:, :], 0.0))
            sync()
            dve.sem_inc(s_acz)

            def residual(r):
                more = V.value_load(flag[0:1, 0:1], min_val=0, max_val=T * P)
                with dve.If(more > 0):
                    mine = Tally(r_dv)
                    sizes = [(24, 9), (13, 1), (13, 1)]
                    per, perm = sizes[r]
                    mine.base = sum(3 + a * T + b * NC for a, b in sizes[:r])

                    def link(ins):
                        dve.wait_ge(r_dv, mine.add(ins))
                    link(V.memset(rzero, 0.0))
                    link(V.memset(rzero.rearrange("p (j c) -> p j c", c=CR)[:, :, 50], -BIG))
                    link(V.memset(rw, 1.0))
                    dve.sem_inc(r_zero)
                    dve.sem_inc(r_go)

                    def body(i):
                        mine.turn(i, per)
                        n = i + T * r
                        one = bass.ds(i, 1)
                        key = resc[:, one]
                        wait(dve, r_sc, n * 16)
                        tick(i)
                        link(V.tensor_scalar(rc[0], key, 0.0, None, ALU.is_ge))
                        link(V.tensor_scalar(rc[1], gdst[:, one], trash, None, ALU.subtract))
                        link(V.tensor_tensor(rc[2], rc[0], rc[1], ALU.mult))
                        link(V.tensor_scalar(idx[:, 1, 0:1], rc[2], trash, None, ALU.add))
                        dve.sem_inc(r_ix)
                        link(V.tensor_scalar(rdk, ident[:, :], key, None, ALU.mult))
                        if r == 0:
                            link(V.tensor_scalar(rdl, ident[:, :], lcol[:, one], None, ALU.mult))
                        dve.sem_inc(r_q)
                        dve.wait_ge(r_bk, n + 1)
                        link(V.tensor_scalar(req, psum[:, 0, 0:P], key, None, ALU.is_equal))
                        link(V.tensor_tensor_reduce(out=rjunk, in0=req, in1=tril[:, :], scale=1.0, scalar=0.0,
                                                    op0=ALU.mult, op1=ALU.add, accum_out=rc[3]))
                        link(V.tensor_scalar(rc[4], rc[3], 0.0, None, ALU.is_equal))
                        link(V.tensor_tensor(rc[4], rc[4], rc[2], ALU.mult))
                        link(V.tensor_scalar(idxs[:, 0, 0:1], rc[4], trash, None, ALU.add))
                        dve.wait_ge(r_x, n * 16 + 16)
                        if r == 0:
                            link(V.tensor_scalar(rt1, psum[:, 0, 0:P], key, -BIG, ALU.not_equal, ALU.mult))
                            tick(i)
                            link(V.tensor_tensor_reduce(out=rjunk, in0=rt1, in1=psum[:, 0, P:2 * P], scale=1.0,
                                                        scalar=-BIG * 8, op0=ALU.add, op1=ALU.max, accum_out=rc[5]))
                            link(V.tensor_tensor(rc[6], lcol[:, one], rc[5], ALU.subtract))
                            dve.sem_inc(r_lm)
                            dve.wait_ge(r_ex, n + 1)
                            link(V.tensor_scalar(rw[:, 0:H], gat[:, 0, 0:H], rw[:, H:H + 1], None, ALU.mult))
                        else:
                            if is_reg(i):
                                tick(i)
                            link(V.tensor_copy(rw[:, 0:H], gat[:, 0, 0:H]))
                        dve.sem_inc(r_w)
                        dve.wait_ge(r_st, n * 16 + 16)
                        if r == 0:
                            link(V.tensor_tensor(rc[7], rst[:, 50:51], rc[5], ALU.max))
                            link(V.tensor_tensor(rd2[:, 0:1], rst[:, 50:51], rc[7], ALU.subtract))
                            link(V.tensor_tensor(rd2[:, 1:2], rc[5], rc[7], ALU.subtract))
                            dve.sem_inc(r_df)
                            dve.wait_ge(r_mm, n + 1)
                            link(V.tensor_tensor(rnew, rst, rst, ALU.max))
                            dve.wait_ge(r_dx, n + 1)
                            link(V.tensor_scalar(rs_[:, 0:C0], psum[:, 1, 0:C0], rd2[:, 1:2], None, ALU.mult))
                            link(V.tensor_scalar(rnew[:, 0:C0], rst[:, 0:C0], rd2[:, 0:1], None, ALU.mult))
                            link(V.tensor_tensor(rnew[:, 0:C0], rnew[:, 0:C0], rs_[:, 0:C0], ALU.add))
                            link(V.tensor_tensor(rnew[:, 49:50], rst[:, 49:50], psum[:, 1, 49:50], ALU.add))
                            link(V.tensor_tensor(rnew[:, 50:51], rc[7], rc[7], ALU.max))
                        else:
                            dve.wait_ge(r_mm, n + 1)
                            link(V.tensor_tensor(rnew, rst, rst, ALU.max))
                            link(V.tensor_tensor(rnew[:, 0:H], rst[:, 0:H], psum[:, 1, 0:H], ALU.add))
                        dve.sem_inc(r_new)
                        assert mine.k == per, (mine.k, per, r)
                    turns(dve, T, body)
                    mine.close(T)
                    ch = rchunk.rearrange("p (j c) -> p j c", c=CR)

                    def merge(c):
                        mine.turn(c, perm)
                        js = bass.ds(c * CH, CH)
                        dve.wait_ge(r_ld, (c + 1) * 16 + 16 * NC * r)
                        if r:
                            link(V.tensor_tensor(acc[:, js, :], acc[:, js, :], ch[:, :, 0:H], ALU.add))
                        else:
                            mx = rzero[:, 0:CH]
                            link(V.tensor_tensor(mx, smax[:, js], ch[:, :, 50], ALU.max))
                            link(V.tensor_tensor(rdf[:, 0:CH], smax[:, js], mx, ALU.subtract))
                            link(V.tensor_tensor(rdf[:, CH:2 * CH], ch[:, :, 50], mx, ALU.subtract))
                            dve.sem_inc(r_mf)
                            dve.wait_ge(r_mx, c + 1)
                            link(V.tensor_tensor(ch[:, :, 0:C0], ch[:, :, 0:C0],
                                                 rdf[:, CH:2 * CH].unsqueeze(2).to_broadcast([P, CH, C0]), ALU.mult))
                            a = acc0[:, js, :]
                            link(V.tensor_tensor(a, a, rdf[:, 0:CH].unsqueeze(2).to_broadcast([P, CH, C0]), ALU.mult))
                            link(V.tensor_tensor(a, a, ch[:, :, 0:C0], ALU.add))
                            link(V.tensor_tensor(indeg[:, js], indeg[:, js], ch[:, :, 49], ALU.add))
                            link(V.tensor_tensor(smax[:, js], mx, mx, ALU.max))
                            link(V.tensor_tensor(rd2[:, 0:1], rd2[:, 0:1], rd2[:, 0:1], ALU.max))
                        dve.sem_inc(r_use)
                        assert mine.k == perm, (mine.k, perm)
                    turns(dve, NC, merge)

            def produce0(it, g, W):
                n = it * 2 + g
                dve.wait_ge(s_rl[g], it * 32 + 32)
                if is_reg(it) or it > 0:
                    dve.wait_ge(s_mm, n * 1 - 1)
                sl = [slice(k * P, (k + 1) * P) for k in range(Q)]
                for k in range(Q):
                    i = it * U + g * Q + k
                    note(V.tensor_scalar(t1[:, k, :], drow[g][:, sl[k]], dcol[:, bass.ds(i, 1)], -BIG, ALU.not_equal, ALU.mult))
                sync()
                for k in range(Q):
                    tick(it)
                    link(V.tensor_tensor_reduce(out=junk, in0=t1[:, k, :], in1=lrow[g][:, sl[k]], scale=1.0, scalar=-BIG * 8,
                                                op0=ALU.add, op1=ALU.max, accum_out=mloc[:, g, k:k + 1]))
                    link(V.tensor_tensor_reduce(out=junk, in0=t1[:, k, :], in1=tril[:, :], scale=1.0, scalar=0.0,
                                                op0=ALU.mult, op1=ALU.add, accum_out=fsum[:, g, k:k + 1]))
                dve.sem_inc(s_rdone)
                note(V.tensor_tensor(lm[:, g, :], lcol[:, bass.ds(it * U + g * Q, Q)], mloc[:, g, :], ALU.subtract))
                link(V.tensor_scalar(wrow[:, g * Q:(g + 1) * Q, C0 + 1], fsum[:, g, :], firstv, None, ALU.is_equal))
                link(V.tensor_tensor(wrow[:, g * Q:(g + 1) * Q, C0], mloc[:, g, :], wrow[:, g * Q:(g + 1) * Q, C0 + 1], ALU.mult))
                dve.sem_inc(s_edge)
                for k in range(Q):
                    i = it * U + g * Q + k
                    V.tensor_scalar(oneh[:, g * Q + k, 0:W * P], iota[:, 0:W * P], relc[:, bass.ds(i, 1)], None, ALU.is_equal).then_inc(s_oh, 1)

            def combine0(it, g, W):
                n = it * 2 + g
                dve.wait_ge(s_st, n * 1 + 1)
                st = psum[:, 4 + g, 0:Q * W * 3].rearrange("p (k c) -> p k c", c=3)
                cd = cand[:, 0:Q * W]
                link(V.tensor_scalar(cd, st[:, :, 1], -1.0, BIG, ALU.add, ALU.mult))
                link(V.tensor_tensor(cd, cd, st[:, :, 0], ALU.add))
                js = []
                for k in range(Q):
                    j = V.value_load(base[0:1, bass.ds(it * U + g * Q + k, 1)], min_val=0, max_val=T - 1)
                    js.append(j)
                    m = smax[:, bass.ds(j, W)]
                    c_ = cand[:, k * W:(k + 1) * W]
                    link(V.tensor_tensor(dif[:, g, 0, k * W:(k + 1) * W], m, c_, ALU.subtract))
                    note(V.tensor_tensor(m, m, c_, ALU.max))
                    link(V.tensor_tensor(indeg[:, bass.ds(j, W)], indeg[:, bass.ds(j, W)], st[:, k * W:(k + 1) * W, 2], ALU.add))
                d = dif[:, g, :, 0:Q * W]
                link(V.tensor_scalar(d[:, 1], d[:, 0], -1.0, 0.0, ALU.mult, ALU.min))
                link(V.tensor_scalar(d[:, 0], d[:, 0], 0.0, None, ALU.min))
                dve.sem_inc(s_df)
                dve.wait_ge(s_dx, n * 1 + 1)
                dve.wait_ge(s_mm, n * 1 + 1)
                for h in range(2):
                    pr = prod[:, 0:2 * W * C0].rearrange("p (w c) -> p w c", c=C0)
                    ps = psum[:, 2 * g + h, 0:2 * W * C0].rearrange("p (w c) -> p w c", c=C0)
                    d1 = dif[:, g, 1, h * 2 * W:(h + 1) * 2 * W].unsqueeze(2).to_broadcast([P, 2 * W, C0])
                    link(V.tensor_tensor(pr, ps, d1, ALU.mult))
                    for k in (2 * h, 2 * h + 1):
                        a = acc0[:, bass.ds(js[k], W), :]
                        d0 = dif[:, g, 0, k * W:(k + 1) * W].unsqueeze(2).to_broadcast([P, W, C0])
                        link(V.tensor_tensor(a, a, d0, ALU.mult))
                        link(V.tensor_tensor(a, a, pr[:, (k % 2) * W:(k % 2 + 1) * W, :], ALU.add))
                dve.sem_inc(s_cmb)

            PR0 = Q + 2 * Q + 3
            CM0 = 2 + 3 * Q + 2 + 2 * (1 + 4)
            PER0 = 2 * (PR0 + CM0)

            def body0(it, w, after):
                own.turn(it, PER0)
                produce0(it, 1, w)
                combine0(it, 0, w)
                if after is not None:
                    produce0(it + 1, 0, after)
                combine0(it, 1, w)
                assert own.k == PER0 - (PR0 if after is None else 0), (own.k, PER0)
            produce0(0, 0, SEGS[0][2])
            segments(dve, body0)
            own.base += PER0 * IT - PR0
            own.per, own.it, own.k = 0, 0, 0
            residual(0)

            def v3(b, n=CH):
                return b[:, 0:n * H].rearrange("p (j c) -> p j c", c=H)

            def bc(v, n=CH):
                return v[:, 0:n].unsqueeze(2).to_broadcast([P, n, H])

            def vec(v, n=CH):
                return v.unsqueeze(1).to_broadcast([P, n, H])

            ans = Tally(s_ans)
            ans.base = 1

            def ask(ins):
                ins.then_inc(s_ask, 1)
                ans.k += 1
                dve.wait_ge(s_ans, ans.value())

            def norm(y, to, n=CH):
                link(V.tensor_reduce(small[0][:, 0:n], v3(y, n), AX.X, ALU.add))
                link(V.tensor_scalar(small[0][:, 0:n], small[0][:, 0:n], 1.0 / H, None, ALU.mult))
                link(V.tensor_tensor(v3(y, n), v3(y, n), bc(small[0], n), ALU.subtract))
                link(V.tensor_tensor(v3(sbuf_, n), v3(y, n), v3(y, n), ALU.mult))
                ask(V.tensor_reduce(small[1][:, 0:n], v3(sbuf_, n), AX.X, ALU.add))
                link(V.reciprocal(small[3][:, 0:n], small[2][:, 0:n]))
                return V.tensor_tensor(to, v3(y, n), bc(small[3], n), ALU.mult)

            def nodes0(c):
                own.turn(c, 12)
                ans.turn(c, 2)
                js = bass.ds(c * CH, CH)
                link(V.tensor_scalar(small[0], acc0[:, js, H], 1e-30, None, ALU.max))
                link(V.reciprocal(small[0], small[0]))
                link(V.tensor_tensor(v3(ybuf), acc0[:, js, 0:H], bc(small[0]), ALU.mult))
                ask(V.tensor_scalar(tbuf, ybuf, 0.0, None, ALU.min))
                link(V.tensor_scalar(ybuf, ybuf, 0.0, None, ALU.max))
                link(V.tensor_tensor(v3(ybuf), v3(ybuf), X[:, js, :], ALU.add))
                link(V.scalar_tensor_tensor(ybuf, ubuf, -1.0, ybuf, ALU.add, ALU.add))
                link(norm(ybuf, X[:, js, :]))
                dve.sem_inc(s_n0)
                assert own.k == 12, own.k
            for g in range(2):
                dve.wait_ge(s_vs[g], 16 * IT)
            dve.wait_ge(s_zero, 16 * TABLES * (IT + 1))
            turns(dve, NC, nodes0)
            own.close(NC)
            ans.close(NC)

            link(V.tensor_scalar(dtra, gsrc[:, :], trash, None, ALU.subtract))
            note(V.scalar_tensor_tensor(dtra, scol, 0.0, dtra, ALU.is_ge, ALU.mult))
            note(V.memset(hid[0], 1.0))
            note(V.memset(hid[1], 1.0))
            for g in range(2):
                note(V.memset(msg[g][:, :, H + 1], 1.0))
            sync()
            dve.sem_inc(s_acz)

            def group1(it, g):
                n = it * 2 + g
                sl = [slice(k * P, (k + 1) * P) for k in range(Q)]
                dve.wait_ge(s_al[g], it * 48 + 48 if is_reg(it) or it < IT - 1 or g == 0 else it * 48 + 64)
                wait(dve, s_os, n - 1)
                for k in range(Q):
                    i = it * U + g * Q + k
                    note(V.tensor_scalar(eqm[g][:, k, :], drow[g][:, sl[k]], scol[:, bass.ds(i, 1)], None, ALU.is_equal))
                sync()
                dve.sem_inc(s_eq)
                for k in range(Q):
                    link(V.tensor_tensor_reduce(out=junk, in0=eqm[g][:, k, :], in1=tril[:, :], scale=1.0, scalar=0.0,
                                                op0=ALU.mult, op1=ALU.add, accum_out=rank[:, g, k:k + 1]))
                link(V.scalar_tensor_tensor(idf, rank[:, g, :], 0.0, dtra[:, bass.ds(it * U + g * Q, Q)], ALU.is_equal, ALU.mult))
                if is_reg(it) or it > 0:
                    for k in range(Q):
                        dve.wait_ge(s_sc[g * Q + k], it * 16)
                V.tensor_scalar(idxs[:, g, :], idf, trash, None, ALU.add).then_inc(s_sx, 1)
                gg = gat[:, g * Q:(g + 1) * Q, :]
                for k in range(Q):
                    dve.wait_ge(s_ga[g * Q + k], it * 16 + 16 + 16 * IT)
                if is_reg(it):
                    dve.sem_inc(s_tick)
                note(V.tensor_tensor(qmu, ecol[:, bass.ds(it * U + g * Q, Q)], gg[:, :, H + GE], ALU.mult))
                link(V.tensor_tensor(uv, gg[:, :, H:H + GE], vse[g], ALU.mult))
                link(V.tensor_reduce(adp, uv, AX.X, ALU.add))
                dve.sem_inc(s_rs)
                dve.wait_ge(s_gt, n * 1 + 1)
                link(V.tensor_tensor(m1, psum[:, 4 + g, 0:Q * H].rearrange("p (k c) -> p k c", k=Q),
                                     adp.unsqueeze(2).to_broadcast([P, Q, H]), ALU.add))
                link(V.tensor_tensor(m2, m1, gg[:, :, 0:H], ALU.mult))
                note(V.tensor_copy(msg[g][:, :, H], gg[:, :, H + GE]))
                link(V.tensor_tensor(msg[g][:, :, 0:H], m2, qmu.unsqueeze(2).to_broadcast([P, Q, H]), ALU.mult))
                dve.sem_inc(s_ms)

            PER1 = 2 * (Q + Q + 1 + 3 + 4)

            def body1(it):
                own.turn(it, PER1)
                group1(it, 0)
                group1(it, 1)
                assert own.k == PER1, own.k
            turns(dve, IT, body1)
            own.close(IT)

            def nodes1(q):
                own.turn(q, 2 * 25)
                ans.turn(q, 6)
                for s in range(2):
                    c = q * 2 + s
                    js = bass.ds(c * CH, CH)
                    t = aload[s]
                    tv = t[0].rearrange("p (j c) -> p j c", c=C1)
                    dve.wait_ge(s_ld[s], q * 64 + 64)
                    note(V.tensor_tensor(t[0], t[0], t[1], ALU.add))
                    link(V.tensor_tensor(t[2], t[2], t[3], ALU.add))
                    link(V.tensor_tensor(t[0], t[0], t[2], ALU.add))
                    note(V.tensor_copy(small[6], tv[:, :, H + 1]))
                    link(V.tensor_scalar(small[0], tv[:, :, H], 1e-8, None, ALU.max))
                    link(V.reciprocal(small[0], small[0]))
                    link(V.tensor_tensor(v3(ybuf), tv[:, :, 0:H], bc(small[0]), ALU.mult))
                    dve.sem_inc(s_sum)
                    link(V.tensor_tensor(v3(ybuf), v3(ybuf), X[:, js, :], ALU.add))
                    link(norm(ybuf, v3(ybuf)))
                    link(V.tensor_tensor(v3(ybuf), v3(ybuf), vec(vecs[0]), ALU.mult))
                    link(V.tensor_tensor(v3(ybuf), v3(ybuf), vec(vecs[1]), ALU.add))
                    link(V.tensor_tensor(v3(ybuf), v3(ybuf), X[:, js, :], ALU.add))
                    link(norm(ybuf, X[:, js, :]))
                    ask(V.tensor_scalar(small[4], small[6], 1.0, None, ALU.max))
                    link(V.reciprocal(small[5], small[5]))
                    if is_reg(q) or q > 0:
                        dve.wait_ge(s_t2[s], q * 16)
                    link(V.tensor_tensor(v3(stg[s]), X[:, js, :], bc(small[5]), ALU.mult))
                    dve.sem_inc(s_n1)
                assert own.k == 2 * 25, own.k
            turns(dve, NC // 2, nodes1)
            own.close(NC // 2)
            ans.close(NC // 2)
            ask(V.tensor_scalar(tbuf[:, 0:T], indeg[:, 0:T], 1.0, None, ALU.max))
            link(V.reciprocal(cj, cj))
            ask(V.tensor_scalar(tbuf[:, 0:T], indeg[:, 0:T], 1.0, None, ALU.add))
            link(V.reciprocal(smax[:, 0:T], smax[:, 0:T]))
            ans.base, ans.k = ans.base + ans.k, 0
            link(V.memset(ACC[:, :], 0.0))
            for s in range(2):
                dve.wait_ge(s_t2[s], 16 * (NC // 2))

            def edges(layer):
                def produce(it, g, W):
                    n = it * 2 + g
                    if is_reg(it) or it > 0:
                        dve.wait_ge(s_mm2[layer], n * 1 - 1)
                    for k in range(Q):
                        i = it * U + g * Q + k
                        V.tensor_scalar(oneh[:, g * Q + k, 0:W * P], iota[:, 0:W * P], relc[:, bass.ds(i, 1)], None,
                                        ALU.is_equal).then_inc(s_oh2[layer], 1)

                def combine(it, g, W):
                    n = it * 2 + g
                    dve.wait_ge(s_mm2[layer], n * 1 + 1)
                    if is_reg(it):
                        dve.sem_inc(s_tick)
                    for k in range(Q):
                        j = V.value_load(base[0:1, bass.ds(it * U + g * Q + k, 1)], min_val=0, max_val=T - 1)
                        a = acc[:, bass.ds(j, W), :]
                        at = (k % 2) * W * H
                        ps = psum[:, 2 * g + k // 2, at:at + W * H].rearrange("p (w c) -> p w c", c=H)
                        link(V.tensor_tensor(a, a, ps, ALU.add))
                    dve.sem_inc(s_cm2[layer])

                def body(it, w, after):
                    own.turn(it, 2 * Q)
                    produce(it, 1, w)
                    combine(it, 0, w)
                    if after is not None:
                        produce(it + 1, 0, after)
                    combine(it, 1, w)
                produce(0, 0, SEGS[0][2])
                segments(dve, body)
                own.close(IT)
                residual(1 + layer)

            edges(0)

            note(V.memset(oneh[0:H + 1, :, :], 1.0))
            sync()
            PER2 = 14

            def nodes2(it):
                own.turn(it, PER2)
                ans.turn(it, 1)
                js = bass.ds(it * U, U)
                y, z = v3(ybuf, U), v3(tbuf, U)
                link(V.tensor_scalar(small[7][:, 0:U], indeg[:, js], 0.0, None, ALU.is_equal))
                note(V.tensor_tensor(z, X[:, js, :], small[7][:, 0:U].unsqueeze(2).to_broadcast([P, U, H]), ALU.mult))
                link(V.tensor_tensor(y, acc[:, js, :], cj[:, js].unsqueeze(2).to_broadcast([P, U, H]), ALU.mult))
                link(V.tensor_tensor(y, y, z, ALU.add))
                dve.sem_inc(s_na)
                dve.wait_ge(s_nmm, it * 2 + 1)
                ps = psum[:, 2, 0:U * H].rearrange("p (k c) -> p k c", k=U)
                link(V.tensor_scalar(y, ps, 0.0, None, ALU.max))
                link(V.tensor_tensor(y, y, X[:, js, :], ALU.add))
                link(norm(ybuf, y, U))
                dve.sem_inc(s_na)
                note(V.tensor_copy(X[:, js, :], y))
                dve.wait_ge(s_nmm, it * 2 + 2)
                ps = psum[:, 3, 0:U * H].rearrange("p (k c) -> p k c", k=U)
                link(V.tensor_tensor(acc[:, js, :], ps, smax[:, js].unsqueeze(2).to_broadcast([P, U, H]), ALU.mult))
                dve.sem_inc(s_n2)
                assert own.k == PER2, own.k
            turns(dve, IT, nodes2)
            own.close(IT)
            ans.close(IT)
            dve.wait_ge(s_t3, 16 * IT)

            edges(1)

            av = acc[:, 0:T, :]
            link(V.tensor_tensor(av, av, bc(smax, T), ALU.mult))
            link(V.tensor_tensor(av, av, vec(vecs[2], T), ALU.add))

            def masked():
                note(V.tensor_scalar(acc[:, FULL, :], acc[:, FULL, :], valid, None, ALU.mult))
                link(V.memset(acc[:, FULL + 1:T, :], 0.0))
            masked()
            V.tensor_reduce(sbuf_[:, 0:H], av.rearrange("p j c -> p c j"), AX.X, ALU.add).then_inc(s_bn, 1)
            dve.wait_ge(s_bm, 1)
            link(V.tensor_scalar(ubuf[:, 0:H], psum[:, 0, 0:H], 1.0 / N, None, ALU.mult))
            link(V.tensor_tensor(av, av, vec(ubuf[:, 0:H], T), ALU.subtract))
            masked()
            link(V.memset(tbuf[:, 0:H], 0.0))
            ask(V.tensor_copy(small[1][:, 0:1], tbuf[:, 0:1]))
            ans.base, ans.k = ans.base + ans.k, 0

            def squares(c):
                own.turn(c, 3)
                a = acc[:, bass.ds(c * CH, CH), :]
                link(V.tensor_tensor(v3(ybuf), a, a, ALU.mult))
                link(V.tensor_reduce(sbuf_[:, 0:H], v3(ybuf).rearrange("p j c -> p c j"), AX.X, ALU.add))
                link(V.tensor_tensor(tbuf[:, 0:H], tbuf[:, 0:H], sbuf_[:, 0:H], ALU.add))
            turns(dve, NC, squares)
            own.close(NC)
            V.tensor_copy(sbuf_[:, 0:H], tbuf[:, 0:H]).then_inc(s_bn, 1)
            dve.wait_ge(s_bm, 2)
            ask(V.tensor_copy(tbuf[:, 0:H], psum[:, 1, 0:H]))
            ans.base, ans.k = ans.base + ans.k, 0
            link(V.reciprocal(ubuf[:, 0:H], ybuf[:, 0:H]))
            link(V.tensor_tensor(vecs[3], vecs[3], ubuf[:, 0:H], ALU.mult))

            def nodes3(c):
                own.turn(c, 10)
                ans.turn(c, 1)
                js = bass.ds(c * CH, CH)
                link(V.tensor_tensor(v3(ybuf), acc[:, js, :], vec(vecs[3]), ALU.mult))
                link(V.tensor_tensor(v3(ybuf), v3(ybuf), vec(vecs[4]), ALU.add))
                link(V.tensor_scalar(ybuf, ybuf, 0.0, None, ALU.max))
                link(V.tensor_tensor(v3(ybuf), v3(ybuf), X[:, js, :], ALU.add))
                link(norm(ybuf, X[:, js, :]))
                dve.sem_inc(s_n3)
                assert own.k == 10, own.k
            turns(dve, NC, nodes3)
            own.close(NC)


_INS = ['x', 'src', 'dst', 'edge_attr_40', 'edge_weight', 'edge_weight1', 'node_type_119', 'node_vec',
        'L1_gnn_W1', 'L1_gnn_b1', 'L1_gnn_W2', 'L1_gnn_b2', 'L1_gnn_emb', 'L1_gnn_adaptW', 'L1_gnn_gamma',
        'L1_gnn_beta', 'L2_gnn_W', 'L2_gnn_b', 'L3_gnn_W', 'L3_gnn_b', 'L3_gnn_gamma', 'L3_gnn_beta']


def kernel(**inputs):
    import numpy as _np
    import concourse.bacc as _bacc
    from concourse import mybir as _mybir
    from concourse.bass_utils import run_bass_kernel_spmd as _run

    nc = _bacc.Bacc("TRN2", target_bir_lowering=False, num_devices=1)
    arrays, args = {}, []
    for name in _INS:
        a = _np.ascontiguousarray(inputs[name])
        arrays[f"in_{name}_dram"] = a
        args.append(nc.dram_tensor(f"in_{name}_dram", a.shape, _mybir.dt.from_np(a.dtype), kind="ExternalInput").ap())
    args.append(nc.dram_tensor("out_0_dram", (N, H), F32, kind="ExternalOutput").ap())
    build(nc, *args)
    r = _run(nc, [arrays], core_ids=[0])
    return r.results[0]["out_0_dram"]
```

```python
import concourse.bass as bass
from concourse import mybir
from contextlib import ExitStack

F32 = mybir.dt.float32
I32 = mybir.dt.int32
BF16 = mybir.dt.bfloat16
FP16 = mybir.dt.float16
ALU = mybir.AluOpType
ACT = mybir.ActivationFunctionType
AX = mybir.AxisListType

P = 128
N = 50000
H = 48
GE = 32
R = 40
NEL = 119
T = 392
FULL = N // P
REST = N - FULL * P
U = 8
IT = T // U
Q = 4
W = 4
SEGS = [(0, 17, 2), (17, 34, 3), (34, IT, 4)]
TA = T + W
C0 = H + 1
C1 = H + 2
K0 = H + GE
K1 = H + GE + 1
TABLES = 4
CH = 14
NC = T // CH
BIG = 2.0 ** 120
KEY = 2.0 ** 100
PARTS = 3
EPS = 1e-5
AW = 6568
PI = 3.141592653589793


class Tally:

    def __init__(self, sem):
        self.sem, self.base, self.per, self.it, self.k = sem, 0, 0, 0, 0

    def value(self):
        return self.base + self.k + (self.it * self.per if self.per else 0)

    def add(self, ins, n=1):
        ins.then_inc(self.sem, n)
        self.k += n
        return self.value()

    def turn(self, it, per):
        if not self.per:
            self.base += self.k
        self.it, self.per, self.k = it, per, 0

    def close(self, turns):
        self.base += turns * self.per
        self.per, self.it, self.k = 0, 0, 0


def is_reg(v):
    return not isinstance(v, int)


def wait(eng, sem, v):
    if is_reg(v) or v > 0:
        eng.wait_ge(sem, v)


def turns(eng, n, body):
    body(0)
    with eng.Fori(1, n - 1) as i:
        body(i)
    body(n - 1)


def segments(eng, body):
    for n, (a, b, w) in enumerate(SEGS):
        body(a, w, w)
        with eng.Fori(a + 1, b - 1) as i:
            body(i, w, w)
        body(b - 1, w, SEGS[n + 1][2] if n + 1 < len(SEGS) else None)


def build(nc, x, src, dst, attr, ew, ew1, ntype, nvec, W1, b1, W2, b2, emb, adaptW, gamma, beta,
          L2W, L2b, L3W, L3b, L3g, L3be, out):
    ctx = ExitStack()
    with ctx:
        def sb(name, shape, dt=F32):
            return ctx.enter_context(nc.sbuf_tensor(name, shape, dt))

        def sem(name):
            return ctx.enter_context(nc.semaphore(name))

        def dram(name, shape, dt=F32):
            return nc.dram_tensor(name, shape, dt, kind="Internal").ap()

        tab0 = dram("tab0", (P * T, K0))
        tab1 = dram("tab1", (P * T, K1))
        tab2 = dram("tab2", (P * T, PARTS * H), BF16)
        tab3 = dram("tab3", (P * T, PARTS * H), BF16)
        aggs = [dram(f"agg{k}", (P * T + P, C1)) for k in range(TABLES)]
        rows_d = [dram(f"rows{a}", (T * P,)) for a in range(3)]
        srcemb = dram("srcemb", (P, T * GE))
        tab0v = tab0.rearrange("(p j) c -> p j c", p=P)
        tab1v = tab1.rearrange("(p j) c -> p j c", p=P)
        tab2v = tab2.rearrange("(p j) c -> p j c", p=P)
        tab3v = tab3.rearrange("(p j) c -> p j c", p=P)
        aggv = [a[0:P * T, :].rearrange("(p j) c -> p (j c)", p=P) for a in aggs]

        X = sb("X", [P, T, H])
        ACC = sb("ACC", [P, TA * C0])
        acc0 = ACC[:, :].rearrange("p (j c) -> p j c", c=C0)
        acc = acc0[:, :, 0:H]
        cols = sb("cols", [P, 5, T])
        dcol, scol, lcol, ecol, mcol = (cols[:, a, :] for a in range(5))
        relc = sb("relc", [P, T])
        gsrc = sb("gsrc", [P, T], I32)
        gdst = sb("gdst", [P, T], I32)
        base = sb("base", [1, T], I32)
        smax = sb("smax", [P, TA])
        ident = sb("ident", [P, P])
        tril = sb("tril", [P, P])
        ones = sb("ones", [P, P])
        iota = sb("iota", [P, W * P], FP16)
        oneb = sb("oneb", [P, 2], BF16)
        pcol = sb("pcol", [P, 8])
        trash, firstv, halfpi, epsc, valid = (pcol[:, a:a + 1] for a in range(5))
        idx = sb("idx", [P, 2, Q], I32)
        flag = sb("flag", [1, 1], I32)
        flagr = sb("flagr", [P, 1])
        flagf = sb("flagf", [1, P])
        wsm = sb("wsm", [P, 864])
        W1T = wsm[0:R, 0:H]
        W2T = wsm[0:H + 1, 48:96]
        L2WT = wsm[0:H + 1, 96:144]
        L3Ws = wsm[0:H, 144:192]
        EU = wsm[0:NEL, 192:256]
        b1c = wsm[0:H, 256:257]
        embT = wsm[0:GE, 257:257 + NEL]
        adT = wsm[0:GE, 376:408]
        w1raw = wsm[0:H, 408:448]
        w2raw = wsm[0:H, 448:496]
        l2raw = wsm[0:H, 496:544]
        adraw = wsm[0:GE, 544:576]
        b1raw = wsm[0:1, 576:624]
        vecs = [wsm[:, 624 + 48 * a:672 + 48 * a] for a in range(5)]

        A1 = sb("A1", [P, AW])
        idxs = sb("idxs", [P, 2, Q], I32)

        RI = ACC[:, 0:1024].bitcast(I32).rearrange("p (a b e) -> p a b e", a=2, b=4)
        RF = ACC[:, 1024:3584].rearrange("p (a b e) -> p a b e", a=5, b=4)
        zb = [ACC[0:NEL, 4096 + 1024 * s:5120 + 1024 * s].bitcast(I32) for s in range(2)]
        zoh = [ACC[0:NEL, 6144 + 1024 * s:7168 + 1024 * s] for s in range(2)]
        st0 = [ACC[:, 8192 + 640 * s:8832 + 640 * s].rearrange("p (t c) -> p t c", t=U) for s in range(2)]
        stu = [ACC[:, 9600 + 264 * s:9864 + 264 * s].rearrange("p (t c) -> p t c", t=U) for s in range(2)]

        o = 0

        def cut(n):
            nonlocal o
            o += n
            assert o <= AW, o
            return A1[:, o - n:o]

        gat = cut(U * K1).rearrange("p (k c) -> p k c", k=U)
        gatb = gat.rearrange("p k c -> p (k c)")[:, 0:U * PARTS * H // 2].bitcast(BF16).rearrange(
            "p (k b c) -> p k b c", k=U, b=PARTS)
        oneh = sb("oneh", [P, U, W * P], BF16)
        wrow = cut(U * C0).rearrange("p (k c) -> p k c", k=U)
        wpar = cut(U * PARTS * C0 // 2).bitcast(BF16).rearrange("p (k b c) -> p k b c", k=U, b=PARTS)
        NS = 5
        wst = cut(U * 3).bitcast(BF16).rearrange("p (k c) -> p k c", k=U)
        drow = [cut(Q * P) for _ in range(2)]
        lrow = [cut(Q * P) for _ in range(2)]
        tmpc, tmpd, tmpi = drow[0][:, 0:T], drow[1][:, 0:T], lrow[0][:, 0:T].bitcast(I32)
        tmpr = lrow[1][:, 0:T]
        dtra = lcol
        cj = lcol
        resc = mcol
        keyd = [cut(Q * P).rearrange("p (k c) -> p k c", k=Q) for _ in range(2)]
        mloc = cut(2 * Q).rearrange("p (g k) -> p g k", g=2)
        lm = cut(2 * Q).rearrange("p (g k) -> p g k", g=2)
        mf, mr = cut(Q), cut(Q)
        cand, cinv, cpen = cut(W * Q), cut(W * Q), cut(W * Q)
        dif = cut(2 * 2 * W * Q).rearrange("p (g h k) -> p g h k", g=2, h=2)
        prod = [cut(2 * W * C0) for _ in range(2)]
        junk = cut(Q * P // 2).bitcast(BF16).rearrange("p (k c) -> p k c", k=Q)
        rest = cut(Q * C0).rearrange("p (k c) -> p k c", k=Q)
        junk1 = prod[0][:, 0:P]
        zero = cut(U * C1)
        att = [ACC[:, 160 * s:160 * s + 160].rearrange("p (k c) -> p k c", k=Q) for s in range(2)]
        vse = [ACC[:, 320 + 128 * s:448 + 128 * s].rearrange("p (k c) -> p k c", k=Q) for s in range(2)]
        attT = [ACC[0:R, 600 + 512 * s:1112 + 512 * s] for s in range(2)]
        hid = [ACC[0:H + 1, 1700 + 512 * s:2212 + 512 * s] for s in range(2)]
        msg = [ACC[:, 2800 + 200 * s:3000 + 200 * s].rearrange("p (k c) -> p k c", k=Q) for s in range(2)]
        osum = [ACC[:, 3200 + 200 * s:3400 + 200 * s].rearrange("p (k c) -> p k c", k=Q) for s in range(2)]
        eqm = [ACC[:, 3600 + 512 * s:4112 + 512 * s].rearrange("p (k c) -> p k c", k=Q) for s in range(2)]
        uv = ACC[:, 4700:4828].rearrange("p (k c) -> p k c", k=Q)
        m1 = ACC[:, 4900:5092].rearrange("p (k c) -> p k c", k=Q)
        m2 = ACC[:, 5100:5292].rearrange("p (k c) -> p k c", k=Q)
        adp = ACC[:, 5300:5304]
        qmu = ACC[:, 5304:5308]
        rank = ACC[:, 5308:5316].rearrange("p (g k) -> p g k", g=2)
        idf = ACC[:, 5316:5320]
        aload = [[ACC[:, 5400 + 700 * (4 * s + k):6100 + 700 * (4 * s + k)] for k in range(TABLES)] for s in range(2)]
        NCOL = CH * H
        ybuf, sbuf_, tbuf, ubuf = (A1[:, NCOL * a:NCOL * (a + 1)] for a in range(4))
        stg = [A1[:, 2800 + 1008 * s:3808 + 1008 * s].bitcast(BF16).rearrange("p (j b c) -> p j b c", b=PARTS, c=H)
               for s in range(2)]
        small = [A1[:, 4900 + 16 * a:4900 + 16 * a + CH] for a in range(8)]
        onehf = oneh[:, :, :].rearrange("p k c -> p (k c)").bitcast(F32)
        hT = onehf[0:H + 1, 0:1024]
        hT2 = onehf[0:H + 1, 1024:2048]

        psum = ctx.enter_context(nc.psum_tensor("psum", [P, 8, 512], F32))

        CR = 52
        states = dram("states", (P * T + P, CR))
        statev = states[0:P * T, :].rearrange("(p j) c -> p (j c)", p=P)
        RA = A1[:, U * K1:U * K1 + 2800]
        req, rt1, rjunk, rdk, rdl = (RA[:, a * P:(a + 1) * P] for a in range(5))
        rw, rst, rnew, rs_ = (RA[:, 640 + CR * a:640 + CR * (a + 1)] for a in range(4))
        rc = [RA[:, 848 + a:849 + a] for a in range(16)]
        rd2 = RA[:, 864:866]
        rdf = RA[:, 868:868 + 2 * CH]
        rchunk = RA[:, 1024:1024 + CH * CR]
        rzero = RA[:, 2048:2048 + CH * CR]

        r_go, r_zero, r_init, r_ld, r_use, r_pl, r_x, r_ix, r_st, r_q, r_bk, r_lm, r_ex, r_w, r_mm, r_df, r_dx, \
            r_new, r_sc, r_dv, r_mf, r_mx = (sem("r_" + n) for n in (
                "go", "zero", "init", "ld", "use", "pl", "x", "ix", "st", "q", "bk", "lm", "ex", "w", "mm", "df",
                "dx", "new", "sc", "dv", "mf", "mx"))
        s_const = sem("s_const")
        s_pad = sem("s_pad")
        s_rows = sem("s_rows")
        s_w = sem("s_w")
        s_rowf = sem("s_rowf")
        s_rowd = sem("s_rowd")
        s_tp = sem("s_tp")
        s_cp = sem("s_cp")
        s_bb = sem("s_bb")
        s_flag = sem("s_flag")
        s_zl = [sem(f"s_zl{s}") for s in range(2)]
        s_zo, s_zm, s_ze, s_zx = sem("s_zo"), sem("s_zm"), sem("s_ze"), sem("s_zx")
        s_zs = [sem(f"s_zs{s}") for s in range(2)]
        s_prep = sem("s_prep")
        s_dv = sem("s_dv")
        s_pl = sem("s_pl")
        s_tick = sem("s_tick")
        s_ask, s_ans = sem("s_ask"), sem("s_ans")
        s_ga = [sem(f"s_ga{k}") for k in range(U)]
        s_rl = [sem(f"s_rl{g}") for g in range(2)]
        s_vs = [sem(f"s_vs{g}") for g in range(2)]
        s_key, s_edge, s_oh, s_wr, s_sc0, s_hi, s_par, s_mm, s_df, s_dx, s_cmb, s_rdone = (sem(n) for n in (
            "s_key", "s_edge", "s_oh", "s_wr", "s_scl", "s_hi", "s_par", "s_mm", "s_df", "s_dx", "s_cmb", "s_rdone"))
        s_zero = sem("s_zero")
        s_n0 = sem("s_n0")
        s_t1 = sem("s_t1")
        s_al = [sem(f"s_al{g}") for g in range(2)]
        s_at, s_ac, s_hd, s_si, s_gt, s_ms, s_eq, s_os, s_oc, s_sx, s_rs = (sem(n) for n in (
            "s_at", "s_ac", "s_hd", "s_si", "s_gt", "s_ms", "s_eq", "s_os", "s_oc", "s_sx", "s_rs"))
        s_sc = [sem(f"s_sc{k}") for k in range(U)]
        s_ld = [sem(f"s_ld{g}") for g in range(2)]
        s_sum, s_n1 = sem("s_sum"), sem("s_n1")
        s_t2 = [sem(f"s_t2{g}") for g in range(2)]
        s_acz = sem("s_acz")
        s_oh2, s_mm2, s_cm2, s_gu2 = [sem("s_oh2"), sem("s_oh3")], [sem("s_mm2"), sem("s_mm3")], \
            [sem("s_cm2"), sem("s_cm3")], sem("s_gu2")
        s_na, s_ntp, s_ncp, s_nmm = sem("s_na"), sem("s_ntp"), sem("s_ncp"), sem("s_nmm")
        s_n2 = sem("s_n2")
        s_t3 = sem("s_t3")
        s_bn, s_bm = sem("s_bn"), sem("s_bm")
        s_n3 = sem("s_n3")
        s_out = sem("s_out")

        block = ctx.enter_context(nc.Block())

        @block.sync
        def _(sp):
            def residual(r):
                sp.wait_ge(s_flag, 3)
                more = sp.value_load(flag[0:1, 0:1], min_val=0, max_val=T * P)
                with sp.If(more > 0):
                    sp.wait_ge(r_zero, r + 1)
                    with sp.Fori(0, NC) as c:
                        sp.dma_start(statev[:, bass.ds(c * (CH * CR), CH * CR)], rzero).then_inc(r_init, 16)
                    sp.dma_start(states[P * T:P * T + P, :], rzero[:, 0:CR]).then_inc(r_init, 16)
                    sp.wait_ge(r_sc, 16 * T * (r + 1))
                    sp.dma_start(rchunk, statev[:, 0:CH * CR]).then_inc(r_ld, 16)
                    with sp.Fori(1, NC) as c:
                        sp.wait_ge(r_use, c * 1 + NC * r)
                        sp.dma_start(rchunk, statev[:, bass.ds(c * (CH * CR), CH * CR)]).then_inc(r_ld, 16)

            sp.wait_ge(s_pad, 1)
            sp.dma_start(RI[0:6, 0, 3, :], dst[384 * P:FULL * P].rearrange("(p e) -> p e", e=P)).then_inc(s_rows, 16)
            for a, arr in enumerate((dst, src, ew1.rearrange("e a -> (e a)"), ew, nvec)):
                to = RI[:, a] if a < 2 else RF[:, a]
                sp.dma_start(to[:, 0:3, :], arr[0:384 * P].rearrange("(b p e) -> p b e", b=3, e=P)).then_inc(s_rows, 16)
                if a:
                    sp.dma_start(to[0:6, 3, :], arr[384 * P:FULL * P].rearrange("(p e) -> p e", e=P)).then_inc(s_rows, 16)
                sp.dma_start(to[6:7, 3, 0:REST], arr[FULL * P:N].rearrange("(a e) -> a e", a=1)).then_inc(s_rows, 16)
            for to, of in ((w1raw, W1), (w2raw, W2), (l2raw, L2W), (adraw, adaptW),
                           (EU[:, 0:GE], emb), (L3Ws, L3W),
                           (W2T[H:H + 1, :], b2.rearrange("(a n) -> a n", a=1)),
                           (L2WT[H:H + 1, :], L2b.rearrange("(a n) -> a n", a=1)),
                           (b1raw, b1.rearrange("(a n) -> a n", a=1))):
                sp.dma_start(to, of).then_inc(s_w, 16)
            for a, v in enumerate((gamma, beta, L3b, L3g, L3be)):
                sp.dma_start(vecs[a], v.partition_broadcast(P)).then_inc(s_w, 16)
            sp.dma_start(X[:, 0:FULL, :], x[0:FULL * P, :].rearrange("(j p) c -> p j c", p=P)).then_inc(s_rows, 16)
            sp.dma_start(X[0:REST, FULL, :], x[FULL * P:N, :]).then_inc(s_rows, 16)
            sp.wait_ge(s_rowf, 1)
            for a in range(3):
                v = rows_d[a].rearrange("(t e) -> t e", e=P)
                sp.dma_start(v[0:384, :].rearrange("(b p) e -> p b e", b=3), RF[:, a, 0:3, :]).then_inc(s_rowd, 16)
                sp.dma_start(v[384:T, :], RF[0:U, a, 3, :]).then_inc(s_rowd, 16)

            def load_z(m, s):
                n = min(U * P, N - U * P * (IT - 1)) if (not is_reg(m) and m == IT - 1) else U * P
                wait(sp, s_zo, m - 1)
                sp.dma_start(zb[s][:, 0:n], ntype[bass.ds(m * (U * P), n)].partition_broadcast(NEL)).then_inc(s_zl[s], 16)

            def store_z(m, s):
                sp.wait_ge(s_ze, m * 1 + 1)
                sp.wait_ge(s_zx, m * 1 + 1)
                sp.dma_start(tab0v[:, bass.ds(m * U, U), :], st0[s]).then_inc(s_zs[s], 16)
                sp.dma_start(tab1v[:, bass.ds(m * U, U), H:K1], stu[s]).then_inc(s_zs[s], 16)

            sp.wait_ge(s_pad, 2)
            load_z(0, 0)
            load_z(1, 1)
            store_z(0, 0)
            load_z(2, 0)
            store_z(1, 1)
            with sp.Fori(1, IT // 2 - 1) as q:
                load_z(q * 2 + 1, 1)
                store_z(q * 2, 0)
                load_z(q * 2 + 2, 0)
                store_z(q * 2 + 1, 1)
            load_z(IT - 2, 1)
            store_z(IT - 3, 0)
            load_z(IT - 1, 0)
            store_z(IT - 2, 1)
            store_z(IT - 1, 0)

            def rows0(it):
                for g in range(2):
                    n = it * 2 + g
                    wait(sp, s_rdone, n - 1)
                    wait(sp, s_key, n * Q - Q)
                    for to, a in ((drow[g], 0), (lrow[g], 2)):
                        sp.dma_start(to, rows_d[a][bass.ds(n * (Q * P), Q * P)].partition_broadcast(P)).then_inc(s_rl[g], 16)

            def side0(it):
                for g in range(2):
                    for k in range(Q):
                        sp.wait_ge(s_ga[g * Q + k], it * 16 + 16)
                    sp.dma_start(srcemb[:, bass.ds(it * (U * GE) + g * Q * GE, Q * GE)].rearrange("p (k c) -> p k c", k=Q),
                                 gat[:, g * Q:(g + 1) * Q, H:K0]).then_inc(s_vs[g], 16)
                for k in range(TABLES):
                    sp.dma_start(aggv[k][:, bass.ds(it * (U * C1), U * C1)], zero[:, :]).then_inc(s_zero, 16)

            sp.wait_ge(s_rowd, 96)
            sp.wait_ge(s_acz, 1)
            for k in range(TABLES):
                sp.dma_start(aggs[k][P * T:P * T + P, :], zero[:, 0:C1]).then_inc(s_zero, 16)
            rows0(0)
            with sp.Fori(0, IT - 1) as it:
                rows0(it + 1)
                side0(it)
            side0(IT - 1)

            residual(0)

            def out0(c):
                sp.wait_ge(s_n0, c * 1 + 1)
                sp.dma_start(tab1v[:, bass.ds(c * CH, CH), 0:H], X[:, bass.ds(c * CH, CH), :]).then_inc(s_t1, 16)
            turns(sp, NC, out0)

            def load1(it, last=False):
                for g in range(2):
                    n = it * 2 + g
                    tail = last and g == 1
                    wait(sp, s_at, n - 1)
                    wait(sp, s_rs, n - 1)
                    if tail:
                        r = FULL - (T - Q)
                        sp.dma_start(att[g][:, 0:r, :], attr[(T - Q) * P:FULL * P, :].rearrange("(k p) c -> p k c", p=P)).then_inc(s_al[g], 16)
                        sp.dma_start(att[g][0:REST, r, :], attr[FULL * P:N, :]).then_inc(s_al[g], 16)
                    else:
                        sp.dma_start(att[g], attr[bass.ds(n * (Q * P), Q * P), :].rearrange("(k p) c -> p k c", p=P)).then_inc(s_al[g], 16)
                    sp.dma_start(vse[g], srcemb[:, bass.ds(n * (Q * GE), Q * GE)].rearrange("p (k c) -> p k c", k=Q)).then_inc(s_al[g], 16)
                    sp.dma_start(drow[g], rows_d[1][bass.ds(n * (Q * P), Q * P)].partition_broadcast(P)).then_inc(s_al[g], 16)
            for g in range(2):
                sp.wait_ge(s_vs[g], 16 * IT)
            load1(0)
            with sp.Fori(1, IT - 1) as it:
                load1(it)
            load1(IT - 1, True)

            for k in range(U):
                sp.wait_ge(s_sc[k], 16 * IT)

            def load_a(c, s):
                wait(sp, s_sum, c - 1)
                for k in range(TABLES):
                    sp.dma_start(aload[s][k], aggv[k][:, bass.ds(c * (CH * C1), CH * C1)]).then_inc(s_ld[s], 16)

            def store_a(c, s):
                sp.wait_ge(s_n1, c * 1 + 1)
                sp.dma_start(tab2v[:, bass.ds(c * CH, CH), :], stg[s].rearrange("p j b c -> p j (b c)")).then_inc(s_t2[s], 16)
            load_a(0, 0)
            load_a(1, 1)
            store_a(0, 0)
            load_a(2, 0)
            store_a(1, 1)
            with sp.Fori(1, NC // 2 - 1) as q:
                load_a(q * 2 + 1, 1)
                store_a(q * 2, 0)
                load_a(q * 2 + 2, 0)
                store_a(q * 2 + 1, 1)
            load_a(NC - 1, 1)
            store_a(NC - 2, 0)
            store_a(NC - 1, 1)

            residual(1)

            def out2(it):
                sp.wait_ge(s_n2, it * 1 + 1)
                sp.dma_start(tab3v[:, bass.ds(it * U, U), :], stg[0][:, 0:U].rearrange("p j b c -> p j (b c)")).then_inc(s_t3, 16)
            turns(sp, IT, out2)

            residual(2)

            def out3(c):
                sp.wait_ge(s_n3, c * 1 + 1)
                sp.dma_start(out[bass.ds(c * (CH * P), CH * P), :].rearrange("(j p) c -> p j c", p=P),
                             X[:, bass.ds(c * CH, CH), :]).then_inc(s_out, 16)
            with sp.Fori(0, NC - 1) as c:
                out3(c)
            sp.wait_ge(s_n3, NC)
            j = (NC - 1) * CH
            sp.dma_start(out[j * P:FULL * P, :].rearrange("(j p) c -> p j c", p=P), X[:, j:FULL, :]).then_inc(s_out, 16)
            sp.dma_start(out[FULL * P:N, :], X[0:REST, FULL, :]).then_inc(s_out, 16)
            sp.wait_ge(s_out, 16 * (NC + 1))
            sp.wait_ge(s_t3, 16 * IT)

        @block.gpsimd
        def _(pool):
            own = Tally(s_pl)

            def link(ins):
                pool.wait_ge(s_pl, own.add(ins))

            def tick(v):
                if is_reg(v):
                    pool.sem_inc(s_tick)

            link(pool.memset(ident[:, :], 0.0))
            link(pool.affine_select(out=ident[:, :], in_=ident[:, :], compare_op=ALU.not_equal, fill=1.0,
                                    base=0, pattern=[[-1, P]], channel_multiplier=1))
            link(pool.memset(tril[:, :], 1.0))
            link(pool.affine_select(out=tril[:, :], in_=tril[:, :], compare_op=ALU.is_gt, fill=0.0,
                                    base=0, pattern=[[-1, P]], channel_multiplier=1))
            link(pool.iota(iota[:, :], [[1, W * P]], base=0, channel_multiplier=0, allow_small_or_imprecise_dtypes=True))
            link(pool.iota(pcol[:, 6:7], [[1, 1]], base=0, channel_multiplier=1, allow_small_or_imprecise_dtypes=True))
            link(pool.iota(trash, [[1, 1]], base=P * T, channel_multiplier=1, allow_small_or_imprecise_dtypes=True))
            pool.memset(ones[:, :], 1.0).then_inc(s_const, 1)

            def gathers(table, to, index, it, g, free):
                free()
                pool.tensor_copy(idx[:, g, :], index[:, bass.ds(it * U + g * Q, Q)]).then_inc(s_pl, 1)
                own.k += 1
                pool.wait_ge(s_pl, own.value())
                tick(it)
                for k in range(Q):
                    pool.indirect_dma_start(to(g * Q + k), None, table[:, :],
                                            bass.IndirectOffsetOnAxis(ap=idx[:, g, k:k + 1], axis=0)).then_inc(s_ga[g * Q + k], 16)

            def residual(r, table):
                pool.wait_ge(s_flag, 3)
                more = pool.value_load(flag[0:1, 0:1], min_val=0, max_val=T * P)
                with pool.If(more > 0):
                    for g in range(2):
                        pool.wait_ge(s_vs[g], 16 * IT)
                    pool.wait_ge(r_go, r + 1)
                    pool.wait_ge(r_init, 16 * (NC + 1) * (r + 1))

                    def body(i):
                        n = i + T * r
                        wait(pool, r_sc, n * 16)
                        pool.tensor_copy(idx[:, 0, 0:1], gsrc[:, bass.ds(i, 1)]).then_inc(r_pl, 1)
                        pool.wait_ge(r_pl, n + 1)
                        tick(i)
                        to = gat[:, 0, 0:K0] if r == 0 else gatb[:, 0].rearrange("p b c -> p (b c)")
                        pool.indirect_dma_start(to, None, table[:, :],
                                                bass.IndirectOffsetOnAxis(ap=idx[:, 0, 0:1], axis=0)).then_inc(r_x, 16)
                        pool.wait_ge(r_ix, n + 1)
                        tick(i)
                        pool.indirect_dma_start(rst, None, states[:, :],
                                                bass.IndirectOffsetOnAxis(ap=idx[:, 1, 0:1], axis=0)).then_inc(r_st, 16)
                        pool.wait_ge(r_new, n + 1)
                        tick(i)
                        pool.indirect_dma_start(states[:, :], bass.IndirectOffsetOnAxis(ap=idxs[:, 0, 0:1], axis=0),
                                                rnew, None).then_inc(r_sc, 16)
                    turns(pool, T, body)

            pool.wait_ge(s_prep, 1)
            pool.wait_ge(s_zs[0], 32 * (IT // 2 + 1))
            pool.wait_ge(s_zs[1], 32 * (IT // 2))

            def free0(it, g):
                n = it * 2 + g
                if is_reg(it) or it > 0:
                    pool.wait_ge(s_vs[g], it * 16)
                    pool.wait_ge(s_sc0, n * 4 - 4)
                    for k in range(Q):
                        pool.wait_ge(s_ga[g * Q + k], it * 16)
                    tick(it)

            def body0(it):
                own.turn(it, 2)
                for g in range(2):
                    gathers(tab0, lambda k: gat[:, k, 0:K0], gsrc, it, g, lambda: free0(it, g))
            turns(pool, IT, body0)
            own.close(IT)
            residual(0, tab0)

            pool.wait_ge(s_t1, 16 * NC)
            pool.wait_ge(s_zero, 16 * TABLES * (IT + 1))

            def free1(it, g):
                n = it * 2 + g
                if is_reg(it) or it > 0:
                    pool.wait_ge(s_ms, n * 1 - 1)
                    for k in range(Q):
                        pool.wait_ge(s_ga[g * Q + k], it * 16 + 16 * IT)
                    tick(it)

            def scatter(it, g):
                n = it * 2 + g
                pool.wait_ge(s_oc, n * 1 + 1)
                pool.wait_ge(s_sx, n * 1 + 1)
                for k in range(Q):
                    wait(pool, s_sc[(1 - g) * Q + k], it * 16 + 16 * g)
                tick(it)
                for k in range(Q):
                    pool.indirect_dma_start(aggs[k][:, :], bass.IndirectOffsetOnAxis(ap=idxs[:, g, k:k + 1], axis=0),
                                            osum[g][:, k, :], None, compute_op=ALU.add).then_inc(s_sc[g * Q + k], 16)

            def body1(it, last=False):
                own.turn(it, 2)
                own.k = 1
                gathers(tab1, lambda k: gat[:, k, :], gdst, it, 1, lambda: free1(it, 1))
                scatter(it, 0)
                if not last:
                    own.turn(it + 1, 2)
                    gathers(tab1, lambda k: gat[:, k, :], gdst, it + 1, 0, lambda: free1(it + 1, 0))
                scatter(it, 1)
            own.turn(0, 2)
            gathers(tab1, lambda k: gat[:, k, :], gdst, 0, 0, lambda: None)
            body1(0)
            with pool.Fori(1, IT - 1) as it:
                body1(it)
            body1(IT - 1, True)
            own.close(IT)

            for layer in range(2):
                if layer == 0:
                    pool.wait_ge(s_t2[0], 16 * (NC // 2))
                    pool.wait_ge(s_t2[1], 16 * (NC // 2))
                else:
                    pool.wait_ge(s_t3, 16 * IT)

                def free2(it, g):
                    n = it * 2 + g
                    if is_reg(it) or it > 0:
                        pool.wait_ge(s_mm2[layer], n * 1 - 1)
                        for k in range(Q):
                            pool.wait_ge(s_ga[g * Q + k], it * 16 + 16 * IT * (2 + layer))
                        tick(it)

                def body2(it):
                    own.turn(it, 2)
                    for g in range(2):
                        gathers((tab2, tab3)[layer], lambda k: gatb[:, k].rearrange("p b c -> p (b c)"), gsrc, it, g, lambda: free2(it, g))
                turns(pool, IT, body2)
                own.close(IT)
                residual(1 + layer, (tab2, tab3)[layer])

        @block.scalar
        def _(act):
            def tick(v):
                if is_reg(v):
                    act.sem_inc(s_tick)

            def emb_out(m, s):
                act.wait_ge(s_zm, m * 1 + 1)
                if is_reg(m) or m > 1:
                    act.wait_ge(s_zs[s], 16 * (m - s))
                ps = psum[:, s, :].rearrange("p (t c) -> p t c", c=2 * GE)
                act.copy(st0[s][:, :, H:K0], ps[:, :, 0:GE])
                act.copy(stu[s][:, :, 0:GE], ps[:, :, GE:2 * GE]).then_inc(s_ze, 1)
            emb_out(0, 0)
            emb_out(1, 1)
            with act.Fori(1, IT // 2) as q:
                emb_out(q * 2, 0)
                emb_out(q * 2 + 1, 1)
            emb_out(IT - 1, 0)
            act.wait_ge(s_ask, 1)
            act.activation(tmpc[:, :], tmpd[:, :], ACT.Sin, bias=halfpi, scale=-PI / 6.0).then_inc(s_ans, 1)

            def residual(r):
                act.wait_ge(s_flag, 3)
                more = act.value_load(flag[0:1, 0:1], min_val=0, max_val=T * P)
                if r:
                    return
                with act.If(more > 0):
                    def body(i):
                        act.wait_ge(r_lm, i + 1)
                        act.activation(rw[:, H:H + 1], rc[6], ACT.Exp).then_inc(r_ex, 1)
                        act.wait_ge(r_df, i + 1)
                        act.activation(rd2, rd2, ACT.Exp).then_inc(r_dx, 1)
                    turns(act, T, body)

                    def merge(c):
                        act.wait_ge(r_mf, c + 1)
                        act.activation(rdf, rdf, ACT.Exp).then_inc(r_mx, 1)
                    turns(act, NC, merge)

            def keys0(it, g):
                n = it * 2 + g
                act.wait_ge(s_rl[g], it * 32 + 32)
                wait(act, s_rdone, n - 1)
                tick(it)
                for k in range(Q):
                    act.activation(keyd[g][:, k, :], drow[g][:, k * P:(k + 1) * P], ACT.Abs,
                                   bias=dcol[:, bass.ds(it * U + g * Q + k, 1)], scale=KEY).then_inc(s_key, 1)

            def factors0(it, g, W):
                act.wait_ge(s_df, it * 2 + g + 1)
                d = dif[:, g, :, 0:Q * W]
                act.activation(d, d, ACT.Exp).then_inc(s_dx, 1)

            def group0(it, g, W, after):
                n = it * 2 + g
                act.wait_ge(s_edge, n * 1 + 1)
                wait(act, s_par, n - 1)
                tick(it)
                act.activation(wrow[:, g * Q:(g + 1) * Q, H], lm[:, g, :], ACT.Exp).then_inc(s_wr, 1)
                act.wait_ge(s_wr, n * 1 + 1)
                for k in range(g * Q, (g + 1) * Q):
                    act.wait_ge(s_ga[k], it * 16 + 16)
                    act.mul(wrow[:, k, 0:H], gat[:, k, 0:H], wrow[:, k, H:H + 1]).then_inc(s_sc0, 1)
                act.wait_ge(s_sc0, n * Q + Q)
                wait(act, s_mm, n - 1)
                act.copy(wpar[:, g * Q:(g + 1) * Q, 0, :], wrow[:, g * Q:(g + 1) * Q, :]).then_inc(s_hi, 1)
                if g:
                    factors0(it, 0, W)
                elif is_reg(it) or it > 0:
                    factors0(it - 1, 1, W if before[0] is None else before[0])
                if after is not None:
                    keys0(it + 1, g)

            before = [None]

            def body0(it, w, after):
                before[0] = next((SEGS[n - 1][2] for n, (a, _, _) in enumerate(SEGS) if n and not is_reg(it) and a == it), None)
                group0(it, 0, w, after)
                group0(it, 1, w, after)
            keys0(0, 0)
            keys0(0, 1)
            segments(act, body0)
            factors0(IT - 1, 1, SEGS[-1][2])
            residual(0)

            asked = Tally(s_ask)
            asked.base = 1
            said = Tally(s_ans)
            said.base = 1

            def answer(o_, i_, f, **kw):
                asked.k += 1
                act.wait_ge(s_ask, asked.value())
                act.activation(o_, i_, f, **kw).then_inc(s_ans, 1)

            def nodes0(c):
                asked.turn(c, 2)
                answer(ubuf, tbuf, ACT.Exp)
                answer(small[2], small[1], ACT.Sqrt, bias=epsc, scale=1.0 / H)
            turns(act, NC, nodes0)
            asked.close(NC)

            def group1(it, g):
                n = it * 2 + g
                act.wait_ge(s_at, n * 1 + 1)
                act.copy(attT[g], psum[0:R, g, :]).then_inc(s_ac, 1)
                act.wait_ge(s_hd, n * 1 + 1)
                act.activation(hid[g][0:H, :], psum[0:H, 2 + g, :], ACT.Silu, bias=b1c).then_inc(s_si, 1)
                act.wait_ge(s_os, n * 1 + 1)
                if is_reg(it) or it > 0:
                    for k in range(Q):
                        act.wait_ge(s_sc[g * Q + k], it * 16)
                act.copy(osum[g], psum[:, 6 + g, 0:Q * C1].rearrange("p (k c) -> p k c", k=Q)).then_inc(s_oc, 1)

            def body1(it):
                group1(it, 0)
                group1(it, 1)
            act.wait_ge(s_acz, 2)
            turns(act, IT, body1)

            def nodes1(q):
                asked.turn(q, 6)
                for s in range(2):
                    answer(small[2], small[1], ACT.Sqrt, bias=epsc, scale=1.0 / H)
                    answer(small[2], small[1], ACT.Sqrt, bias=epsc, scale=1.0 / H)
                    answer(small[5], small[4], ACT.Sqrt)
            turns(act, NC // 2, nodes1)
            asked.close(NC // 2)

            residual(1)
            answer(cj, tbuf[:, 0:T], ACT.Sqrt)
            answer(smax[:, 0:T], tbuf[:, 0:T], ACT.Sqrt)
            asked.base, asked.k = asked.base + asked.k, 0
            def nodes2(it):
                asked.turn(it, 1)
                act.wait_ge(s_ntp, it * 2 + 1)
                act.copy(hT[0:H, :].rearrange("p (b c) -> p b c", b=2), psum[0:H, 0:2, :]).then_inc(s_ncp, 1)
                answer(small[2][:, 0:U], small[1][:, 0:U], ACT.Sqrt, bias=epsc, scale=1.0 / H)
                act.wait_ge(s_ntp, it * 2 + 2)
                act.copy(hT2[0:H, :].rearrange("p (b c) -> p b c", b=2), psum[0:H, 0:2, :]).then_inc(s_ncp, 1)
            turns(act, IT, nodes2)
            asked.close(IT)

            answer(small[2][:, 0:1], small[1][:, 0:1], ACT.Copy)
            asked.base, asked.k = asked.base + asked.k, 0
            answer(ybuf[:, 0:H], tbuf[:, 0:H], ACT.Sqrt, bias=epsc, scale=1.0 / N)
            asked.base, asked.k = asked.base + asked.k, 0

            def nodes3(c):
                asked.turn(c, 1)
                answer(small[2], small[1], ACT.Sqrt, bias=epsc, scale=1.0 / H)
            turns(act, NC, nodes3)

        @block.tensor
        def _(pe):
            tile = [slice(k * P, (k + 1) * P) for k in range(U)]

            def tick(v):
                if is_reg(v):
                    pe.sem_inc(s_tick)

            def residual(r):
                pe.wait_ge(s_flag, 3)
                more = pe.value_load(flag[0:1, 0:1], min_val=0, max_val=T * P)
                with pe.If(more > 0):
                    def body(i):
                        n = i + T * r
                        pe.wait_ge(r_q, n + 1)
                        tick(i)
                        mm = pe.matmul(psum[:, 0, 0:P], ones[:, :], rdk, start=True, stop=True)
                        if r == 0:
                            mm = pe.matmul(psum[:, 0, P:2 * P], ones[:, :], rdl, start=True, stop=True)
                        mm.then_inc(r_bk, 1)
                        pe.wait_ge(r_w, n + 1)
                        tick(i)
                        pe.matmul(psum[:, 1, 0:CR - 2], req, rw[:, 0:CR - 2], start=True, stop=True).then_inc(r_mm, 1)
                    turns(pe, T, body)

            pe.wait_ge(s_const, 1)
            pe.wait_ge(s_w, 16 * 14)
            pe.transpose(psum[0:R, 0, 0:H], w1raw, ident[0:H, 0:H])
            pe.transpose(psum[0:H, 0, 64:64 + H], w2raw, ident[0:H, 0:H])
            pe.transpose(psum[0:H, 0, 128:128 + H], l2raw, ident[0:H, 0:H])
            pe.transpose(psum[0:GE, 0, 192:192 + GE], adraw, ident[0:GE, 0:GE])
            pe.transpose(psum[0:GE, 0, 256:256 + NEL], EU[:, 0:GE], ident[0:NEL, 0:NEL])
            pe.transpose(psum[0:H, 0, 400:401], b1raw, ident[0:1, 0:1]).then_inc(s_tp, 1)
            pe.wait_ge(s_cp, 1)
            pe.matmul(psum[0:NEL, 0, 0:GE], embT, adT, start=True, stop=True).then_inc(s_tp, 1)
            pe.wait_ge(s_rowf, 1)
            for a in range(5):
                for b in range(4):
                    n = P if b < 3 else U
                    t = pe.transpose(psum[:, 1 + a, b * P:b * P + n], RF[0:n, a, b, :], ident[0:n, 0:n])
                t.then_inc(s_tp, 1)
            pe.wait_ge(s_cp, 7)
            pe.wait_ge(s_flag, 1)
            pe.matmul(psum[:, 6, 0:T], ones[0:1, :], tmpc[0:1, :], start=True, stop=True).then_inc(s_bb, 1)
            pe.wait_ge(s_flag, 2)
            pe.transpose(psum[0:1, 7, 0:P], flagr[:, :], ident[:, :]).then_inc(s_bb, 1)

            def emb_mm(m, s):
                pe.wait_ge(s_zo, m * 1 + 1)
                wait(pe, s_ze, m - 1)
                for k in range(U):
                    mm = pe.matmul(psum[:, s, k * 2 * GE:(k + 1) * 2 * GE], zoh[s][:, tile[k]], EU, start=True, stop=True)
                mm.then_inc(s_zm, 1)
            emb_mm(0, 0)
            emb_mm(1, 1)
            with pe.Fori(1, IT // 2) as q:
                emb_mm(q * 2, 0)
                emb_mm(q * 2 + 1, 1)
            emb_mm(IT - 1, 0)

            def group0(it, g, W):
                n = it * 2 + g
                wait(pe, s_cmb, n - 1)
                pe.wait_ge(s_oh, n * Q + Q)
                pe.wait_ge(s_edge, n * 1 + 1)
                for k in range(Q):
                    for w in range(W):
                        at = (k * W + w) * NS
                        pe.matmul(psum[:, 4 + g, at:at + NS], oneh[:, g * Q + k, tile[w]], wst[:, g * Q + k, 0:NS],
                                  start=True, stop=True)
                pe.wait_ge(s_par, n * 1 + 1)
                for k in range(Q):
                    for w in range(W):
                        at = ((k % 2) * W + w) * C0
                        for b in range(PARTS):
                            mm = pe.matmul(psum[:, 2 * g + k // 2, at:at + C0], oneh[:, g * Q + k, tile[w]],
                                           wpar[:, g * Q + k, b, :], start=b == 0, stop=b == PARTS - 1)
                mm.then_inc(s_mm, 1)

            def body0(it, w, _):
                group0(it, 0, w)
                group0(it, 1, w)
            segments(pe, body0)
            residual(0)

            def group1(it, g):
                n = it * 2 + g
                pe.wait_ge(s_al[g], it * 48 + 48 if is_reg(it) or it < IT - 1 or g == 0 else it * 48 + 64)
                wait(pe, s_ac, n - 1)
                tick(it)
                for k in range(Q):
                    t = pe.transpose(psum[0:R, g, tile[k]], att[g][:, k, :], ident[:, :])
                t.then_inc(s_at, 1)
                pe.wait_ge(s_ac, n * 1 + 1)
                wait(pe, s_si, n - 1)
                tick(it)
                pe.matmul(psum[0:H, 2 + g, :], W1T, attT[g], start=True, stop=True).then_inc(s_hd, 1)
                pe.wait_ge(s_si, n * 1 + 1)
                wait(pe, s_ms, n - 1)
                for k in range(Q):
                    mm = pe.matmul(psum[:, 4 + g, k * H:(k + 1) * H], hid[g][:, tile[k]], W2T, start=True, stop=True)
                mm.then_inc(s_gt, 1)
                pe.wait_ge(s_ms, n * 1 + 1)
                pe.wait_ge(s_eq, n * 1 + 1)
                wait(pe, s_oc, n - 1)
                for k in range(Q):
                    mm = pe.matmul(psum[:, 6 + g, k * C1:(k + 1) * C1], eqm[g][:, k, :], msg[g][:, k, :], start=True, stop=True)
                mm.then_inc(s_os, 1)

            def body1(it):
                group1(it, 0)
                group1(it, 1)
            pe.wait_ge(s_acz, 2)
            turns(pe, IT, body1)

            for layer in range(2):
                def group2(it, g, W):
                    n = it * 2 + g
                    wait(pe, s_cm2[layer], n - 1)
                    for k in range(Q):
                        pe.wait_ge(s_oh2[layer], it * U + g * Q + k + 1)
                        pe.wait_ge(s_ga[g * Q + k], it * 16 + 16 + 16 * IT * (2 + layer))
                        for w in range(W):
                            at = ((k % 2) * W + w) * C0
                            if layer == 0:
                                pe.matmul(psum[:, 2 * g + k // 2, at + H:at + C0], oneh[:, g * Q + k, tile[w]],
                                          oneb[:, 0:1], start=True, stop=True)
                            for b in range(PARTS):
                                mm = pe.matmul(psum[:, 2 * g + k // 2, at:at + H], oneh[:, g * Q + k, tile[w]],
                                               gatb[:, g * Q + k, b, :], start=b == 0, stop=b == PARTS - 1)
                    mm.then_inc(s_mm2[layer], 1)

                def body2(it, w, _):
                    group2(it, 0, w)
                    group2(it, 1, w)
                segments(pe, body2)
                residual(1 + layer)
                if layer:
                    break

                def nodes2(it):
                    for h, (to, wgt) in enumerate(((hT, L2WT), (hT2[0:H, :], L3Ws))):
                        pe.wait_ge(s_na, it * 2 + h + 1)
                        tick(it)
                        for k in range(U):
                            t = pe.transpose(psum[0:H, k // 4, (k % 4) * P:(k % 4 + 1) * P],
                                             ybuf[:, k * H:(k + 1) * H], ident[:, :])
                        t.then_inc(s_ntp, 1)
                        pe.wait_ge(s_ncp, it * 2 + h + 1)
                        for k in range(U):
                            mm = pe.matmul(psum[:, 2 + h, k * H:(k + 1) * H], to[:, tile[k]], wgt, start=True, stop=True)
                        mm.then_inc(s_nmm, 1)
                turns(pe, IT, nodes2)

            for h in range(2):
                pe.wait_ge(s_bn, h + 1)
                pe.matmul(psum[:, h, 0:H], ones[:, :], sbuf_[:, 0:H], start=True, stop=True).then_inc(s_bm, 1)

        @block.vector
        def _(dve):
            own = Tally(s_dv)
            V = nc.vector

            def link(ins):
                dve.wait_ge(s_dv, own.add(ins))

            def note(ins):
                own.add(ins)

            def tick(v):
                if is_reg(v):
                    dve.sem_inc(s_tick)

            def sync():
                dve.wait_ge(s_dv, own.value())

            note(V.memset(RI[:, :, 3, :], -1))
            note(V.memset(RF[:, 2:5, 3, :], 0.0))
            note(V.memset(W2T, 0.0))
            link(V.memset(L2WT, 0.0))
            V.memset(X[:, FULL:T, :], 0.0).then_inc(s_pad, 1)
            note(V.memset(zb[0], 0))
            note(V.memset(zb[1], 0))
            note(V.memset(zero[:, :], 0.0))
            note(V.memset(oneb[:, :], 1.0))
            note(V.memset(smax[:, :], -BIG))
            note(V.memset(halfpi, PI / 2.0))
            note(V.memset(epsc, EPS))
            note(V.memset(wst[:, :, NS - 1], 1.0))
            link(V.memset(valid, 0.0))
            V.memset(pcol[0:64, 4:5], 1.0).then_inc(s_pad, 1)
            note(V.memset(pcol[64:64 + REST - 64, 4:5], 1.0))
            dve.wait_ge(s_rows, 16 * (15 + 2))
            link(V.tensor_copy(RF[:, 0:2], RI))
            V.tensor_copy(flagf[:, 0:1], RF[0:1, 0, 0, 0:1]).then_inc(s_rowf, 1)
            dve.wait_ge(s_tp, 1)
            note(V.tensor_copy(W1T, psum[0:R, 0, 0:H]))
            note(V.tensor_copy(W2T[0:H, :], psum[0:H, 0, 64:64 + H]))
            note(V.tensor_copy(L2WT[0:H, :], psum[0:H, 0, 128:128 + H]))
            note(V.tensor_copy(adT, psum[0:GE, 0, 192:192 + GE]))
            note(V.tensor_copy(b1c, psum[0:H, 0, 400:401]))
            V.tensor_copy(embT, psum[0:GE, 0, 256:256 + NEL]).then_inc(s_cp, 1)
            sync()
            dve.wait_ge(s_tp, 2)
            V.tensor_copy(EU[:, GE:2 * GE], psum[0:NEL, 0, 0:GE]).then_inc(s_cp, 1)
            for a in range(5):
                dve.wait_ge(s_tp, 3 + a)
                V.tensor_copy(cols[:, a, :], psum[:, 1 + a, 0:T]).then_inc(s_cp, 1)
            dve.wait_ge(s_cp, 7)
            link(V.tensor_scalar(tmpc[0:1, :], dcol[0:1, :], 0.0, None, ALU.max))
            link(V.tensor_copy(tmpi[0:1, :], tmpc[0:1, :]))
            link(V.tensor_scalar(base[:, :], tmpi[0:1, :], 7, None, ALU.arith_shift_right))
            V.tensor_scalar(tmpc[0:1, :], base[:, :], float(P), None, ALU.mult).then_inc(s_flag, 1)
            dve.wait_ge(s_bb, 1)
            link(V.tensor_tensor(relc[:, :], dcol, psum[:, 6, 0:T], ALU.subtract))
            link(V.tensor_scalar(tmpc[:, :], relc[:, :], 0.0, None, ALU.is_ge))
            for a, b, w in SEGS:
                js = slice(a * U, b * U)
                note(V.scalar_tensor_tensor(tmpd[:, js], relc[:, js], float(w * P), tmpc[:, js], ALU.is_lt, ALU.mult))
            sync()
            link(V.tensor_scalar(tmpd[:, :], tmpd[:, :], -1.0, 1.0, ALU.mult, ALU.add))
            link(V.scalar_tensor_tensor(tmpc[:, :], dcol, 1.0, tmpd[:, :], ALU.add, ALU.mult))
            link(V.tensor_scalar(tmpr, tmpc[:, :], -1.0, None, ALU.add))
            V.tensor_reduce(flagr[:, :], tmpc[:, :], AX.X, ALU.max).then_inc(s_flag, 1)
            dve.wait_ge(s_bb, 2)
            link(V.tensor_reduce(flagf[:, 0:1], psum[0:1, 7, 0:P], AX.X, ALU.max))
            V.tensor_copy(flag[:, :], flagf[:, 0:1]).then_inc(s_flag, 1)
            for c_, to in ((scol, gsrc), (dcol, gdst)):
                link(V.tensor_scalar(tmpi[:, :], c_, 0.0, None, ALU.max))
                link(V.tensor_scalar(to[:, :], tmpi[:, :], 7, None, ALU.arith_shift_right))
                link(V.tensor_scalar(tmpi[:, :], tmpi[:, :], P - 1, None, ALU.bitwise_and))
                link(V.scalar_tensor_tensor(to[:, :], tmpi[:, :], float(T), to[:, :], ALU.mult, ALU.add))
            link(V.tensor_scalar(dcol, dcol, -KEY, None, ALU.mult))
            V.tensor_copy(tmpc[:, 0:1], dcol[:, 0:1]).then_inc(s_prep, 1)
            link(V.scalar_tensor_tensor(tmpd[:, :], ecol, -1.0, ecol, ALU.mult, ALU.max))
            V.tensor_scalar(tmpd[:, :], tmpd[:, :], 6.0, None, ALU.min).then_inc(s_ask, 1)

            def emb_oh(m, s):
                last = not is_reg(m) and m == IT - 1
                q = (m - s) // 2 if not is_reg(m) else None
                dve.wait_ge(s_zl[s], 8 * (m - s) + 16)
                wait(dve, s_zm, m - 1)
                V.tensor_scalar(zoh[s], zb[s], pcol[0:NEL, 6:7], None, ALU.is_equal).then_inc(s_zo, 1)
                if is_reg(m) or m > 1:
                    dve.wait_ge(s_zs[s], 16 * (m - s))
                    if is_reg(m):
                        dve.sem_inc(s_tick)
                note(V.tensor_copy(st0[s][:, :, 0:H], X[:, bass.ds(m * U, U), :]))
                link(V.tensor_copy(stu[s][:, :, GE], mcol[:, bass.ds(m * U, U)]))
                dve.sem_inc(s_zx)
            own.turn(0, 2)
            emb_oh(0, 0)
            own.turn(1, 2)
            emb_oh(1, 1)
            with dve.Fori(1, IT // 2) as q:
                own.turn(q * 2, 2)
                emb_oh(q * 2, 0)
                own.turn(q * 2 + 1, 2)
                emb_oh(q * 2 + 1, 1)
            own.turn(IT - 1, 2)
            emb_oh(IT - 1, 0)
            own.close(IT)
            dve.wait_ge(s_ans, 1)
            link(V.tensor_scalar(tmpc[:, :], tmpc[:, :], 0.5, 0.5, ALU.mult, ALU.add))
            link(V.scalar_tensor_tensor(ecol, ecol, 6.0, tmpc[:, :], ALU.is_lt, ALU.mult))
            link(V.tensor_copy(resc, tmpr))
            dve.wait_ge(s_rowd, 96)
            dve.wait_ge(s_zs[0], 32 * (IT // 2 + 1))
            dve.wait_ge(s_zs[1], 32 * (IT // 2))
            note(V.memset(ACC[:, :], 0.0))
            sync()
            dve.sem_inc(s_acz)

            def residual(r):
                more = V.value_load(flag[0:1, 0:1], min_val=0, max_val=T * P)
                with dve.If(more > 0):
                    mine = Tally(r_dv)
                    sizes = [(23, 8), (14, 1), (14, 1)]
                    per, perm = sizes[r]
                    mine.base = sum(3 + a * T + b * NC for a, b in sizes[:r])

                    def link(ins):
                        dve.wait_ge(r_dv, mine.add(ins))
                    link(V.memset(rzero, 0.0))
                    link(V.memset(rzero.rearrange("p (j c) -> p j c", c=CR)[:, :, 50], -BIG))
                    link(V.memset(rw, 1.0))
                    dve.sem_inc(r_zero)
                    dve.sem_inc(r_go)

                    def body(i):
                        mine.turn(i, per)
                        n = i + T * r
                        one = bass.ds(i, 1)
                        key = resc[:, one]
                        wait(dve, r_sc, n * 16)
                        tick(i)
                        link(V.tensor_scalar(rc[0], key, 0.0, None, ALU.is_ge))
                        link(V.tensor_scalar(rc[1], gdst[:, one], trash, None, ALU.subtract))
                        link(V.tensor_tensor(rc[2], rc[0], rc[1], ALU.mult))
                        link(V.tensor_scalar(idx[:, 1, 0:1], rc[2], trash, None, ALU.add))
                        dve.sem_inc(r_ix)
                        link(V.tensor_scalar(rdk, ident[:, :], key, None, ALU.mult))
                        if r == 0:
                            link(V.tensor_scalar(rdl, ident[:, :], lcol[:, one], None, ALU.mult))
                        dve.sem_inc(r_q)
                        dve.wait_ge(r_bk, n + 1)
                        link(V.tensor_scalar(req, psum[:, 0, 0:P], key, None, ALU.is_equal))
                        link(V.tensor_tensor_reduce(out=rjunk, in0=req, in1=tril[:, :], scale=1.0, scalar=0.0,
                                                    op0=ALU.mult, op1=ALU.add, accum_out=rc[3]))
                        link(V.tensor_scalar(rc[4], rc[3], 0.0, None, ALU.is_equal))
                        link(V.tensor_tensor(rc[4], rc[4], rc[2], ALU.mult))
                        link(V.tensor_scalar(idxs[:, 0, 0:1], rc[4], trash, None, ALU.add))
                        dve.wait_ge(r_x, n * 16 + 16)
                        if r == 0:
                            link(V.tensor_scalar(rt1, psum[:, 0, 0:P], key, -BIG, ALU.not_equal, ALU.mult))
                            tick(i)
                            link(V.tensor_tensor_reduce(out=rjunk, in0=rt1, in1=psum[:, 0, P:2 * P], scale=1.0,
                                                        scalar=-BIG * 8, op0=ALU.add, op1=ALU.max, accum_out=rc[5]))
                            link(V.tensor_tensor(rc[6], lcol[:, one], rc[5], ALU.subtract))
                            dve.sem_inc(r_lm)
                            dve.wait_ge(r_ex, n + 1)
                            link(V.tensor_scalar(rw[:, 0:H], gat[:, 0, 0:H], rw[:, H:H + 1], None, ALU.mult))
                        else:
                            if is_reg(i):
                                tick(i)
                            link(V.tensor_tensor(rw[:, 0:H], gatb[:, 0, 0, :], gatb[:, 0, 1, :], ALU.add))
                            link(V.tensor_tensor(rw[:, 0:H], rw[:, 0:H], gatb[:, 0, 2, :], ALU.add))
                        dve.sem_inc(r_w)
                        dve.wait_ge(r_st, n * 16 + 16)
                        if r == 0:
                            link(V.tensor_tensor(rc[7], rst[:, 50:51], rc[5], ALU.max))
                            link(V.tensor_tensor(rd2[:, 0:1], rst[:, 50:51], rc[7], ALU.subtract))
                            link(V.tensor_tensor(rd2[:, 1:2], rc[5], rc[7], ALU.subtract))
                            dve.sem_inc(r_df)
                            dve.wait_ge(r_mm, n + 1)
                            link(V.tensor_tensor(rnew, rst, rst, ALU.max))
                            dve.wait_ge(r_dx, n + 1)
                            link(V.tensor_scalar(rs_[:, 0:C0], psum[:, 1, 0:C0], rd2[:, 1:2], None, ALU.mult))
                            link(V.tensor_scalar(rnew[:, 0:C0], rst[:, 0:C0], rd2[:, 0:1], None, ALU.mult))
                            link(V.tensor_tensor(rnew[:, 0:C0], rnew[:, 0:C0], rs_[:, 0:C0], ALU.add))
                            link(V.tensor_tensor(rnew[:, 50:51], rc[7], rc[7], ALU.max))
                        else:
                            dve.wait_ge(r_mm, n + 1)
                            link(V.tensor_tensor(rnew, rst, rst, ALU.max))
                            link(V.tensor_tensor(rnew[:, 0:C0], rst[:, 0:C0], psum[:, 1, 0:C0], ALU.add))
                        dve.sem_inc(r_new)
                        assert mine.k == per, (mine.k, per, r)
                    turns(dve, T, body)
                    mine.close(T)
                    ch = rchunk.rearrange("p (j c) -> p j c", c=CR)

                    def merge(c):
                        mine.turn(c, perm)
                        js = bass.ds(c * CH, CH)
                        dve.wait_ge(r_ld, (c + 1) * 16 + 16 * NC * r)
                        if r:
                            link(V.tensor_tensor(acc0[:, js, :], acc0[:, js, :], ch[:, :, 0:C0], ALU.add))
                        else:
                            mx = rzero[:, 0:CH]
                            link(V.tensor_tensor(mx, smax[:, js], ch[:, :, 50], ALU.max))
                            link(V.tensor_tensor(rdf[:, 0:CH], smax[:, js], mx, ALU.subtract))
                            link(V.tensor_tensor(rdf[:, CH:2 * CH], ch[:, :, 50], mx, ALU.subtract))
                            dve.sem_inc(r_mf)
                            dve.wait_ge(r_mx, c + 1)
                            link(V.tensor_tensor(ch[:, :, 0:C0], ch[:, :, 0:C0],
                                                 rdf[:, CH:2 * CH].unsqueeze(2).to_broadcast([P, CH, C0]), ALU.mult))
                            a = acc0[:, js, :]
                            link(V.tensor_tensor(a, a, rdf[:, 0:CH].unsqueeze(2).to_broadcast([P, CH, C0]), ALU.mult))
                            link(V.tensor_tensor(a, a, ch[:, :, 0:C0], ALU.add))
                            link(V.tensor_tensor(smax[:, js], mx, mx, ALU.max))
                            link(V.tensor_tensor(rd2[:, 0:1], rd2[:, 0:1], rd2[:, 0:1], ALU.max))
                        dve.sem_inc(r_use)
                        assert mine.k == perm, (mine.k, perm)
                    turns(dve, NC, merge)

            def bases(it, g):
                _, js = nc.values_load_multi_w_load_instructions(
                    base[0:1, bass.ds(it * U + g * Q, Q)], engines=[mybir.EngineType.DVE], min_val=0, max_val=T - 1)
                return js

            def need(v):
                dve.wait_ge(s_dv, v)

            def onehot0(it, g, k, W):
                i = it * U + g * Q + k
                V.tensor_scalar(oneh[:, g * Q + k, 0:W * P], iota[:, 0:W * P], relc[:, bass.ds(i, 1)], None,
                                ALU.is_equal).then_inc(s_oh, 1)

            def maximum0(it, g, k):
                i = it * U + g * Q + k
                dve.wait_ge(s_key, i + 1)
                tick(it)
                return own.add(V.tensor_tensor_reduce(
                    out=junk[:, k, :], in0=lrow[g][:, k * P:(k + 1) * P], in1=keyd[g][:, k, :], scale=1.0,
                    scalar=-BIG, op0=ALU.subtract, op1=ALU.max, accum_out=mloc[:, g, k:k + 1]))

            def edges0(it, g, v):
                st = wst[:, g * Q:(g + 1) * Q, :]
                need(v)
                dve.sem_inc(s_rdone)
                v = own.add(V.tensor_tensor(lm[:, g, :], lcol[:, bass.ds(it * U + g * Q, Q)], mloc[:, g, :], ALU.subtract))
                yield
                need(v)
                v = own.add(V.tensor_scalar(st[:, :, 3], lm[:, g, :], 0.0, None, ALU.is_equal))
                yield
                need(v)
                v = own.add(V.tensor_tensor(mf, mloc[:, g, :], st[:, :, 3], ALU.mult))
                yield
                need(v)
                v = own.add(V.tensor_scalar(st[:, :, 0], mf, 1.0, None, ALU.mult))
                yield
                need(v)
                v = own.add(V.tensor_tensor(mr, mf, st[:, :, 0], ALU.subtract))
                yield
                need(v)
                v = own.add(V.tensor_scalar(st[:, :, 1], mr, 1.0, None, ALU.mult))
                yield
                need(v)
                v = own.add(V.tensor_tensor(st[:, :, 2], mr, st[:, :, 1], ALU.subtract))
                yield
                need(v)
                dve.sem_inc(s_edge)

            def step0(it, g, W, nxt, prev):
                n = it * 2 + g
                last = own.value()
                if nxt:
                    wait(dve, s_mm, nxt[0] * 2 + nxt[1] - 1)
                    tick(it)
                if prev:
                    pit, pg, pW = prev
                    js = bases(pit, pg)
                    dve.wait_ge(s_mm, pit * 2 + pg + 1)
                    tick(it)
                    st = psum[:, 4 + pg, 0:Q * pW * NS].rearrange("p (k c) -> p k c", c=NS)
                    cd, ci, cp = cand[:, 0:Q * pW], cinv[:, 0:Q * pW], cpen[:, 0:Q * pW]
                    a = own.add(V.tensor_scalar(ci, st[:, :, 3], 1.0, None, ALU.max))
                    b = own.add(V.tensor_scalar(cd, st[:, :, 0], 1.0, None, ALU.mult))
                    c = own.add(V.tensor_scalar(cp, st[:, :, 3], 1.0, -1.0, ALU.min, ALU.add))
                    if nxt:
                        onehot0(*nxt[:2], 0, nxt[2])
                    need(c)
                    b = own.add(V.tensor_tensor(cd, cd, st[:, :, 1], ALU.add))
                    a = own.add(V.reciprocal(ci, ci))
                    if nxt:
                        onehot0(*nxt[:2], 1, nxt[2])
                    need(a)
                    b = own.add(V.tensor_tensor(cd, cd, st[:, :, 2], ALU.add))
                    if nxt:
                        onehot0(*nxt[:2], 2, nxt[2])
                    need(b)
                    b = own.add(V.tensor_tensor(cd, cd, ci, ALU.mult))
                    if nxt:
                        onehot0(*nxt[:2], 3, nxt[2])
                    need(b)
                    last = own.add(V.scalar_tensor_tensor(cd, cp, BIG, cd, ALU.mult, ALU.add))
                elif nxt:
                    for k in range(Q):
                        onehot0(*nxt[:2], k, nxt[2])
                v = 0
                for k in range(Q):
                    if nxt:
                        v = maximum0(*nxt[:2], k)
                    if prev:
                        need(last)
                        m = smax[:, bass.ds(js[k], pW)]
                        c_ = cand[:, k * pW:(k + 1) * pW]
                        own.add(V.tensor_tensor(dif[:, pg, 0, k * pW:(k + 1) * pW], m, c_, ALU.subtract))
                        last = own.add(V.tensor_tensor(m, m, c_, ALU.max))
                if prev:
                    d = dif[:, pg, :, 0:Q * pW]
                    need(last)
                    need(own.add(V.tensor_scalar(d[:, 1], d[:, 0], -1.0, 0.0, ALU.mult, ALU.min)))
                    need(own.add(V.tensor_scalar(d[:, 0], d[:, 0], 0.0, None, ALU.min)))
                    dve.sem_inc(s_df)
                edge = edges0(*nxt[:2], v) if nxt else iter(())
                hi = wpar[:, g * Q:(g + 1) * Q, :, :]
                wr = wrow[:, g * Q:(g + 1) * Q, :]
                next(edge, None)
                dve.wait_ge(s_hi, n * 1 + 1)
                a = own.add(V.tensor_tensor(rest, wr, hi[:, :, 0, :], ALU.subtract))
                if prev:
                    dve.wait_ge(s_dx, pit * 2 + pg + 1)
                pr = []
                for h in range(2):
                    if prev:
                        pr.append(prod[h][:, 0:2 * pW * C0].rearrange("p (w c) -> p w c", c=C0))
                        ps = psum[:, 2 * pg + h, 0:2 * pW * C0].rearrange("p (w c) -> p w c", c=C0)
                        d1 = dif[:, pg, 1, h * 2 * pW:(h + 1) * 2 * pW].unsqueeze(2).to_broadcast([P, 2 * pW, C0])
                        last = own.add(V.tensor_tensor(pr[h], ps, d1, ALU.mult))
                    need(a)
                    if h == 0:
                        a = own.add(V.tensor_scalar(hi[:, :, 1, :], rest, 1.0, None, ALU.mult))
                    else:
                        V.tensor_tensor(hi[:, :, 2, :], rest, hi[:, :, 1, :], ALU.subtract).then_inc(s_par, 1)
                for k in range(Q if prev else 0):
                    ac = acc0[:, bass.ds(js[k], pW), :]
                    d0 = dif[:, pg, 0, k * pW:(k + 1) * pW].unsqueeze(2).to_broadcast([P, pW, C0])
                    need(last)
                    last = own.add(V.tensor_tensor(ac, ac, d0, ALU.mult))
                    next(edge, None)
                    need(last)
                    last = own.add(V.tensor_tensor(ac, ac, pr[k // 2][:, (k % 2) * pW:(k % 2 + 1) * pW, :], ALU.add))
                    next(edge, None)
                for _ in edge:
                    pass
                if prev:
                    need(last)
                    dve.sem_inc(s_cmb)

            NXT0, PRV0, OWN0 = Q + 7, 8 + 2 * Q + 2 + 2 + 2 * Q, 2
            PER0 = 2 * (NXT0 + PRV0 + OWN0)

            def body0(it, w, after):
                first = not is_reg(it) and it == 0
                own.turn(it, PER0)
                if first:
                    own.k = PRV0
                    before = None
                else:
                    bw = w if is_reg(it) else next((SEGS[n - 1][2] for n, (a, _, _) in enumerate(SEGS) if n and a == it), w)
                    before = (it - 1, 1, bw)
                step0(it, 0, w, (it, 1, w), before)
                step0(it, 1, w, (it + 1, 0, after) if after else None, (it, 0, w))
                assert own.k == PER0 - (NXT0 if not after else 0), (own.k, PER0)
            for k in range(Q):
                onehot0(0, 0, k, SEGS[0][2])
            for k in range(Q):
                v = maximum0(0, 0, k)
            for _ in edges0(0, 0, v):
                pass
            own.base, own.k = own.base + own.k - PRV0, 0
            segments(dve, body0)
            own.base, own.per, own.it, own.k = own.base + PER0 * IT - NXT0, 0, 0, 0
            pit, pg, pW = IT - 1, 1, SEGS[-1][2]
            js = bases(pit, pg)
            dve.wait_ge(s_mm, pit * 2 + pg + 1)
            st = psum[:, 4 + pg, 0:Q * pW * NS].rearrange("p (k c) -> p k c", c=NS)
            cd, ci, cp = cand[:, 0:Q * pW], cinv[:, 0:Q * pW], cpen[:, 0:Q * pW]
            link(V.tensor_scalar(ci, st[:, :, 3], 1.0, None, ALU.max))
            link(V.reciprocal(ci, ci))
            link(V.tensor_scalar(cp, st[:, :, 3], 1.0, -1.0, ALU.min, ALU.add))
            link(V.tensor_scalar(cd, st[:, :, 0], 1.0, None, ALU.mult))
            link(V.tensor_tensor(cd, cd, st[:, :, 1], ALU.add))
            link(V.tensor_tensor(cd, cd, st[:, :, 2], ALU.add))
            link(V.tensor_tensor(cd, cd, ci, ALU.mult))
            link(V.scalar_tensor_tensor(cd, cp, BIG, cd, ALU.mult, ALU.add))
            for k in range(Q):
                m = smax[:, bass.ds(js[k], pW)]
                c_ = cand[:, k * pW:(k + 1) * pW]
                note(V.tensor_tensor(dif[:, pg, 0, k * pW:(k + 1) * pW], m, c_, ALU.subtract))
                link(V.tensor_tensor(m, m, c_, ALU.max))
            d = dif[:, pg, :, 0:Q * pW]
            link(V.tensor_scalar(d[:, 1], d[:, 0], -1.0, 0.0, ALU.mult, ALU.min))
            link(V.tensor_scalar(d[:, 0], d[:, 0], 0.0, None, ALU.min))
            dve.sem_inc(s_df)
            dve.wait_ge(s_dx, 2 * IT)
            pr = prod[0][:, 0:2 * pW * C0].rearrange("p (w c) -> p w c", c=C0)
            for h in range(2):
                ps = psum[:, 2 * pg + h, 0:2 * pW * C0].rearrange("p (w c) -> p w c", c=C0)
                link(V.tensor_tensor(pr, ps, d[:, 1, h * 2 * pW:(h + 1) * 2 * pW].unsqueeze(2).to_broadcast([P, 2 * pW, C0]), ALU.mult))
                for k in (2 * h, 2 * h + 1):
                    ac = acc0[:, bass.ds(js[k], pW), :]
                    link(V.tensor_tensor(ac, ac, d[:, 0, k * pW:(k + 1) * pW].unsqueeze(2).to_broadcast([P, pW, C0]), ALU.mult))
                    link(V.tensor_tensor(ac, ac, pr[:, (k % 2) * pW:(k % 2 + 1) * pW, :], ALU.add))
            residual(0)

            def v3(b, n=CH):
                return b[:, 0:n * H].rearrange("p (j c) -> p j c", c=H)

            def bc(v, n=CH):
                return v[:, 0:n].unsqueeze(2).to_broadcast([P, n, H])

            def vec(v, n=CH):
                return v.unsqueeze(1).to_broadcast([P, n, H])

            ans = Tally(s_ans)
            ans.base = 1

            def ask(ins):
                ins.then_inc(s_ask, 1)
                ans.k += 1
                dve.wait_ge(s_ans, ans.value())

            def norm(y, to, n=CH):
                link(V.tensor_reduce(small[0][:, 0:n], v3(y, n), AX.X, ALU.add))
                link(V.tensor_scalar(small[0][:, 0:n], small[0][:, 0:n], 1.0 / H, None, ALU.mult))
                link(V.tensor_tensor(v3(y, n), v3(y, n), bc(small[0], n), ALU.subtract))
                link(V.tensor_tensor(v3(sbuf_, n), v3(y, n), v3(y, n), ALU.mult))
                ask(V.tensor_reduce(small[1][:, 0:n], v3(sbuf_, n), AX.X, ALU.add))
                link(V.reciprocal(small[3][:, 0:n], small[2][:, 0:n]))
                return V.tensor_tensor(to, v3(y, n), bc(small[3], n), ALU.mult)

            def split(y, to, n=CH):
                link(V.tensor_copy(to[:, 0:n, 0, :], v3(y, n)))
                link(V.tensor_tensor(v3(y, n), v3(y, n), to[:, 0:n, 0, :], ALU.subtract))
                link(V.tensor_copy(to[:, 0:n, 1, :], v3(y, n)))
                link(V.tensor_tensor(to[:, 0:n, 2, :], v3(y, n), to[:, 0:n, 1, :], ALU.subtract))

            def nodes0(c):
                own.turn(c, 12)
                ans.turn(c, 2)
                js = bass.ds(c * CH, CH)
                link(V.tensor_scalar(small[0], acc0[:, js, H], 1e-30, None, ALU.max))
                link(V.reciprocal(small[0], small[0]))
                link(V.tensor_tensor(v3(ybuf), acc0[:, js, 0:H], bc(small[0]), ALU.mult))
                ask(V.tensor_scalar(tbuf, ybuf, 0.0, None, ALU.min))
                link(V.tensor_scalar(ybuf, ybuf, 0.0, None, ALU.max))
                link(V.tensor_tensor(v3(ybuf), v3(ybuf), X[:, js, :], ALU.add))
                link(V.scalar_tensor_tensor(ybuf, ubuf, -1.0, ybuf, ALU.add, ALU.add))
                link(norm(ybuf, X[:, js, :]))
                dve.sem_inc(s_n0)
                assert own.k == 12, own.k
            for g in range(2):
                dve.wait_ge(s_vs[g], 16 * IT)
            dve.wait_ge(s_zero, 16 * TABLES * (IT + 1))
            turns(dve, NC, nodes0)
            own.close(NC)
            ans.close(NC)

            link(V.tensor_scalar(dtra, gsrc[:, :], trash, None, ALU.subtract))
            note(V.scalar_tensor_tensor(dtra, scol, 0.0, dtra, ALU.is_ge, ALU.mult))
            note(V.memset(hid[0], 1.0))
            note(V.memset(hid[1], 1.0))
            for g in range(2):
                note(V.memset(msg[g][:, :, H + 1], 1.0))
            sync()
            dve.sem_inc(s_acz)

            def group1(it, g):
                n = it * 2 + g
                sl = [slice(k * P, (k + 1) * P) for k in range(Q)]
                dve.wait_ge(s_al[g], it * 48 + 48 if is_reg(it) or it < IT - 1 or g == 0 else it * 48 + 64)
                wait(dve, s_os, n - 1)
                for k in range(Q):
                    i = it * U + g * Q + k
                    note(V.tensor_scalar(eqm[g][:, k, :], drow[g][:, sl[k]], scol[:, bass.ds(i, 1)], None, ALU.is_equal))
                sync()
                dve.sem_inc(s_eq)
                for k in range(Q):
                    link(V.tensor_tensor_reduce(out=junk1, in0=eqm[g][:, k, :], in1=tril[:, :], scale=1.0, scalar=0.0,
                                                op0=ALU.mult, op1=ALU.add, accum_out=rank[:, g, k:k + 1]))
                link(V.scalar_tensor_tensor(idf, rank[:, g, :], 0.0, dtra[:, bass.ds(it * U + g * Q, Q)], ALU.is_equal, ALU.mult))
                if is_reg(it) or it > 0:
                    for k in range(Q):
                        dve.wait_ge(s_sc[g * Q + k], it * 16)
                V.tensor_scalar(idxs[:, g, :], idf, trash, None, ALU.add).then_inc(s_sx, 1)
                gg = gat[:, g * Q:(g + 1) * Q, :]
                for k in range(Q):
                    dve.wait_ge(s_ga[g * Q + k], it * 16 + 16 + 16 * IT)
                if is_reg(it):
                    dve.sem_inc(s_tick)
                note(V.tensor_tensor(qmu, ecol[:, bass.ds(it * U + g * Q, Q)], gg[:, :, H + GE], ALU.mult))
                link(V.tensor_tensor(uv, gg[:, :, H:H + GE], vse[g], ALU.mult))
                link(V.tensor_reduce(adp, uv, AX.X, ALU.add))
                dve.sem_inc(s_rs)
                dve.wait_ge(s_gt, n * 1 + 1)
                link(V.tensor_tensor(m1, psum[:, 4 + g, 0:Q * H].rearrange("p (k c) -> p k c", k=Q),
                                     adp.unsqueeze(2).to_broadcast([P, Q, H]), ALU.add))
                link(V.tensor_tensor(m2, m1, gg[:, :, 0:H], ALU.mult))
                note(V.tensor_copy(msg[g][:, :, H], gg[:, :, H + GE]))
                link(V.tensor_tensor(msg[g][:, :, 0:H], m2, qmu.unsqueeze(2).to_broadcast([P, Q, H]), ALU.mult))
                dve.sem_inc(s_ms)

            PER1 = 2 * (Q + Q + 1 + 3 + 4)

            def body1(it):
                own.turn(it, PER1)
                group1(it, 0)
                group1(it, 1)
                assert own.k == PER1, own.k
            turns(dve, IT, body1)
            own.close(IT)

            def nodes1(q):
                own.turn(q, 2 * 29)
                ans.turn(q, 6)
                for s in range(2):
                    c = q * 2 + s
                    js = bass.ds(c * CH, CH)
                    t = aload[s]
                    tv = t[0].rearrange("p (j c) -> p j c", c=C1)
                    dve.wait_ge(s_ld[s], q * 64 + 64)
                    note(V.tensor_tensor(t[0], t[0], t[1], ALU.add))
                    link(V.tensor_tensor(t[2], t[2], t[3], ALU.add))
                    link(V.tensor_tensor(t[0], t[0], t[2], ALU.add))
                    note(V.tensor_copy(small[6], tv[:, :, H + 1]))
                    link(V.tensor_scalar(small[0], tv[:, :, H], 1e-8, None, ALU.max))
                    link(V.reciprocal(small[0], small[0]))
                    link(V.tensor_tensor(v3(ybuf), tv[:, :, 0:H], bc(small[0]), ALU.mult))
                    dve.sem_inc(s_sum)
                    link(V.tensor_tensor(v3(ybuf), v3(ybuf), X[:, js, :], ALU.add))
                    link(norm(ybuf, v3(ybuf)))
                    link(V.tensor_tensor(v3(ybuf), v3(ybuf), vec(vecs[0]), ALU.mult))
                    link(V.tensor_tensor(v3(ybuf), v3(ybuf), vec(vecs[1]), ALU.add))
                    link(V.tensor_tensor(v3(ybuf), v3(ybuf), X[:, js, :], ALU.add))
                    link(norm(ybuf, X[:, js, :]))
                    ask(V.tensor_scalar(small[4], small[6], 1.0, None, ALU.max))
                    link(V.reciprocal(small[5], small[5]))
                    if is_reg(q) or q > 0:
                        dve.wait_ge(s_t2[s], q * 16)
                    link(V.tensor_tensor(v3(ybuf), X[:, js, :], bc(small[5]), ALU.mult))
                    split(ybuf, stg[s])
                    dve.sem_inc(s_n1)
                assert own.k == 2 * 29, own.k
            turns(dve, NC // 2, nodes1)
            own.close(NC // 2)
            ans.close(NC // 2)
            link(V.memset(ACC[:, :], 0.0))
            for s in range(2):
                dve.wait_ge(s_t2[s], 16 * (NC // 2))

            def edges(layer):
                def produce(it, g, W):
                    n = it * 2 + g
                    if is_reg(it) or it > 0:
                        dve.wait_ge(s_mm2[layer], n * 1 - 1)
                    for k in range(Q):
                        i = it * U + g * Q + k
                        V.tensor_scalar(oneh[:, g * Q + k, 0:W * P], iota[:, 0:W * P], relc[:, bass.ds(i, 1)], None,
                                        ALU.is_equal).then_inc(s_oh2[layer], 1)

                def combine(it, g, W):
                    n = it * 2 + g
                    js = bases(it, g)
                    dve.wait_ge(s_mm2[layer], n * 1 + 1)
                    for k in range(Q):
                        C = C0 if layer == 0 else H
                        a = acc0[:, bass.ds(js[k], W), 0:C]
                        at = (k % 2) * W * C0
                        ps = psum[:, 2 * g + k // 2, at:at + W * C0].rearrange("p (w c) -> p w c", c=C0)[:, :, 0:C]
                        link(V.tensor_tensor(a, a, ps, ALU.add))
                    dve.sem_inc(s_cm2[layer])

                def body(it, w, after):
                    own.turn(it, 2 * Q)
                    produce(it, 1, w)
                    combine(it, 0, w)
                    if after is not None:
                        produce(it + 1, 0, after)
                    combine(it, 1, w)
                produce(0, 0, SEGS[0][2])
                segments(dve, body)
                own.close(IT)
                residual(1 + layer)

            edges(0)

            note(V.memset(hT, 1.0))
            note(V.memset(hT2, 1.0))
            sync()
            ask(V.tensor_scalar(tbuf[:, 0:T], acc0[:, 0:T, H], 1.0, None, ALU.max))
            link(V.reciprocal(cj, cj))
            ask(V.tensor_scalar(tbuf[:, 0:T], acc0[:, 0:T, H], 1.0, None, ALU.add))
            link(V.reciprocal(smax[:, 0:T], smax[:, 0:T]))
            ans.base, ans.k = ans.base + ans.k, 0
            PER2 = 19

            def nodes2(it):
                own.turn(it, PER2)
                ans.turn(it, 1)
                js = bass.ds(it * U, U)
                y, z = v3(ybuf, U), v3(tbuf, U)
                link(V.tensor_scalar(small[7][:, 0:U], acc0[:, js, H], 0.0, None, ALU.is_equal))
                note(V.tensor_tensor(z, X[:, js, :], small[7][:, 0:U].unsqueeze(2).to_broadcast([P, U, H]), ALU.mult))
                link(V.tensor_tensor(y, acc[:, js, :], cj[:, js].unsqueeze(2).to_broadcast([P, U, H]), ALU.mult))
                link(V.tensor_tensor(y, y, z, ALU.add))
                dve.sem_inc(s_na)
                dve.wait_ge(s_nmm, it * 2 + 1)
                ps = psum[:, 2, 0:U * H].rearrange("p (k c) -> p k c", k=U)
                link(V.tensor_scalar(y, ps, 0.0, None, ALU.max))
                link(V.tensor_tensor(y, y, X[:, js, :], ALU.add))
                link(norm(ybuf, y, U))
                dve.sem_inc(s_na)
                note(V.tensor_copy(X[:, js, :], y))
                dve.wait_ge(s_nmm, it * 2 + 2)
                ps = psum[:, 3, 0:U * H].rearrange("p (k c) -> p k c", k=U)
                link(V.tensor_tensor(z, ps, smax[:, js].unsqueeze(2).to_broadcast([P, U, H]), ALU.mult))
                tick(it)
                note(V.tensor_copy(acc[:, js, :], z))
                wait(dve, s_t3, it * 16)
                tick(it)
                split(tbuf, stg[0], U)
                dve.sem_inc(s_n2)
                assert own.k == PER2, own.k
            turns(dve, IT, nodes2)
            own.close(IT)
            ans.close(IT)
            dve.wait_ge(s_t3, 16 * IT)

            edges(1)

            av = acc[:, 0:T, :]
            link(V.tensor_tensor(av, av, bc(smax, T), ALU.mult))
            link(V.tensor_tensor(av, av, vec(vecs[2], T), ALU.add))

            def masked():
                note(V.tensor_scalar(acc[:, FULL, :], acc[:, FULL, :], valid, None, ALU.mult))
                link(V.memset(acc[:, FULL + 1:T, :], 0.0))
            masked()
            V.tensor_reduce(sbuf_[:, 0:H], av.rearrange("p j c -> p c j"), AX.X, ALU.add).then_inc(s_bn, 1)
            dve.wait_ge(s_bm, 1)
            link(V.tensor_scalar(ubuf[:, 0:H], psum[:, 0, 0:H], 1.0 / N, None, ALU.mult))
            link(V.tensor_tensor(av, av, vec(ubuf[:, 0:H], T), ALU.subtract))
            masked()
            link(V.memset(tbuf[:, 0:H], 0.0))
            ask(V.tensor_copy(small[1][:, 0:1], tbuf[:, 0:1]))
            ans.base, ans.k = ans.base + ans.k, 0

            def squares(c):
                own.turn(c, 3)
                a = acc[:, bass.ds(c * CH, CH), :]
                link(V.tensor_tensor(v3(ybuf), a, a, ALU.mult))
                link(V.tensor_reduce(sbuf_[:, 0:H], v3(ybuf).rearrange("p j c -> p c j"), AX.X, ALU.add))
                link(V.tensor_tensor(tbuf[:, 0:H], tbuf[:, 0:H], sbuf_[:, 0:H], ALU.add))
            turns(dve, NC, squares)
            own.close(NC)
            V.tensor_copy(sbuf_[:, 0:H], tbuf[:, 0:H]).then_inc(s_bn, 1)
            dve.wait_ge(s_bm, 2)
            ask(V.tensor_copy(tbuf[:, 0:H], psum[:, 1, 0:H]))
            ans.base, ans.k = ans.base + ans.k, 0
            link(V.reciprocal(ubuf[:, 0:H], ybuf[:, 0:H]))
            link(V.tensor_tensor(vecs[3], vecs[3], ubuf[:, 0:H], ALU.mult))

            def nodes3(c):
                own.turn(c, 10)
                ans.turn(c, 1)
                js = bass.ds(c * CH, CH)
                link(V.tensor_tensor(v3(ybuf), acc[:, js, :], vec(vecs[3]), ALU.mult))
                link(V.tensor_tensor(v3(ybuf), v3(ybuf), vec(vecs[4]), ALU.add))
                link(V.tensor_scalar(ybuf, ybuf, 0.0, None, ALU.max))
                link(V.tensor_tensor(v3(ybuf), v3(ybuf), X[:, js, :], ALU.add))
                link(norm(ybuf, X[:, js, :]))
                dve.sem_inc(s_n3)
                assert own.k == 10, own.k
            turns(dve, NC, nodes3)
            own.close(NC)


_INS = ['x', 'src', 'dst', 'edge_attr_40', 'edge_weight', 'edge_weight1', 'node_type_119', 'node_vec',
        'L1_gnn_W1', 'L1_gnn_b1', 'L1_gnn_W2', 'L1_gnn_b2', 'L1_gnn_emb', 'L1_gnn_adaptW', 'L1_gnn_gamma',
        'L1_gnn_beta', 'L2_gnn_W', 'L2_gnn_b', 'L3_gnn_W', 'L3_gnn_b', 'L3_gnn_gamma', 'L3_gnn_beta']


def kernel(**inputs):
    import numpy as _np
    import concourse.bacc as _bacc
    from concourse import mybir as _mybir
    from concourse.bass_utils import run_bass_kernel_spmd as _run

    nc = _bacc.Bacc("TRN2", target_bir_lowering=False, num_devices=1)
    arrays, args = {}, []
    for name in _INS:
        a = _np.ascontiguousarray(inputs[name])
        arrays[f"in_{name}_dram"] = a
        args.append(nc.dram_tensor(f"in_{name}_dram", a.shape, _mybir.dt.from_np(a.dtype), kind="ExternalInput").ap())
    args.append(nc.dram_tensor("out_0_dram", (N, H), F32, kind="ExternalOutput").ap())
    build(nc, *args)
    r = _run(nc, [arrays], core_ids=[0])
    return r.results[0]["out_0_dram"]
```

```python
import concourse.bass as bass
from concourse import mybir
from contextlib import ExitStack

F32 = mybir.dt.float32
I32 = mybir.dt.int32
BF16 = mybir.dt.bfloat16
FP16 = mybir.dt.float16
ALU = mybir.AluOpType
ACT = mybir.ActivationFunctionType
AX = mybir.AxisListType

P = 128
N = 50000
H = 48
GE = 32
R = 40
NEL = 119
T = 392
FULL = N // P
REST = N - FULL * P
U = 8
IT = T // U
Q = 4
W = 4
SEGS = [(0, 17, 2), (17, 34, 3), (34, IT, 4)]
TA = T + W
C0 = H + 1
C1 = H + 2
K0 = H + GE
K1 = H + GE + 1
TABLES = 4
CH = 14
NC = T // CH
BIG = 2.0 ** 120
KEY = 2.0 ** 100
PARTS = 3
EPS = 1e-5
AW = 6568
PI = 3.141592653589793


class Tally:

    def __init__(self, sem):
        self.sem, self.base, self.per, self.it, self.k = sem, 0, 0, 0, 0

    def value(self):
        return self.base + self.k + (self.it * self.per if self.per else 0)

    def add(self, ins, n=1):
        ins.then_inc(self.sem, n)
        self.k += n
        return self.value()

    def turn(self, it, per):
        if not self.per:
            self.base += self.k
        self.it, self.per, self.k = it, per, 0

    def close(self, turns):
        self.base += turns * self.per
        self.per, self.it, self.k = 0, 0, 0


class Own:

    def __init__(self, eng, sem):
        self.eng, self.sem, self.k = eng, sem, 0

    def value(self):
        return self.k

    def add(self, ins):
        ins.then_inc(self.sem, 1)
        self.k += 1
        return self.k

    def renew(self):
        if self.k:
            self.eng.wait_ge(self.sem, self.k)
            self.eng.sem_clear(self.sem)
            self.k = 0


def is_reg(v):
    return not isinstance(v, int)


def wait(eng, sem, v):
    if is_reg(v) or v > 0:
        eng.wait_ge(sem, v)


def turns(eng, n, body):
    body(0)
    with eng.Fori(1, n - 1) as i:
        body(i)
    body(n - 1)


def together(*chains):
    live = list(chains)
    while live:
        live = [c for c in live if next(c, live) is not live]


def segments(eng, body):
    for n, (a, b, w) in enumerate(SEGS):
        body(a, w, w)
        with eng.Fori(a + 1, b - 1) as i:
            body(i, w, w)
        body(b - 1, w, SEGS[n + 1][2] if n + 1 < len(SEGS) else None)


def build(nc, x, src, dst, attr, ew, ew1, ntype, nvec, W1, b1, W2, b2, emb, adaptW, gamma, beta,
          L2W, L2b, L3W, L3b, L3g, L3be, out):
    ctx = ExitStack()
    with ctx:
        def sb(name, shape, dt=F32):
            return ctx.enter_context(nc.sbuf_tensor(name, shape, dt))

        def sem(name):
            return ctx.enter_context(nc.semaphore(name))

        def dram(name, shape, dt=F32):
            return nc.dram_tensor(name, shape, dt, kind="Internal").ap()

        tab0 = dram("tab0", (P * T, K0))
        tab1 = dram("tab1", (P * T, K1))
        tab2 = dram("tab2", (P * T, PARTS * H), BF16)
        tab3 = dram("tab3", (P * T, PARTS * H), BF16)
        aggs = [dram(f"agg{k}", (P * T + P, C1)) for k in range(TABLES)]
        rows_d = [dram(f"rows{a}", (T * P,)) for a in range(3)]
        srcemb = dram("srcemb", (P, T * GE))
        tab0v = tab0.rearrange("(p j) c -> p j c", p=P)
        tab1v = tab1.rearrange("(p j) c -> p j c", p=P)
        tab2v = tab2.rearrange("(p j) c -> p j c", p=P)
        tab3v = tab3.rearrange("(p j) c -> p j c", p=P)
        aggv = [a[0:P * T, :].rearrange("(p j) c -> p (j c)", p=P) for a in aggs]

        X = sb("X", [P, T, H])
        ACC = sb("ACC", [P, TA * C0])
        acc0 = ACC[:, :].rearrange("p (j c) -> p j c", c=C0)
        acc = acc0[:, :, 0:H]
        cols = sb("cols", [P, 5, T])
        dcol, scol, lcol, ecol, mcol = (cols[:, a, :] for a in range(5))
        relc = sb("relc", [P, T])
        gsrc = sb("gsrc", [P, T], I32)
        gdst = sb("gdst", [P, T], I32)
        base = sb("base", [1, T], I32)
        smax = sb("smax", [P, TA])
        ident = sb("ident", [P, P])
        tril = sb("tril", [P, P])
        ones = sb("ones", [P, P])
        iota = sb("iota", [P, W * P], FP16)
        oneb = sb("oneb", [P, 2], BF16)
        pcol = sb("pcol", [P, 8])
        trash, halfpi, epsc, valid = (pcol[:, a:a + 1] for a in (0, 2, 3, 4))
        idx = sb("idx", [P, 2, Q], I32)
        flag = sb("flag", [1, 1], I32)
        flagr = sb("flagr", [P, 1])
        flagf = sb("flagf", [1, P])
        wsm = sb("wsm", [P, 864])
        W1T = wsm[0:R, 0:H]
        W2T = wsm[0:H + 1, 48:96]
        bd = sb("bd", [P, 4 * H])
        L2BD = bd[0:2 * H + 1, 0:2 * H]
        L3BD = bd[0:2 * H, 2 * H:4 * H]
        EU = wsm[0:NEL, 192:256]
        b1c = wsm[0:H, 256:257]
        embT = wsm[0:GE, 257:257 + NEL]
        adT = wsm[0:GE, 376:408]
        w1raw = wsm[0:H, 408:448]
        w2raw = wsm[0:H, 448:496]
        l2raw = wsm[0:H, 496:544]
        adraw = wsm[0:GE, 544:576]
        b1raw = wsm[0:1, 576:624]
        vecs = [wsm[:, 624 + 48 * a:672 + 48 * a] for a in range(5)]

        A1 = sb("A1", [P, AW])
        idxs = sb("idxs", [P, 2, Q], I32)

        RI = ACC[:, 0:1024].bitcast(I32).rearrange("p (a b e) -> p a b e", a=2, b=4)
        RF = ACC[:, 1024:3584].rearrange("p (a b e) -> p a b e", a=5, b=4)
        zb = [ACC[0:NEL, 4096 + 1024 * s:5120 + 1024 * s].bitcast(I32) for s in range(2)]
        zoh = [ACC[0:NEL, 6144 + 1024 * s:7168 + 1024 * s] for s in range(2)]
        st0 = [ACC[:, 8192 + 640 * s:8832 + 640 * s].rearrange("p (t c) -> p t c", t=U) for s in range(2)]
        stu = [ACC[:, 9600 + 264 * s:9864 + 264 * s].rearrange("p (t c) -> p t c", t=U) for s in range(2)]

        o = 0

        def cut(n):
            nonlocal o
            o += n
            assert o <= AW, o
            return A1[:, o - n:o]

        gat = cut(U * K1).rearrange("p (k c) -> p k c", k=U)
        gatb = gat.rearrange("p k c -> p (k c)")[:, 0:U * PARTS * H // 2].bitcast(BF16).rearrange(
            "p (k b c) -> p k b c", k=U, b=PARTS)
        oneh = sb("oneh", [P, U, W * P], BF16)
        wrow = cut(U * C0).rearrange("p (k c) -> p k c", k=U)
        wpar = cut(U * PARTS * C0 // 2).bitcast(BF16).rearrange("p (k b c) -> p k b c", k=U, b=PARTS)
        NS = 5
        wst = cut(U * 3).bitcast(BF16).rearrange("p (k c) -> p k c", k=U)
        drow = [cut(Q * P) for _ in range(2)]
        lrow = [cut(Q * P) for _ in range(2)]
        tmpc, tmpd, tmpi = drow[0][:, 0:T], drow[1][:, 0:T], lrow[0][:, 0:T].bitcast(I32)
        tmpr = lrow[1][:, 0:T]
        dtra = lcol
        cj = lcol
        resc = mcol
        keyd = [cut(Q * P).rearrange("p (k c) -> p k c", k=Q) for _ in range(2)]
        mloc = cut(2 * Q).rearrange("p (g k) -> p g k", g=2)
        lm = cut(2 * Q).rearrange("p (g k) -> p g k", g=2)
        mf, mr = cut(Q), cut(Q)
        cand, cinv, cpen = cut(W * Q), cut(W * Q), cut(W * Q)
        dif = cut(2 * 2 * W * Q).rearrange("p (g h k) -> p g h k", g=2, h=2)
        prod = [cut(2 * W * C0) for _ in range(2)]
        junk = cut(Q * P // 2).bitcast(BF16).rearrange("p (k c) -> p k c", k=Q)
        rest = cut(Q * C0).rearrange("p (k c) -> p k c", k=Q)
        junk1 = prod[0][:, 0:P]
        zero = cut(U * C1)
        att = [ACC[:, 160 * s:160 * s + 160].rearrange("p (k c) -> p k c", k=Q) for s in range(2)]
        vse = [ACC[:, 320 + 128 * s:448 + 128 * s].rearrange("p (k c) -> p k c", k=Q) for s in range(2)]
        attT = [ACC[0:R, 600 + 512 * s:1112 + 512 * s] for s in range(2)]
        hid = [ACC[0:H + 1, 1700 + 512 * s:2212 + 512 * s] for s in range(2)]
        msg = [ACC[:, 2800 + 200 * s:3000 + 200 * s].rearrange("p (k c) -> p k c", k=Q) for s in range(2)]
        osum = [ACC[:, 3200 + 200 * s:3400 + 200 * s].rearrange("p (k c) -> p k c", k=Q) for s in range(2)]
        eqm = [ACC[:, 3600 + 512 * s:4112 + 512 * s].rearrange("p (k c) -> p k c", k=Q) for s in range(2)]
        uv = ACC[:, 4700:4828].rearrange("p (k c) -> p k c", k=Q)
        m1 = ACC[:, 4900:5092].rearrange("p (k c) -> p k c", k=Q)
        m2 = ACC[:, 5100:5292].rearrange("p (k c) -> p k c", k=Q)
        adp = ACC[:, 5300:5304]
        qmu = ACC[:, 5304:5308]
        rank = ACC[:, 5308:5316].rearrange("p (g k) -> p g k", g=2)
        idf = ACC[:, 5316:5320]
        aload = [[ACC[:, 5400 + 700 * (4 * s + k):6100 + 700 * (4 * s + k)] for k in range(TABLES)] for s in range(2)]
        NCOL = CH * H
        ybuf, sbuf_, tbuf, ubuf = (A1[:, NCOL * a:NCOL * (a + 1)] for a in range(4))
        stg = [A1[:, 2800 + 1008 * s:3808 + 1008 * s].bitcast(BF16).rearrange("p (j b c) -> p j b c", b=PARTS, c=H)
               for s in range(2)]
        small = [A1[:, 4900 + 16 * a:4900 + 16 * a + CH] for a in range(8)]
        rows_ = [ybuf, tbuf]
        sqrs = [sbuf_, ubuf]
        sums = [small, [A1[:, 5100 + 16 * a:5100 + 16 * a + CH] for a in range(8)]]
        mean0 = [A1[:, NCOL * a:NCOL * (a + 1)] for a in (4, 5)]
        exps0 = [A1[:, NCOL * a:NCOL * (a + 1)] for a in (6, 7)]
        sums0 = [[A1[:, 8 * NCOL + 16 * (8 * s + a):8 * NCOL + 16 * (8 * s + a) + CH] for a in range(8)] for s in range(2)]
        r2buf, n2buf, x2buf, pbuf, zbuf2 = ybuf, tbuf, ubuf, A1[:, 5300:5684], A1[:, 5700:6084]
        mean3 = A1[:, 5300:5300 + H]
        onehf = oneh[:, :, :].rearrange("p k c -> p (k c)").bitcast(F32)
        hT = onehf[0:2 * H + 1, 0:512]
        hT2 = onehf[0:2 * H, 512:1024]

        psum = ctx.enter_context(nc.psum_tensor("psum", [P, 8, 512], F32))

        CR = 52
        states = dram("states", (P * T + P, CR))
        statev = states[0:P * T, :].rearrange("(p j) c -> p (j c)", p=P)
        RA = A1[:, U * K1:U * K1 + 2800]
        req, rt1, rjunk, rdk, rdl = (RA[:, a * P:(a + 1) * P] for a in range(5))
        rw, rst, rnew, rs_ = (RA[:, 640 + CR * a:640 + CR * (a + 1)] for a in range(4))
        rc = [RA[:, 848 + a:849 + a] for a in range(16)]
        rd2 = RA[:, 864:866]
        rdf = RA[:, 868:868 + 2 * CH]
        rchunk = RA[:, 1024:1024 + CH * CR]
        rzero = RA[:, 2048:2048 + CH * CR]

        r_go, r_zero, r_init, r_ld, r_use, r_pl, r_x, r_ix, r_st, r_q, r_bk, r_lm, r_ex, r_w, r_mm, r_df, r_dx, \
            r_new, r_sc, r_dv, r_mf, r_mx = (sem("r_" + n) for n in (
                "go", "zero", "init", "ld", "use", "pl", "x", "ix", "st", "q", "bk", "lm", "ex", "w", "mm", "df",
                "dx", "new", "sc", "dv", "mf", "mx"))
        s_const = sem("s_const")
        s_pad = sem("s_pad")
        s_rows = sem("s_rows")
        s_x = sem("s_x")
        s_w = sem("s_w")
        s_bd = sem("s_bd")
        s_rowf = sem("s_rowf")
        s_rowd = sem("s_rowd")
        s_tp = sem("s_tp")
        s_cp = sem("s_cp")
        s_bb = sem("s_bb")
        s_flag = sem("s_flag")
        s_zl = [sem(f"s_zl{s}") for s in range(2)]
        s_zo, s_zm, s_ze, s_zx = sem("s_zo"), sem("s_zm"), sem("s_ze"), sem("s_zx")
        s_zs = [sem(f"s_zs{s}") for s in range(2)]
        s_prep = sem("s_prep")
        s_dv = sem("s_dv")
        s_pl = sem("s_pl")
        s_tick = sem("s_tick")
        s_ask, s_ans = sem("s_ask"), sem("s_ans")
        s_ga = [sem(f"s_ga{k}") for k in range(U)]
        s_rl = [sem(f"s_rl{g}") for g in range(2)]
        s_vs = [sem(f"s_vs{g}") for g in range(2)]
        s_key, s_edge, s_oh, s_wr, s_sc0, s_hi, s_par, s_mm, s_df, s_dx, s_cmb, s_rdone = (sem(n) for n in (
            "s_key", "s_edge", "s_oh", "s_wr", "s_scl", "s_hi", "s_par", "s_mm", "s_df", "s_dx", "s_cmb", "s_rdone"))
        s_zero = sem("s_zero")
        s_n0 = sem("s_n0")
        s_t1 = sem("s_t1")
        s_al = [sem(f"s_al{g}") for g in range(2)]
        s_at, s_ac, s_hd, s_si, s_gt, s_ms, s_eq, s_os, s_oc, s_sx, s_rs = (sem(n) for n in (
            "s_at", "s_ac", "s_hd", "s_si", "s_gt", "s_ms", "s_eq", "s_os", "s_oc", "s_sx", "s_rs"))
        s_sc = [sem(f"s_sc{k}") for k in range(U)]
        s_ld = [sem(f"s_ld{g}") for g in range(2)]
        s_sum, s_n1 = sem("s_sum"), sem("s_n1")
        s_t2 = [sem(f"s_t2{g}") for g in range(2)]
        s_acz = sem("s_acz")
        s_oh2, s_mm2, s_cm2 = [sem("s_oh2"), sem("s_oh3")], [sem("s_mm2"), sem("s_mm3")], \
            [sem("s_cm2"), sem("s_cm3")]
        s_na, s_ntp, s_ncp, s_nmm = sem("s_na"), sem("s_ntp"), sem("s_ncp"), sem("s_nmm")
        s_n2 = sem("s_n2")
        s_cen = sem("s_cen")
        s_sq = sem("s_sq")
        s_var = sem("s_var")
        s_std = sem("s_std")
        s_y0, s_e0 = sem("s_y0"), sem("s_e0")
        s_agg, s_deg, s_dst = sem("s_agg"), sem("s_deg"), sem("s_dst")
        s_pa, s_pb, s_pc, s_pd = (sem(n) for n in ("s_pa", "s_pb", "s_pc", "s_pd"))
        s_na2, s_ntp2, s_ncp2, s_nmm2, s_nrd, s_nrd2, s_nx = (sem(n) for n in (
            "s_na2", "s_ntp2", "s_ncp2", "s_nmm2", "s_nrd", "s_nrd2", "s_nx"))
        s_t3 = sem("s_t3")
        s_bs, s_bq, s_bm = sem("s_bs"), sem("s_bq"), sem("s_bm")
        s_n3 = sem("s_n3")
        s_out = sem("s_out")

        def in2(j):
            return is_reg(j) or 0 <= j < IT

        def pipeline(eng, body):
            for i in range(-2, 3):
                body(i)
            with eng.Fori(0, (IT - 5) // 2) as q:
                body(q * 2 + 3)
                body(q * 2 + 4)
            for i in range(IT - 2, IT + 2):
                body(i)

        block = ctx.enter_context(nc.Block())

        @block.sync
        def _(sp):
            def residual(r):
                sp.wait_ge(s_flag, 3)
                more = sp.value_load(flag[0:1, 0:1], min_val=0, max_val=T * P)
                with sp.If(more > 0):
                    sp.wait_ge(r_zero, r + 1)
                    with sp.Fori(0, NC) as c:
                        sp.dma_start(statev[:, bass.ds(c * (CH * CR), CH * CR)], rzero).then_inc(r_init, 16)
                    sp.dma_start(states[P * T:P * T + P, :], rzero[:, 0:CR]).then_inc(r_init, 16)
                    sp.wait_ge(r_sc, 16 * T * (r + 1))
                    sp.dma_start(rchunk, statev[:, 0:CH * CR]).then_inc(r_ld, 16)
                    with sp.Fori(1, NC) as c:
                        sp.wait_ge(r_use, c * 1 + NC * r)
                        sp.dma_start(rchunk, statev[:, bass.ds(c * (CH * CR), CH * CR)]).then_inc(r_ld, 16)

            sp.wait_ge(s_pad, 1)
            sp.dma_start(RI[0:6, 0, 3, :], dst[384 * P:FULL * P].rearrange("(p e) -> p e", e=P)).then_inc(s_rows, 16)
            for a, arr in enumerate((dst, src, ew1.rearrange("e a -> (e a)"), ew, nvec)):
                to = RI[:, a] if a < 2 else RF[:, a]
                sp.dma_start(to[:, 0:3, :], arr[0:384 * P].rearrange("(b p e) -> p b e", b=3, e=P)).then_inc(s_rows, 16)
                if a:
                    sp.dma_start(to[0:6, 3, :], arr[384 * P:FULL * P].rearrange("(p e) -> p e", e=P)).then_inc(s_rows, 16)
                sp.dma_start(to[6:7, 3, 0:REST], arr[FULL * P:N].rearrange("(a e) -> a e", a=1)).then_inc(s_rows, 16)
            for to, of in ((w1raw, W1), (w2raw, W2), (l2raw, L2W), (adraw, adaptW),
                           (EU[:, 0:GE], emb), (L3BD[0:H, 0:H], L3W), (L3BD[H:2 * H, H:2 * H], L3W),
                           (W2T[H:H + 1, :], b2.rearrange("(a n) -> a n", a=1)),
                           (L2BD[2 * H:, 0:H], L2b.rearrange("(a n) -> a n", a=1)),
                           (L2BD[2 * H:, H:], L2b.rearrange("(a n) -> a n", a=1)),
                           (b1raw, b1.rearrange("(a n) -> a n", a=1))):
                sp.dma_start(to, of).then_inc(s_w, 16)
            for a, v in enumerate((gamma, beta, L3b, L3g, L3be)):
                sp.dma_start(vecs[a], v.partition_broadcast(P)).then_inc(s_w, 16)
            sp.dma_start(X[:, 0:FULL, :], x[0:FULL * P, :].rearrange("(j p) c -> p j c", p=P)).then_inc(s_x, 16)
            sp.dma_start(X[0:REST, FULL, :], x[FULL * P:N, :]).then_inc(s_x, 16)
            sp.wait_ge(s_cp, 1)
            sp.dma_start(L2BD[H:2 * H, H:], L2BD[0:H, 0:H]).then_inc(s_bd, 16)
            sp.wait_ge(s_rowf, 1)
            for a in range(3):
                v = rows_d[a].rearrange("(t e) -> t e", e=P)
                sp.dma_start(v[0:384, :].rearrange("(b p) e -> p b e", b=3), RF[:, a, 0:3, :]).then_inc(s_rowd, 16)
                sp.dma_start(v[384:T, :], RF[0:U, a, 3, :]).then_inc(s_rowd, 16)

            def load_z(m, s):
                n = min(U * P, N - U * P * (IT - 1)) if (not is_reg(m) and m == IT - 1) else U * P
                wait(sp, s_zo, m - 1)
                sp.dma_start(zb[s][:, 0:n], ntype[bass.ds(m * (U * P), n)].partition_broadcast(NEL)).then_inc(s_zl[s], 16)

            def store_z(m, s):
                sp.wait_ge(s_ze, m * 1 + 1)
                sp.wait_ge(s_zx, m * 1 + 1)
                sp.dma_start(tab0v[:, bass.ds(m * U, U), :], st0[s]).then_inc(s_zs[s], 16)
                sp.dma_start(tab1v[:, bass.ds(m * U, U), H:K1], stu[s]).then_inc(s_zs[s], 16)

            sp.wait_ge(s_pad, 2)
            load_z(0, 0)
            load_z(1, 1)
            with sp.Fori(0, IT // 2 - 1) as q:
                load_z(q * 2 + 2, 0)
                store_z(q * 2, 0)
                load_z(q * 2 + 3, 1)
                store_z(q * 2 + 1, 1)
            load_z(IT - 1, 0)
            store_z(IT - 3, 0)
            store_z(IT - 2, 1)
            store_z(IT - 1, 0)

            def rows0(it):
                for g in range(2):
                    n = it * 2 + g
                    wait(sp, s_rdone, n - 1)
                    wait(sp, s_key, n * Q - Q)
                    for to, a in ((drow[g], 0), (lrow[g], 2)):
                        sp.dma_start(to, rows_d[a][bass.ds(n * (Q * P), Q * P)].partition_broadcast(P)).then_inc(s_rl[g], 16)

            def side0(it):
                for g in range(2):
                    for k in range(Q):
                        sp.wait_ge(s_ga[g * Q + k], it * 16 + 16)
                    sp.dma_start(srcemb[:, bass.ds(it * (U * GE) + g * Q * GE, Q * GE)].rearrange("p (k c) -> p k c", k=Q),
                                 gat[:, g * Q:(g + 1) * Q, H:K0]).then_inc(s_vs[g], 16)
                for k in range(TABLES):
                    sp.dma_start(aggv[k][:, bass.ds(it * (U * C1), U * C1)], zero[:, :]).then_inc(s_zero, 16)

            sp.wait_ge(s_rowd, 96)
            sp.wait_ge(s_acz, 1)
            for k in range(TABLES):
                sp.dma_start(aggs[k][P * T:P * T + P, :], zero[:, 0:C1]).then_inc(s_zero, 16)
            rows0(0)
            with sp.Fori(0, IT - 1) as it:
                rows0(it + 1)
                side0(it)
            side0(IT - 1)

            residual(0)

            def out0(c):
                sp.wait_ge(s_n0, c * 1 + 1)
                sp.dma_start(tab1v[:, bass.ds(c * CH, CH), 0:H], X[:, bass.ds(c * CH, CH), :]).then_inc(s_t1, 16)
            turns(sp, NC, out0)

            def load1(it, last=False):
                for g in range(2):
                    n = it * 2 + g
                    tail = last and g == 1
                    wait(sp, s_at, n - 1)
                    wait(sp, s_rs, n - 1)
                    if tail:
                        r = FULL - (T - Q)
                        sp.dma_start(att[g][:, 0:r, :], attr[(T - Q) * P:FULL * P, :].rearrange("(k p) c -> p k c", p=P)).then_inc(s_al[g], 16)
                        sp.dma_start(att[g][0:REST, r, :], attr[FULL * P:N, :]).then_inc(s_al[g], 16)
                    else:
                        sp.dma_start(att[g], attr[bass.ds(n * (Q * P), Q * P), :].rearrange("(k p) c -> p k c", p=P)).then_inc(s_al[g], 16)
                    sp.dma_start(vse[g], srcemb[:, bass.ds(n * (Q * GE), Q * GE)].rearrange("p (k c) -> p k c", k=Q)).then_inc(s_al[g], 16)
                    sp.dma_start(drow[g], rows_d[1][bass.ds(n * (Q * P), Q * P)].partition_broadcast(P)).then_inc(s_al[g], 16)
            for g in range(2):
                sp.wait_ge(s_vs[g], 16 * IT)
            load1(0)
            with sp.Fori(1, IT - 1) as it:
                load1(it)
            load1(IT - 1, True)

            for k in range(U):
                sp.wait_ge(s_sc[k], 16 * IT)

            def load_a(c, s):
                wait(sp, s_agg, c - 1)
                for k in range(TABLES):
                    sp.dma_start(aload[s][k], aggv[k][:, bass.ds(c * (CH * C1), CH * C1)]).then_inc(s_ld[s], 16)

            def store_a(c, s):
                sp.wait_ge(s_n1, c * 1 + 1)
                sp.dma_start(tab2v[:, bass.ds(c * CH, CH), :], stg[s].rearrange("p j b c -> p j (b c)")).then_inc(s_t2[s], 16)
            load_a(0, 0)
            load_a(1, 1)
            with sp.Fori(0, NC // 2 - 1) as q:
                load_a(q * 2 + 2, 0)
                load_a(q * 2 + 3, 1)
                store_a(q * 2, 0)
                store_a(q * 2 + 1, 1)
            store_a(NC - 2, 0)
            store_a(NC - 1, 1)

            residual(1)

            def out2(it):
                sp.wait_ge(s_n2, it * 1 + 1)
                sp.dma_start(tab3v[:, bass.ds(it * U, U), :], stg[0][:, 0:U].rearrange("p j b c -> p j (b c)")).then_inc(s_t3, 16)
            turns(sp, IT, out2)

            residual(2)

            def out3(c):
                sp.wait_ge(s_n3, c * 1 + 1)
                sp.dma_start(out[bass.ds(c * (CH * P), CH * P), :].rearrange("(j p) c -> p j c", p=P),
                             X[:, bass.ds(c * CH, CH), :]).then_inc(s_out, 16)
            with sp.Fori(0, NC - 1) as c:
                out3(c)
            sp.wait_ge(s_n3, NC)
            j = (NC - 1) * CH
            sp.dma_start(out[j * P:FULL * P, :].rearrange("(j p) c -> p j c", p=P), X[:, j:FULL, :]).then_inc(s_out, 16)
            sp.dma_start(out[FULL * P:N, :], X[0:REST, FULL, :]).then_inc(s_out, 16)
            sp.wait_ge(s_out, 16 * (NC + 1))
            sp.wait_ge(s_t3, 16 * IT)

        @block.gpsimd
        def _(pool):
            own = Tally(s_pl)

            def link(ins):
                pool.wait_ge(s_pl, own.add(ins))

            def tick(v):
                if is_reg(v):
                    pool.sem_inc(s_tick)

            link(pool.memset(ident[:, :], 0.0))
            link(pool.affine_select(out=ident[:, :], in_=ident[:, :], compare_op=ALU.not_equal, fill=1.0,
                                    base=0, pattern=[[-1, P]], channel_multiplier=1))
            link(pool.memset(tril[:, :], 1.0))
            link(pool.affine_select(out=tril[:, :], in_=tril[:, :], compare_op=ALU.is_gt, fill=0.0,
                                    base=0, pattern=[[-1, P]], channel_multiplier=1))
            link(pool.iota(iota[:, :], [[1, W * P]], base=0, channel_multiplier=0, allow_small_or_imprecise_dtypes=True))
            link(pool.iota(pcol[:, 6:7], [[1, 1]], base=0, channel_multiplier=1, allow_small_or_imprecise_dtypes=True))
            link(pool.iota(trash, [[1, 1]], base=P * T, channel_multiplier=1, allow_small_or_imprecise_dtypes=True))
            pool.memset(ones[:, :], 1.0).then_inc(s_const, 1)

            def gathers(table, to, index, it, g, free):
                free()
                pool.tensor_copy(idx[:, g, :], index[:, bass.ds(it * U + g * Q, Q)]).then_inc(s_pl, 1)
                own.k += 1
                pool.wait_ge(s_pl, own.value())
                tick(it)
                for k in range(Q):
                    pool.indirect_dma_start(to(g * Q + k), None, table[:, :],
                                            bass.IndirectOffsetOnAxis(ap=idx[:, g, k:k + 1], axis=0)).then_inc(s_ga[g * Q + k], 16)

            def residual(r, table):
                pool.wait_ge(s_flag, 3)
                more = pool.value_load(flag[0:1, 0:1], min_val=0, max_val=T * P)
                with pool.If(more > 0):
                    for g in range(2):
                        pool.wait_ge(s_vs[g], 16 * IT)
                    pool.wait_ge(r_go, r + 1)
                    pool.wait_ge(r_init, 16 * (NC + 1) * (r + 1))

                    def body(i):
                        n = i + T * r
                        wait(pool, r_sc, n * 16)
                        pool.tensor_copy(idx[:, 0, 0:1], gsrc[:, bass.ds(i, 1)]).then_inc(r_pl, 1)
                        pool.wait_ge(r_pl, n + 1)
                        tick(i)
                        to = gat[:, 0, 0:K0] if r == 0 else gatb[:, 0].rearrange("p b c -> p (b c)")
                        pool.indirect_dma_start(to, None, table[:, :],
                                                bass.IndirectOffsetOnAxis(ap=idx[:, 0, 0:1], axis=0)).then_inc(r_x, 16)
                        pool.wait_ge(r_ix, n + 1)
                        tick(i)
                        pool.indirect_dma_start(rst, None, states[:, :],
                                                bass.IndirectOffsetOnAxis(ap=idx[:, 1, 0:1], axis=0)).then_inc(r_st, 16)
                        pool.wait_ge(r_new, n + 1)
                        tick(i)
                        pool.indirect_dma_start(states[:, :], bass.IndirectOffsetOnAxis(ap=idxs[:, 0, 0:1], axis=0),
                                                rnew, None).then_inc(r_sc, 16)
                    turns(pool, T, body)

            pool.wait_ge(s_prep, 1)
            pool.wait_ge(s_zs[0], 32 * (IT // 2 + 1))
            pool.wait_ge(s_zs[1], 32 * (IT // 2))

            def free0(it, g):
                n = it * 2 + g
                if is_reg(it) or it > 0:
                    pool.wait_ge(s_vs[g], it * 16)
                    pool.wait_ge(s_sc0, n * 4 - 4)
                    for k in range(Q):
                        pool.wait_ge(s_ga[g * Q + k], it * 16)
                    tick(it)

            def body0(it):
                own.turn(it, 2)
                for g in range(2):
                    gathers(tab0, lambda k: gat[:, k, 0:K0], gsrc, it, g, lambda: free0(it, g))
            turns(pool, IT, body0)
            own.close(IT)
            residual(0, tab0)

            pool.wait_ge(s_t1, 16 * NC)
            pool.wait_ge(s_zero, 16 * TABLES * (IT + 1))

            def free1(it, g):
                n = it * 2 + g
                if is_reg(it) or it > 0:
                    pool.wait_ge(s_ms, n * 1 - 1)
                    for k in range(Q):
                        pool.wait_ge(s_ga[g * Q + k], it * 16 + 16 * IT)
                    tick(it)

            def scatter(it, g):
                n = it * 2 + g
                pool.wait_ge(s_oc, n * 2 + 1)
                pool.wait_ge(s_sx, n * 1 + 1)
                for k in range(Q):
                    wait(pool, s_sc[(1 - g) * Q + k], it * 16 + 16 * g)
                tick(it)
                for k in range(Q):
                    if k == Q // 2:
                        pool.wait_ge(s_oc, n * 2 + 2)
                        tick(it)
                    pool.indirect_dma_start(aggs[k][:, :], bass.IndirectOffsetOnAxis(ap=idxs[:, g, k:k + 1], axis=0),
                                            osum[g][:, k, :], None, compute_op=ALU.add).then_inc(s_sc[g * Q + k], 16)

            def body1(it, last=False):
                own.turn(it, 2)
                own.k = 1
                gathers(tab1, lambda k: gat[:, k, :], gdst, it, 1, lambda: free1(it, 1))
                scatter(it, 0)
                if not last:
                    own.turn(it + 1, 2)
                    gathers(tab1, lambda k: gat[:, k, :], gdst, it + 1, 0, lambda: free1(it + 1, 0))
                scatter(it, 1)
            own.turn(0, 2)
            gathers(tab1, lambda k: gat[:, k, :], gdst, 0, 0, lambda: None)
            body1(0)
            with pool.Fori(1, IT - 1) as it:
                body1(it)
            body1(IT - 1, True)
            own.close(IT)

            for layer in range(2):
                if layer == 0:
                    pool.wait_ge(s_t2[0], 16 * (NC // 2))
                    pool.wait_ge(s_t2[1], 16 * (NC // 2))
                else:
                    pool.wait_ge(s_t3, 16 * IT)

                def free2(it, g):
                    n = it * 2 + g
                    if is_reg(it) or it > 0:
                        pool.wait_ge(s_mm2[layer], n * 1 - 1)
                        for k in range(Q):
                            pool.wait_ge(s_ga[g * Q + k], it * 16 + 16 * IT * (2 + layer))
                        tick(it)

                def body2(it):
                    own.turn(it, 2)
                    for g in range(2):
                        gathers((tab2, tab3)[layer], lambda k: gatb[:, k].rearrange("p b c -> p (b c)"), gsrc, it, g, lambda: free2(it, g))
                turns(pool, IT, body2)
                own.close(IT)
                residual(1 + layer, (tab2, tab3)[layer])

        @block.scalar
        def _(act):
            def tick(v):
                if is_reg(v):
                    act.sem_inc(s_tick)

            def emb_out(m, s):
                act.wait_ge(s_zm, m * 1 + 1)
                if is_reg(m) or m > 1:
                    act.wait_ge(s_zs[s], 16 * (m - s))
                ps = psum[:, s, :].rearrange("p (t c) -> p t c", c=2 * GE)
                act.copy(st0[s][:, :, H:K0], ps[:, :, 0:GE])
                act.copy(stu[s][:, :, 0:GE], ps[:, :, GE:2 * GE]).then_inc(s_ze, 1)
            emb_out(0, 0)
            emb_out(1, 1)
            with act.Fori(1, IT // 2) as q:
                emb_out(q * 2, 0)
                emb_out(q * 2 + 1, 1)
            emb_out(IT - 1, 0)
            act.wait_ge(s_ask, 1)
            act.activation(tmpc[:, :], tmpd[:, :], ACT.Sin, bias=halfpi, scale=-PI / 6.0).then_inc(s_ans, 1)

            def residual(r):
                act.wait_ge(s_flag, 3)
                more = act.value_load(flag[0:1, 0:1], min_val=0, max_val=T * P)
                if r:
                    return
                with act.If(more > 0):
                    def body(i):
                        act.wait_ge(r_lm, i + 1)
                        act.activation(rw[:, H:H + 1], rc[6], ACT.Exp).then_inc(r_ex, 1)
                        act.wait_ge(r_df, i + 1)
                        act.activation(rd2, rd2, ACT.Exp).then_inc(r_dx, 1)
                    turns(act, T, body)

                    def merge(c):
                        act.wait_ge(r_mf, c + 1)
                        act.activation(rdf, rdf, ACT.Exp).then_inc(r_mx, 1)
                    turns(act, NC, merge)

            def keys0(it, g):
                n = it * 2 + g
                act.wait_ge(s_rl[g], it * 32 + 32)
                wait(act, s_rdone, n - 1)
                tick(it)
                for k in range(Q):
                    act.activation(keyd[g][:, k, :], drow[g][:, k * P:(k + 1) * P], ACT.Abs,
                                   bias=dcol[:, bass.ds(it * U + g * Q + k, 1)], scale=KEY).then_inc(s_key, 1)

            def factors0(it, g, W):
                act.wait_ge(s_df, it * 2 + g + 1)
                d = dif[:, g, :, 0:Q * W]
                n = (it * 2 + g) * 3
                act.activation(d[:, 1], d[:, 0], ACT.Relu).then_inc(s_dx, 1)
                act.wait_ge(s_dx, n + 1)
                act.activation(d[:, 0], d[:, 0], ACT.Relu, scale=-1.0).then_inc(s_dx, 1)
                act.wait_ge(s_dx, n + 2)
                act.activation(d, d, ACT.Exp, scale=-1.0).then_inc(s_dx, 1)

            def group0(it, g, W, after):
                n = it * 2 + g
                act.wait_ge(s_edge, n * 1 + 1)
                wait(act, s_par, n - 1)
                tick(it)
                act.activation(wrow[:, g * Q:(g + 1) * Q, H], lm[:, g, :], ACT.Exp).then_inc(s_wr, 1)
                act.wait_ge(s_wr, n * 1 + 1)
                for k in range(g * Q, (g + 1) * Q):
                    act.wait_ge(s_ga[k], it * 16 + 16)
                    act.mul(wrow[:, k, 0:H], gat[:, k, 0:H], wrow[:, k, H:H + 1]).then_inc(s_sc0, 1)
                act.wait_ge(s_sc0, n * Q + Q)
                wait(act, s_mm, n - 1)
                act.copy(wpar[:, g * Q:(g + 1) * Q, 0, :], wrow[:, g * Q:(g + 1) * Q, :]).then_inc(s_hi, 1)
                if g:
                    factors0(it, 0, W)
                elif is_reg(it) or it > 0:
                    factors0(it - 1, 1, W if before[0] is None else before[0])
                if after is not None:
                    keys0(it + 1, g)

            before = [None]

            def body0(it, w, after):
                before[0] = next((SEGS[n - 1][2] for n, (a, _, _) in enumerate(SEGS) if n and not is_reg(it) and a == it), None)
                group0(it, 0, w, after)
                group0(it, 1, w, after)
            keys0(0, 0)
            keys0(0, 1)
            segments(act, body0)
            factors0(IT - 1, 1, SEGS[-1][2])
            residual(0)

            def norm(y, sq, sm, c, n=CH):
                act.wait_ge(s_cen, c + 1)
                act.activation(sq[:, 0:n * H], y[:, 0:n * H], ACT.Square).then_inc(s_sq, 1)
                act.wait_ge(s_var, c + 1)
                act.activation(sm[2][:, 0:n], sm[1][:, 0:n], ACT.Sqrt, bias=epsc, scale=1.0 / H).then_inc(s_std, 1)

            def nodes0(q, exps=True, norms=True):
                for s in range(2 if exps else 0):
                    c = q * 2 + s
                    act.wait_ge(s_y0, c + 1)
                    act.activation(exps0[s], mean0[s], ACT.Relu, scale=-1.0).then_inc(s_e0, 1)
                    act.wait_ge(s_e0, c * 2 + 1)
                    act.activation(exps0[s], exps0[s], ACT.Exp, scale=-1.0).then_inc(s_e0, 1)
                if norms:
                    norms2(q * 2 - 2, q * 2 - 1, sums0)

            def norms2(a, b, sums=sums):
                act.wait_ge(s_cen, a + 1)
                act.activation(sqrs[0], rows_[0], ACT.Square).then_inc(s_sq, 1)
                act.wait_ge(s_cen, b + 1)
                act.activation(sqrs[1], rows_[1], ACT.Square).then_inc(s_sq, 1)
                for sm, c in zip(sums, (a, b)):
                    act.wait_ge(s_var, c + 1)
                    act.activation(sm[2], sm[1], ACT.Sqrt, bias=epsc, scale=1.0 / H).then_inc(s_std, 1)
            nodes0(0, norms=False)
            with act.Fori(1, NC // 2) as q:
                nodes0(q)
            nodes0(NC // 2, exps=False)

            asked = Tally(s_ask)
            asked.base = 1

            def answer(o_, i_, f, **kw):
                asked.k += 1
                act.wait_ge(s_ask, asked.value())
                act.activation(o_, i_, f, **kw).then_inc(s_ans, 1)

            def gate1(it, g):
                n = it * 2 + g
                act.wait_ge(s_at, n * 1 + 1)
                act.copy(attT[g], psum[0:R, g, :]).then_inc(s_ac, 1)
                act.wait_ge(s_hd, n * 1 + 1)
                act.activation(hid[g][0:H, :], psum[0:H, 2 + g, :], ACT.Silu, bias=b1c).then_inc(s_si, 1)

            def sums1(it, g):
                n = it * 2 + g
                act.wait_ge(s_os, n * 2 + 1)
                if is_reg(it) or it > 0:
                    for k in range(Q):
                        act.wait_ge(s_sc[g * Q + k], it * 16)
                for h in range(2):
                    if h:
                        act.wait_ge(s_os, n * 2 + 2)
                    act.copy(osum[g][:, h * (Q // 2):(h + 1) * (Q // 2)], psum[:, 6 * (1 - h) + g, 0:Q // 2 * C1].rearrange(
                        "p (k c) -> p k c", k=Q // 2)).then_inc(s_oc, 1)

            def body1(it):
                gate1(it, 1)
                sums1(it, 0)
                if is_reg(it) or it < IT - 1:
                    gate1(it + 1, 0)
                sums1(it, 1)
            act.wait_ge(s_acz, 2)
            gate1(0, 0)
            turns(act, IT, body1)

            def nodes1(q):
                c = q * 2
                for s in range(2):
                    act.wait_ge(s_deg, c + s + 1)
                    act.activation(sums[s][5], sums[s][4], ACT.Sqrt).then_inc(s_dst, 1)
                norms2(c * 2 + NC, c * 2 + NC + 1)
                norms2(c * 2 + NC + 2, c * 2 + NC + 3)
                for s in range(2):
                    act.wait_ge(s_pa, c + s + 1)
                    if is_reg(q) or q > 0:
                        act.wait_ge(s_t2[s], q * 16)
                    act.copy(stg[s][:, :, 0, :], v3(rows_[s])).then_inc(s_pb, 1)
                for s in range(2):
                    act.wait_ge(s_pc, c + s + 1)
                    act.copy(stg[s][:, :, 1, :], v3(rows_[s])).then_inc(s_pd, 1)

            def v3(b, n=CH):
                return b[:, 0:n * H].rearrange("p (j c) -> p j c", c=H)
            turns(act, NC // 2, nodes1)

            residual(1)
            answer(cj, tbuf[:, 0:T], ACT.Sqrt)
            answer(smax[:, 0:T], tbuf[:, 0:T], ACT.Sqrt)
            asked.base, asked.k = asked.base + asked.k, 0

            def nodes2(i):
                js = bass.ds((i - 2) * U, U)
                if in2(i - 2):
                    act.wait_ge(s_pa, i + NC - 1)
                    wait(act, s_t3, (i - 2) * 16)
                    tick(i)
                    act.copy(stg[0][:, 0:U, 0, :], acc[:, js, :]).then_inc(s_pb, 1)
                if in2(i + 1):
                    act.wait_ge(s_ntp, i + 2)
                    wait(act, s_nmm, i + 1)
                    act.copy(hT[0:2 * H, :], psum[0:2 * H, 0, :]).then_inc(s_ncp, 1)
                if in2(i - 2):
                    act.wait_ge(s_pc, i + NC - 1)
                    act.copy(stg[0][:, 0:U, 1, :], v3(pbuf, U)).then_inc(s_pd, 1)
                if in2(i - 1):
                    act.wait_ge(s_ntp2, i)
                    wait(act, s_nmm2, i - 1)
                    act.copy(hT2, psum[0:2 * H, 2, :]).then_inc(s_ncp2, 1)
                if in2(i):
                    norm(n2buf, sbuf_, sums[0], i + 3 * NC, U)
                    act.wait_ge(s_na2, i + 1)
                    tick(i)
                    act.copy(X[:, bass.ds(i * U, U), :], v3(x2buf, U)).then_inc(s_nx, 1)
            pipeline(act, nodes2)

            def squares3(q):
                for s in range(2):
                    c = q * 2 + s
                    act.wait_ge(s_bs, c + 1 + NC)
                    if is_reg(q) or q > 0:
                        act.wait_ge(s_bm, c - 1 + NC)
                    tick(c)
                    act.activation(v3(sqrs[s]), acc[:, bass.ds(c * CH, CH), :], ACT.Square).then_inc(s_bq, 1)
            turns(act, NC // 2, squares3)
            answer(ybuf[:, 0:H], tbuf[:, 0:H], ACT.Sqrt, bias=epsc, scale=1.0 / N)

            def nodes3(q):
                norms2(q * 2 + 3 * NC + IT, q * 2 + 3 * NC + IT + 1)
            turns(act, NC // 2, nodes3)

        @block.tensor
        def _(pe):
            tile = [slice(k * P, (k + 1) * P) for k in range(U)]

            def tick(v):
                if is_reg(v):
                    pe.sem_inc(s_tick)

            def residual(r):
                pe.wait_ge(s_flag, 3)
                more = pe.value_load(flag[0:1, 0:1], min_val=0, max_val=T * P)
                with pe.If(more > 0):
                    def body(i):
                        n = i + T * r
                        pe.wait_ge(r_q, n + 1)
                        tick(i)
                        mm = pe.matmul(psum[:, 0, 0:P], ones[:, :], rdk, start=True, stop=True)
                        if r == 0:
                            mm = pe.matmul(psum[:, 0, P:2 * P], ones[:, :], rdl, start=True, stop=True)
                        mm.then_inc(r_bk, 1)
                        pe.wait_ge(r_w, n + 1)
                        tick(i)
                        pe.matmul(psum[:, 1, 0:CR - 2], req, rw[:, 0:CR - 2], start=True, stop=True).then_inc(r_mm, 1)
                    turns(pe, T, body)

            pe.wait_ge(s_const, 1)
            pe.wait_ge(s_w, 16 * 16)
            pe.transpose(psum[0:R, 0, 0:H], w1raw, ident[0:H, 0:H])
            pe.transpose(psum[0:H, 0, 64:64 + H], w2raw, ident[0:H, 0:H])
            pe.transpose(psum[0:H, 0, 128:128 + H], l2raw, ident[0:H, 0:H])
            pe.transpose(psum[0:GE, 0, 192:192 + GE], adraw, ident[0:GE, 0:GE])
            pe.transpose(psum[0:GE, 0, 256:256 + NEL], EU[:, 0:GE], ident[0:NEL, 0:NEL])
            pe.transpose(psum[0:H, 0, 400:401], b1raw, ident[0:1, 0:1]).then_inc(s_tp, 1)
            pe.wait_ge(s_cp, 1)
            pe.matmul(psum[0:NEL, 0, 0:GE], embT, adT, start=True, stop=True).then_inc(s_tp, 1)
            pe.wait_ge(s_rowf, 1)
            for a in range(5):
                for b in range(4):
                    n = P if b < 3 else U
                    t = pe.transpose(psum[:, 1 + a, b * P:b * P + n], RF[0:n, a, b, :], ident[0:n, 0:n])
                t.then_inc(s_tp, 1)
            pe.wait_ge(s_cp, 7)
            pe.wait_ge(s_flag, 1)
            pe.matmul(psum[:, 6, 0:T], ones[0:1, :], tmpc[0:1, :], start=True, stop=True).then_inc(s_bb, 1)
            pe.wait_ge(s_flag, 2)
            pe.transpose(psum[0:1, 7, 0:P], flagr[:, :], ident[:, :]).then_inc(s_bb, 1)

            def emb_mm(m, s):
                pe.wait_ge(s_zo, m * 1 + 1)
                wait(pe, s_ze, m - 1)
                for k in range(U):
                    mm = pe.matmul(psum[:, s, k * 2 * GE:(k + 1) * 2 * GE], zoh[s][:, tile[k]], EU, start=True, stop=True)
                mm.then_inc(s_zm, 1)
            emb_mm(0, 0)
            emb_mm(1, 1)
            with pe.Fori(1, IT // 2) as q:
                emb_mm(q * 2, 0)
                emb_mm(q * 2 + 1, 1)
            emb_mm(IT - 1, 0)

            def group0(it, g, W):
                n = it * 2 + g
                wait(pe, s_cmb, n - 1)
                pe.wait_ge(s_oh, n * Q + Q)
                pe.wait_ge(s_edge, n * 1 + 1)
                for k in range(Q):
                    for w in range(W):
                        at = (k * W + w) * NS
                        pe.matmul(psum[:, 4 + g, at:at + NS], oneh[:, g * Q + k, tile[w]], wst[:, g * Q + k, 0:NS],
                                  start=True, stop=True)
                pe.wait_ge(s_par, n * 1 + 1)
                for k in range(Q):
                    for w in range(W):
                        at = ((k % 2) * W + w) * C0
                        for b in range(PARTS):
                            mm = pe.matmul(psum[:, 2 * g + k // 2, at:at + C0], oneh[:, g * Q + k, tile[w]],
                                           wpar[:, g * Q + k, b, :], start=b == 0, stop=b == PARTS - 1)
                mm.then_inc(s_mm, 1)

            def body0(it, w, _):
                group0(it, 0, w)
                group0(it, 1, w)
            segments(pe, body0)
            residual(0)

            def hidden1(it, g):
                n = it * 2 + g
                pe.wait_ge(s_al[g], it * 48 + 48 if is_reg(it) or it < IT - 1 or g == 0 else it * 48 + 64)
                wait(pe, s_ac, n - 1)
                wait(pe, s_oc, n * 2 - 2)
                tick(it)
                for k in range(Q):
                    t = pe.transpose(psum[0:R, g, tile[k]], att[g][:, k, :], ident[:, :])
                t.then_inc(s_at, 1)
                pe.wait_ge(s_ac, n * 1 + 1)
                wait(pe, s_si, n - 1)
                tick(it)
                pe.matmul(psum[0:H, 2 + g, :], W1T, attT[g], start=True, stop=True).then_inc(s_hd, 1)

            def gates1(it, g):
                n = it * 2 + g
                pe.wait_ge(s_si, n * 1 + 1)
                wait(pe, s_ms, n - 1)
                for k in range(Q):
                    mm = pe.matmul(psum[:, 4 + g, k * H:(k + 1) * H], hid[g][:, tile[k]], W2T, start=True, stop=True)
                mm.then_inc(s_gt, 1)

            def equal1(it, g):
                n = it * 2 + g
                pe.wait_ge(s_ms, n * 1 + 1)
                pe.wait_ge(s_eq, n * 1 + 1)
                for k in range(Q):
                    h, at = k // 2, k % 2 * C1
                    mm = pe.matmul(psum[:, 6 * (1 - h) + g, at:at + C1], eqm[g][:, k, :], msg[g][:, k, :], start=True, stop=True)
                    if k % 2:
                        mm.then_inc(s_os, 1)

            def body1(it):
                hidden1(it, 1)
                equal1(it, 0)
                gates1(it, 1)
                if is_reg(it) or it < IT - 1:
                    hidden1(it + 1, 0)
                equal1(it, 1)
                if is_reg(it) or it < IT - 1:
                    gates1(it + 1, 0)
            pe.wait_ge(s_acz, 2)
            hidden1(0, 0)
            gates1(0, 0)
            turns(pe, IT, body1)

            def sum1(q):
                for s in range(2):
                    pe.wait_ge(s_ld[s], q * 64 + 64)
                    if is_reg(q) or q > 0:
                        pe.wait_ge(s_sum, q * 2 + s - 1)
                    tick(q)
                    for h in range(2):
                        half = slice(h * CH // 2 * C1, (h + 1) * CH // 2 * C1)
                        for k in range(TABLES):
                            mm = pe.matmul(psum[:, 2 * s + h, 0:CH // 2 * C1], ident[:, :], aload[s][k][:, half],
                                           start=k == 0, stop=k == TABLES - 1)
                    mm.then_inc(s_agg, 1)
            turns(pe, NC // 2, sum1)

            for layer in range(2):
                def group2(it, g, W):
                    n = it * 2 + g
                    wait(pe, s_cm2[layer], n - 1)
                    for k in range(Q):
                        pe.wait_ge(s_oh2[layer], it * U + g * Q + k + 1)
                        pe.wait_ge(s_ga[g * Q + k], it * 16 + 16 + 16 * IT * (2 + layer))
                        for w in range(W):
                            at = ((k % 2) * W + w) * C0
                            if layer == 0:
                                pe.matmul(psum[:, 2 * g + k // 2, at + H:at + C0], oneh[:, g * Q + k, tile[w]],
                                          oneb[:, 0:1], start=True, stop=True)
                            for b in range(PARTS):
                                mm = pe.matmul(psum[:, 2 * g + k // 2, at:at + H], oneh[:, g * Q + k, tile[w]],
                                               gatb[:, g * Q + k, b, :], start=b == 0, stop=b == PARTS - 1)
                    mm.then_inc(s_mm2[layer], 1)

                def body2(it, w, _):
                    group2(it, 0, w)
                    group2(it, 1, w)
                segments(pe, body2)
                residual(1 + layer)
                if layer:
                    break

                def flip(buf, bank, done):
                    for k in range(U // 2):
                        t = pe.transpose(psum[0:2 * H, bank, tile[k]], buf[:, 2 * k * H:2 * (k + 1) * H], ident[:, :])
                    t.then_inc(done, 1)

                def times(to, wgt, bank, done):
                    for k in range(U // 2):
                        mm = pe.matmul(psum[:, bank, 2 * k * H:2 * (k + 1) * H], to[:, tile[k]], wgt, start=True, stop=True)
                    mm.then_inc(done, 1)

                def nodes2(i):
                    if in2(i + 1):
                        pe.wait_ge(s_na, i + 2)
                        wait(pe, s_ncp, i + 1)
                        tick(i)
                        flip(r2buf, 0, s_ntp)
                    if in2(i - 1):
                        pe.wait_ge(s_na2, i)
                        wait(pe, s_ncp2, i - 1)
                        tick(i)
                        flip(x2buf, 2, s_ntp2)
                    if in2(i + 1):
                        pe.wait_ge(s_ncp, i + 2)
                        wait(pe, s_nrd, i + 1)
                        times(hT, L2BD, 4, s_nmm)
                    if in2(i - 1):
                        pe.wait_ge(s_ncp2, i)
                        wait(pe, s_nrd2, i - 1)
                        times(hT2, L3BD, 5, s_nmm2)
                pe.wait_ge(s_bd, 16)
                pipeline(pe, nodes2)

            def colsum(bank, c, rows, first=False, last=False):
                for h in range(2):
                    mm = pe.matmul(psum[:, bank, 0:NCOL // 2], ones[:, :], rows(h), start=first and h == 0,
                                   stop=last and h == 1)
                return mm

            def sums3(c):
                pe.wait_ge(s_bs, c + 1)
                tick(c)
                colsum(0, c, lambda h: acc[:, bass.ds(c * CH + h * (CH // 2), CH // 2), :],
                       not is_reg(c) and c == 0, not is_reg(c) and c == NC - 1).then_inc(s_bm, 1)
            turns(pe, NC, sums3)

            def squares3(q):
                for s in range(2):
                    c = q * 2 + s
                    pe.wait_ge(s_bq, c + 1)
                    colsum(1, c, lambda h: sqrs[s][:, h * NCOL // 2:(h + 1) * NCOL // 2],
                           not is_reg(c) and c == 0, not is_reg(c) and c == NC - 1).then_inc(s_bm, 1)
            turns(pe, NC // 2, squares3)

        @block.vector
        def _(dve):
            own = Own(dve, s_dv)
            V = nc.vector

            def link(ins):
                dve.wait_ge(s_dv, own.add(ins))

            def note(ins):
                own.add(ins)

            def tick(v):
                if is_reg(v):
                    dve.sem_inc(s_tick)

            def sync():
                dve.wait_ge(s_dv, own.value())

            note(V.memset(RI[:, :, 3, :], -1))
            note(V.memset(RF[:, 2:5, 3, :], 0.0))
            note(V.memset(W2T, 0.0))
            link(V.memset(bd[:, :], 0.0))
            V.memset(X[:, FULL:T, :], 0.0).then_inc(s_pad, 1)
            note(V.memset(zb[0], 0))
            note(V.memset(zb[1], 0))
            note(V.memset(zero[:, :], 0.0))
            note(V.memset(oneb[:, :], 1.0))
            note(V.memset(smax[:, :], -BIG))
            note(V.memset(halfpi, PI / 2.0))
            note(V.memset(epsc, EPS))
            note(V.memset(wst[:, :, NS - 1], 1.0))
            link(V.memset(valid, 0.0))
            V.memset(pcol[0:64, 4:5], 1.0).then_inc(s_pad, 1)
            note(V.memset(pcol[64:64 + REST - 64, 4:5], 1.0))
            dve.wait_ge(s_rows, 16 * 15)
            link(V.tensor_copy(RF[:, 0:2], RI))
            V.tensor_copy(flagf[:, 0:1], RF[0:1, 0, 0, 0:1]).then_inc(s_rowf, 1)
            dve.wait_ge(s_tp, 1)
            note(V.tensor_copy(W1T, psum[0:R, 0, 0:H]))
            note(V.tensor_copy(W2T[0:H, :], psum[0:H, 0, 64:64 + H]))
            note(V.tensor_copy(L2BD[0:H, 0:H], psum[0:H, 0, 128:128 + H]))
            note(V.tensor_copy(adT, psum[0:GE, 0, 192:192 + GE]))
            note(V.tensor_copy(b1c, psum[0:H, 0, 400:401]))
            V.tensor_copy(embT, psum[0:GE, 0, 256:256 + NEL]).then_inc(s_cp, 1)
            sync()
            dve.wait_ge(s_tp, 2)
            V.tensor_copy(EU[:, GE:2 * GE], psum[0:NEL, 0, 0:GE]).then_inc(s_cp, 1)
            for a in range(5):
                dve.wait_ge(s_tp, 3 + a)
                V.tensor_copy(cols[:, a, :], psum[:, 1 + a, 0:T]).then_inc(s_cp, 1)
            dve.wait_ge(s_cp, 7)
            link(V.tensor_scalar(tmpc[0:1, :], dcol[0:1, :], 0.0, float(N - 1), ALU.max, ALU.min))
            link(V.tensor_copy(tmpi[0:1, :], tmpc[0:1, :]))
            link(V.tensor_scalar(base[:, :], tmpi[0:1, :], 7, None, ALU.arith_shift_right))
            V.tensor_scalar(tmpc[0:1, :], base[:, :], float(P), None, ALU.mult).then_inc(s_flag, 1)
            dve.wait_ge(s_bb, 1)
            link(V.tensor_tensor(relc[:, :], dcol, psum[:, 6, 0:T], ALU.subtract))
            link(V.tensor_scalar(tmpc[:, :], relc[:, :], 0.0, None, ALU.is_ge))
            for a, b, w in SEGS:
                js = slice(a * U, b * U)
                note(V.scalar_tensor_tensor(tmpd[:, js], relc[:, js], float(w * P), tmpc[:, js], ALU.is_lt, ALU.mult))
            sync()
            link(V.tensor_scalar(tmpd[:, :], tmpd[:, :], -1.0, 1.0, ALU.mult, ALU.add))
            link(V.scalar_tensor_tensor(tmpc[:, :], dcol, 1.0, tmpd[:, :], ALU.add, ALU.mult))
            link(V.tensor_scalar(tmpr, tmpc[:, :], -1.0, None, ALU.add))
            V.tensor_reduce(flagr[:, :], tmpc[:, :], AX.X, ALU.max).then_inc(s_flag, 1)
            dve.wait_ge(s_bb, 2)
            link(V.tensor_reduce(flagf[:, 0:1], psum[0:1, 7, 0:P], AX.X, ALU.max))
            V.tensor_copy(flag[:, :], flagf[:, 0:1]).then_inc(s_flag, 1)
            for c_, to in ((scol, gsrc), (dcol, gdst)):
                link(V.tensor_scalar(tmpi[:, :], c_, 0.0, None, ALU.max))
                link(V.tensor_scalar(to[:, :], tmpi[:, :], 7, None, ALU.arith_shift_right))
                link(V.tensor_scalar(tmpi[:, :], tmpi[:, :], P - 1, None, ALU.bitwise_and))
                link(V.scalar_tensor_tensor(to[:, :], tmpi[:, :], float(T), to[:, :], ALU.mult, ALU.add))
            link(V.tensor_scalar(dcol, dcol, -KEY, None, ALU.mult))
            V.tensor_copy(tmpc[:, 0:1], dcol[:, 0:1]).then_inc(s_prep, 1)
            link(V.scalar_tensor_tensor(tmpd[:, :], ecol, -1.0, ecol, ALU.mult, ALU.max))
            V.tensor_scalar(tmpd[:, :], tmpd[:, :], 6.0, None, ALU.min).then_inc(s_ask, 1)

            def emb_oh(m, s):
                own.renew()
                dve.wait_ge(s_zl[s], 8 * (m - s) + 16)
                wait(dve, s_zm, m - 1)
                V.tensor_scalar(zoh[s], zb[s], pcol[0:NEL, 6:7], None, ALU.is_equal).then_inc(s_zo, 1)
                if is_reg(m) or m > 1:
                    dve.wait_ge(s_zs[s], 16 * (m - s))
                    if is_reg(m):
                        dve.sem_inc(s_tick)
                note(V.tensor_copy(st0[s][:, :, 0:H], X[:, bass.ds(m * U, U), :]))
                note(V.tensor_copy(stu[s][:, :, GE], mcol[:, bass.ds(m * U, U)]))
                own.renew()
                dve.sem_inc(s_zx)
            dve.wait_ge(s_x, 32)
            emb_oh(0, 0)
            emb_oh(1, 1)
            with dve.Fori(1, IT // 2) as q:
                emb_oh(q * 2, 0)
                emb_oh(q * 2 + 1, 1)
            emb_oh(IT - 1, 0)
            dve.wait_ge(s_ans, 1)
            link(V.tensor_scalar(tmpc[:, :], tmpc[:, :], 0.5, 0.5, ALU.mult, ALU.add))
            link(V.scalar_tensor_tensor(ecol, ecol, 6.0, tmpc[:, :], ALU.is_lt, ALU.mult))
            link(V.tensor_copy(resc, tmpr))
            dve.wait_ge(s_rowd, 96)
            dve.wait_ge(s_zs[0], 32 * (IT // 2 + 1))
            dve.wait_ge(s_zs[1], 32 * (IT // 2))
            note(V.memset(ACC[:, :], 0.0))
            sync()
            dve.sem_inc(s_acz)

            def residual(r):
                more = V.value_load(flag[0:1, 0:1], min_val=0, max_val=T * P)
                with dve.If(more > 0):
                    mine = Tally(r_dv)
                    sizes = [(23, 8), (14, 1), (14, 1)]
                    per, perm = sizes[r]
                    mine.base = sum(3 + a * T + b * NC for a, b in sizes[:r])

                    def link(ins):
                        dve.wait_ge(r_dv, mine.add(ins))
                    link(V.memset(rzero, 0.0))
                    link(V.memset(rzero.rearrange("p (j c) -> p j c", c=CR)[:, :, 50], -BIG))
                    link(V.memset(rw, 1.0))
                    dve.sem_inc(r_zero)
                    dve.sem_inc(r_go)

                    def body(i):
                        mine.turn(i, per)
                        n = i + T * r
                        one = bass.ds(i, 1)
                        key = resc[:, one]
                        wait(dve, r_sc, n * 16)
                        tick(i)
                        link(V.tensor_scalar(rc[0], key, 0.0, None, ALU.is_ge))
                        link(V.tensor_scalar(rc[1], gdst[:, one], trash, None, ALU.subtract))
                        link(V.tensor_tensor(rc[2], rc[0], rc[1], ALU.mult))
                        link(V.tensor_scalar(idx[:, 1, 0:1], rc[2], trash, None, ALU.add))
                        dve.sem_inc(r_ix)
                        link(V.tensor_scalar(rdk, ident[:, :], key, None, ALU.mult))
                        if r == 0:
                            link(V.tensor_scalar(rdl, ident[:, :], lcol[:, one], None, ALU.mult))
                        dve.sem_inc(r_q)
                        dve.wait_ge(r_bk, n + 1)
                        link(V.tensor_scalar(req, psum[:, 0, 0:P], key, None, ALU.is_equal))
                        link(V.tensor_tensor_reduce(out=rjunk, in0=req, in1=tril[:, :], scale=1.0, scalar=0.0,
                                                    op0=ALU.mult, op1=ALU.add, accum_out=rc[3]))
                        link(V.tensor_scalar(rc[4], rc[3], 0.0, None, ALU.is_equal))
                        link(V.tensor_tensor(rc[4], rc[4], rc[2], ALU.mult))
                        link(V.tensor_scalar(idxs[:, 0, 0:1], rc[4], trash, None, ALU.add))
                        dve.wait_ge(r_x, n * 16 + 16)
                        if r == 0:
                            link(V.tensor_scalar(rt1, psum[:, 0, 0:P], key, -BIG, ALU.not_equal, ALU.mult))
                            tick(i)
                            link(V.tensor_tensor_reduce(out=rjunk, in0=rt1, in1=psum[:, 0, P:2 * P], scale=1.0,
                                                        scalar=-BIG * 8, op0=ALU.add, op1=ALU.max, accum_out=rc[5]))
                            link(V.tensor_tensor(rc[6], lcol[:, one], rc[5], ALU.subtract))
                            dve.sem_inc(r_lm)
                            dve.wait_ge(r_ex, n + 1)
                            link(V.tensor_scalar(rw[:, 0:H], gat[:, 0, 0:H], rw[:, H:H + 1], None, ALU.mult))
                        else:
                            if is_reg(i):
                                tick(i)
                            link(V.tensor_tensor(rw[:, 0:H], gatb[:, 0, 0, :], gatb[:, 0, 1, :], ALU.add))
                            link(V.tensor_tensor(rw[:, 0:H], rw[:, 0:H], gatb[:, 0, 2, :], ALU.add))
                        dve.sem_inc(r_w)
                        dve.wait_ge(r_st, n * 16 + 16)
                        if r == 0:
                            link(V.tensor_tensor(rc[7], rst[:, 50:51], rc[5], ALU.max))
                            link(V.tensor_tensor(rd2[:, 0:1], rst[:, 50:51], rc[7], ALU.subtract))
                            link(V.tensor_tensor(rd2[:, 1:2], rc[5], rc[7], ALU.subtract))
                            dve.sem_inc(r_df)
                            dve.wait_ge(r_mm, n + 1)
                            link(V.tensor_tensor(rnew, rst, rst, ALU.max))
                            dve.wait_ge(r_dx, n + 1)
                            link(V.tensor_scalar(rs_[:, 0:C0], psum[:, 1, 0:C0], rd2[:, 1:2], None, ALU.mult))
                            link(V.tensor_scalar(rnew[:, 0:C0], rst[:, 0:C0], rd2[:, 0:1], None, ALU.mult))
                            link(V.tensor_tensor(rnew[:, 0:C0], rnew[:, 0:C0], rs_[:, 0:C0], ALU.add))
                            link(V.tensor_tensor(rnew[:, 50:51], rc[7], rc[7], ALU.max))
                        else:
                            dve.wait_ge(r_mm, n + 1)
                            link(V.tensor_tensor(rnew, rst, rst, ALU.max))
                            link(V.tensor_tensor(rnew[:, 0:C0], rst[:, 0:C0], psum[:, 1, 0:C0], ALU.add))
                        dve.sem_inc(r_new)
                        assert mine.k == per, (mine.k, per, r)
                    turns(dve, T, body)
                    mine.close(T)
                    ch = rchunk.rearrange("p (j c) -> p j c", c=CR)

                    def merge(c):
                        mine.turn(c, perm)
                        js = bass.ds(c * CH, CH)
                        dve.wait_ge(r_ld, (c + 1) * 16 + 16 * NC * r)
                        if r:
                            link(V.tensor_tensor(acc0[:, js, :], acc0[:, js, :], ch[:, :, 0:C0], ALU.add))
                        else:
                            mx = rzero[:, 0:CH]
                            link(V.tensor_tensor(mx, smax[:, js], ch[:, :, 50], ALU.max))
                            link(V.tensor_tensor(rdf[:, 0:CH], smax[:, js], mx, ALU.subtract))
                            link(V.tensor_tensor(rdf[:, CH:2 * CH], ch[:, :, 50], mx, ALU.subtract))
                            dve.sem_inc(r_mf)
                            dve.wait_ge(r_mx, c + 1)
                            link(V.tensor_tensor(ch[:, :, 0:C0], ch[:, :, 0:C0],
                                                 rdf[:, CH:2 * CH].unsqueeze(2).to_broadcast([P, CH, C0]), ALU.mult))
                            a = acc0[:, js, :]
                            link(V.tensor_tensor(a, a, rdf[:, 0:CH].unsqueeze(2).to_broadcast([P, CH, C0]), ALU.mult))
                            link(V.tensor_tensor(a, a, ch[:, :, 0:C0], ALU.add))
                            link(V.tensor_tensor(smax[:, js], mx, mx, ALU.max))
                            link(V.tensor_tensor(rd2[:, 0:1], rd2[:, 0:1], rd2[:, 0:1], ALU.max))
                        dve.sem_inc(r_use)
                        assert mine.k == perm, (mine.k, perm)
                    turns(dve, NC, merge)

            def bases(i, n):
                _, js = nc.values_load_multi_w_load_instructions(
                    base[0:1, bass.ds(i, n)], engines=[mybir.EngineType.DVE], min_val=0, max_val=T - 1,
                    skip_runtime_bounds_check_because="the preparation clamps the nodes that they come from to 0 .. N - 1")
                return list(js)

            def need(v):
                dve.wait_ge(s_dv, v)

            def onehot0(it, g, k, W):
                i = it * U + g * Q + k
                V.tensor_scalar(oneh[:, g * Q + k, 0:W * P], iota[:, 0:W * P], relc[:, bass.ds(i, 1)], None,
                                ALU.is_equal).then_inc(s_oh, 1)

            def maximum0(it, g, k):
                if k == 0:
                    dve.wait_ge(s_key, (it * 2 + g) * Q + Q)
                    tick(it)
                return own.add(V.tensor_tensor_reduce(
                    out=junk[:, k, :], in0=lrow[g][:, k * P:(k + 1) * P], in1=keyd[g][:, k, :], scale=1.0,
                    scalar=-BIG, op0=ALU.subtract, op1=ALU.max, accum_out=mloc[:, g, k:k + 1]))

            def edges0(it, g, v):
                st = wst[:, g * Q:(g + 1) * Q, :]
                need(v)
                dve.sem_inc(s_rdone)
                v = own.add(V.tensor_tensor(lm[:, g, :], lcol[:, bass.ds(it * U + g * Q, Q)], mloc[:, g, :], ALU.subtract))
                yield
                need(v)
                v = own.add(V.tensor_scalar(st[:, :, 3], lm[:, g, :], 0.0, None, ALU.is_equal))
                yield
                need(v)
                v = own.add(V.tensor_tensor(mf, mloc[:, g, :], st[:, :, 3], ALU.mult))
                yield
                need(v)
                v = own.add(V.tensor_scalar(st[:, :, 0], mf, 1.0, None, ALU.mult))
                yield
                need(v)
                v = own.add(V.tensor_tensor(mr, mf, st[:, :, 0], ALU.subtract))
                yield
                need(v)
                v = own.add(V.tensor_scalar(st[:, :, 1], mr, 1.0, None, ALU.mult))
                yield
                need(v)
                v = own.add(V.tensor_tensor(st[:, :, 2], mr, st[:, :, 1], ALU.subtract))
                yield
                need(v)
                dve.sem_inc(s_edge)

            def step0(it, g, W, nxt, prev, js):
                n = it * 2 + g
                last = own.value()
                if prev:
                    pit, pg, pW = prev
                    dve.wait_ge(s_mm, pit * 2 + pg + 1)
                    tick(it)
                    st = psum[:, 4 + pg, 0:Q * pW * NS].rearrange("p (k c) -> p k c", c=NS)
                    cd, ci, cp = cand[:, 0:Q * pW], cinv[:, 0:Q * pW], cpen[:, 0:Q * pW]
                    a = own.add(V.tensor_scalar(ci, st[:, :, 3], 1.0, None, ALU.max))
                    b = own.add(V.tensor_scalar(cd, st[:, :, 0], 1.0, None, ALU.mult))
                    c = own.add(V.tensor_scalar(cp, st[:, :, 3], 1.0, -1.0, ALU.min, ALU.add))
                    if nxt:
                        onehot0(*nxt[:2], 0, nxt[2])
                    need(c)
                    b = own.add(V.tensor_tensor(cd, cd, st[:, :, 1], ALU.add))
                    a = own.add(V.reciprocal(ci, ci))
                    if nxt:
                        onehot0(*nxt[:2], 1, nxt[2])
                    need(a)
                    b = own.add(V.tensor_tensor(cd, cd, st[:, :, 2], ALU.add))
                    if nxt:
                        onehot0(*nxt[:2], 2, nxt[2])
                    need(b)
                    b = own.add(V.tensor_tensor(cd, cd, ci, ALU.mult))
                    if nxt:
                        onehot0(*nxt[:2], 3, nxt[2])
                    need(b)
                    last = own.add(V.scalar_tensor_tensor(cd, cp, BIG, cd, ALU.mult, ALU.add))
                elif nxt:
                    for k in range(Q):
                        onehot0(*nxt[:2], k, nxt[2])
                v = 0
                for k in range(Q):
                    if nxt:
                        v = maximum0(*nxt[:2], k)
                    if prev:
                        need(last)
                        m = smax[:, bass.ds(js[k], pW)]
                        c_ = cand[:, k * pW:(k + 1) * pW]
                        own.add(V.tensor_tensor(dif[:, pg, 0, k * pW:(k + 1) * pW], m, c_, ALU.subtract))
                        last = own.add(V.tensor_tensor(m, m, c_, ALU.max))
                if prev:
                    d = dif[:, pg, :, 0:Q * pW]
                    need(last)
                    dve.sem_inc(s_df)
                edge = edges0(*nxt[:2], v) if nxt else iter(())
                hi = wpar[:, g * Q:(g + 1) * Q, :, :]
                wr = wrow[:, g * Q:(g + 1) * Q, :]
                next(edge, None)
                dve.wait_ge(s_hi, n * 1 + 1)
                a = own.add(V.tensor_tensor(rest, wr, hi[:, :, 0, :], ALU.subtract))
                if prev:
                    dve.wait_ge(s_dx, (pit * 2 + pg + 1) * 3)
                pr = []
                for h in range(2):
                    if prev:
                        pr.append(prod[h][:, 0:2 * pW * C0].rearrange("p (w c) -> p w c", c=C0))
                        ps = psum[:, 2 * pg + h, 0:2 * pW * C0].rearrange("p (w c) -> p w c", c=C0)
                        d1 = dif[:, pg, 1, h * 2 * pW:(h + 1) * 2 * pW].unsqueeze(2).to_broadcast([P, 2 * pW, C0])
                        last = own.add(V.tensor_tensor(pr[h], ps, d1, ALU.mult))
                    need(a)
                    if h == 0:
                        a = own.add(V.tensor_scalar(hi[:, :, 1, :], rest, 1.0, None, ALU.mult))
                    else:
                        V.tensor_tensor(hi[:, :, 2, :], rest, hi[:, :, 1, :], ALU.subtract).then_inc(s_par, 1)
                for k in range(Q if prev else 0):
                    ac = acc0[:, bass.ds(js[k], pW), :]
                    d0 = dif[:, pg, 0, k * pW:(k + 1) * pW].unsqueeze(2).to_broadcast([P, pW, C0])
                    need(last)
                    last = own.add(V.tensor_tensor(ac, ac, d0, ALU.mult))
                    next(edge, None)
                    need(last)
                    last = own.add(V.tensor_tensor(ac, ac, pr[k // 2][:, (k % 2) * pW:(k % 2 + 1) * pW, :], ALU.add))
                    next(edge, None)
                for _ in edge:
                    pass
                if prev:
                    need(last)
                    dve.sem_inc(s_cmb)

            def body0(it, w, after):
                first = not is_reg(it) and it == 0
                own.renew()
                if first:
                    before = None
                else:
                    bw = w if is_reg(it) else next((SEGS[n - 1][2] for n, (a, _, _) in enumerate(SEGS) if n and a == it), w)
                    before = (it - 1, 1, bw)
                js = bases(it * U - Q, 2 * Q) if before else [None] * Q + bases(0, Q)
                step0(it, 0, w, (it, 1, w), before, js[0:Q])
                step0(it, 1, w, (it + 1, 0, after) if after else None, (it, 0, w), js[Q:2 * Q])
                own.renew()
            for k in range(Q):
                onehot0(0, 0, k, SEGS[0][2])
            for k in range(Q):
                v = maximum0(0, 0, k)
            for _ in edges0(0, 0, v):
                pass
            own.renew()
            segments(dve, body0)
            pit, pg, pW = IT - 1, 1, SEGS[-1][2]
            js = bases(pit * U + pg * Q, Q)
            dve.wait_ge(s_mm, pit * 2 + pg + 1)
            st = psum[:, 4 + pg, 0:Q * pW * NS].rearrange("p (k c) -> p k c", c=NS)
            cd, ci, cp = cand[:, 0:Q * pW], cinv[:, 0:Q * pW], cpen[:, 0:Q * pW]
            link(V.tensor_scalar(ci, st[:, :, 3], 1.0, None, ALU.max))
            link(V.reciprocal(ci, ci))
            link(V.tensor_scalar(cp, st[:, :, 3], 1.0, -1.0, ALU.min, ALU.add))
            link(V.tensor_scalar(cd, st[:, :, 0], 1.0, None, ALU.mult))
            link(V.tensor_tensor(cd, cd, st[:, :, 1], ALU.add))
            link(V.tensor_tensor(cd, cd, st[:, :, 2], ALU.add))
            link(V.tensor_tensor(cd, cd, ci, ALU.mult))
            link(V.scalar_tensor_tensor(cd, cp, BIG, cd, ALU.mult, ALU.add))
            for k in range(Q):
                m = smax[:, bass.ds(js[k], pW)]
                c_ = cand[:, k * pW:(k + 1) * pW]
                note(V.tensor_tensor(dif[:, pg, 0, k * pW:(k + 1) * pW], m, c_, ALU.subtract))
                link(V.tensor_tensor(m, m, c_, ALU.max))
            d = dif[:, pg, :, 0:Q * pW]
            dve.sem_inc(s_df)
            dve.wait_ge(s_dx, 2 * IT * 3)
            pr = prod[0][:, 0:2 * pW * C0].rearrange("p (w c) -> p w c", c=C0)
            for h in range(2):
                ps = psum[:, 2 * pg + h, 0:2 * pW * C0].rearrange("p (w c) -> p w c", c=C0)
                link(V.tensor_tensor(pr, ps, d[:, 1, h * 2 * pW:(h + 1) * 2 * pW].unsqueeze(2).to_broadcast([P, 2 * pW, C0]), ALU.mult))
                for k in (2 * h, 2 * h + 1):
                    ac = acc0[:, bass.ds(js[k], pW), :]
                    link(V.tensor_tensor(ac, ac, d[:, 0, k * pW:(k + 1) * pW].unsqueeze(2).to_broadcast([P, pW, C0]), ALU.mult))
                    link(V.tensor_tensor(ac, ac, pr[:, (k % 2) * pW:(k % 2 + 1) * pW, :], ALU.add))
            residual(0)

            def v3(b, n=CH):
                return b[:, 0:n * H].rearrange("p (j c) -> p j c", c=H)

            def bc(v, n=CH):
                return v[:, 0:n].unsqueeze(2).to_broadcast([P, n, H])

            def vec(v, n=CH):
                return v.unsqueeze(1).to_broadcast([P, n, H])

            ans = Tally(s_ans)
            ans.base = 1

            def ask(ins):
                ins.then_inc(s_ask, 1)
                ans.k += 1
                dve.wait_ge(s_ans, ans.value())

            def norm(y, sq, sm, to, c, n=CH, free=None):
                own_ = own.add(V.tensor_reduce(sm[0][:, 0:n], v3(y, n), AX.X, ALU.add))
                yield
                need(own_)
                own_ = own.add(V.tensor_scalar(sm[0][:, 0:n], sm[0][:, 0:n], 1.0 / H, None, ALU.mult))
                yield
                need(own_)
                V.tensor_tensor(v3(y, n), v3(y, n), bc(sm[0], n), ALU.subtract).then_inc(s_cen, 1)
                yield
                dve.wait_ge(s_sq, c + 1)
                V.tensor_reduce(sm[1][:, 0:n], v3(sq, n), AX.X, ALU.add).then_inc(s_var, 1)
                yield
                dve.wait_ge(s_std, c + 1)
                own_ = own.add(V.reciprocal(sm[3][:, 0:n], sm[2][:, 0:n]))
                yield
                need(own_)
                if free:
                    free()
                own_ = own.add(V.tensor_tensor(to, v3(y, n), bc(sm[3], n), ALU.mult))
                yield
                need(own_)
            def step(ins):
                return own.add(ins)

            def elu0(c, s, norm_done):
                y, u, sm = mean0[s], exps0[s], sums0[s][4:]
                js = bass.ds(c * CH, CH)
                v = step(V.tensor_scalar(sm[0], acc0[:, js, H], 1e-30, None, ALU.max))
                yield
                need(v)
                v = step(V.reciprocal(sm[0], sm[0]))
                yield
                need(v)
                V.tensor_tensor(v3(y), acc0[:, js, 0:H], bc(sm[0]), ALU.mult).then_inc(s_y0, 1)
                yield
                dve.wait_ge(s_e0, c * 2 + 2)
                tick(c)
                v = step(V.scalar_tensor_tensor(v3(u), v3(u), -1.0, X[:, js, :], ALU.add, ALU.add))
                yield
                need(v)
                while norm_done and norm_done[0] < 2:
                    yield
                need(v)
                step(V.scalar_tensor_tensor(rows_[s], y, 0.0, u, ALU.max, ALU.add))

            def norm0(c, s, norm_done):
                yield from norm(rows_[s], sqrs[s], sums0[s], X[:, bass.ds(c * CH, CH), :], c)
                dve.sem_inc(s_n0)
                norm_done[0] += 1

            def nodes0(q, elu=True, norms=True):
                done = [0]
                if not norms:
                    together(elu0(0, 0, None), elu0(1, 1, None))
                elif elu:
                    together(elu0(q * 2, 0, done), elu0(q * 2 + 1, 1, done),
                             norm0(q * 2 - 2, 0, done), norm0(q * 2 - 1, 1, done))
                else:
                    together(norm0(q * 2 - 2, 0, done), norm0(q * 2 - 1, 1, done))
                own.renew()
            for g in range(2):
                dve.wait_ge(s_vs[g], 16 * IT)
            dve.wait_ge(s_zero, 16 * TABLES * (IT + 1))
            nodes0(0, norms=False)
            with dve.Fori(1, NC // 2) as q:
                nodes0(q)
            nodes0(NC // 2, elu=False)

            link(V.tensor_scalar(dtra, gsrc[:, :], trash, None, ALU.subtract))
            note(V.scalar_tensor_tensor(dtra, scol, 0.0, dtra, ALU.is_ge, ALU.mult))
            note(V.memset(hid[0], 1.0))
            note(V.memset(hid[1], 1.0))
            for g in range(2):
                note(V.memset(msg[g][:, :, H + 1], 1.0))
            sync()
            dve.sem_inc(s_acz)

            def group1(it, g):
                n = it * 2 + g
                sl = [slice(k * P, (k + 1) * P) for k in range(Q)]
                dve.wait_ge(s_al[g], it * 48 + 48 if is_reg(it) or it < IT - 1 or g == 0 else it * 48 + 64)
                wait(dve, s_os, n * 2 - 2)
                for k in range(Q):
                    i = it * U + g * Q + k
                    note(V.tensor_scalar(eqm[g][:, k, :], drow[g][:, sl[k]], scol[:, bass.ds(i, 1)], None, ALU.is_equal))
                sync()
                dve.sem_inc(s_eq)
                for k in range(Q):
                    link(V.tensor_tensor_reduce(out=junk1, in0=eqm[g][:, k, :], in1=tril[:, :], scale=1.0, scalar=0.0,
                                                op0=ALU.mult, op1=ALU.add, accum_out=rank[:, g, k:k + 1]))
                link(V.scalar_tensor_tensor(idf, rank[:, g, :], 0.0, dtra[:, bass.ds(it * U + g * Q, Q)], ALU.is_equal, ALU.mult))
                if is_reg(it) or it > 0:
                    for k in range(Q):
                        dve.wait_ge(s_sc[g * Q + k], it * 16)
                V.tensor_scalar(idxs[:, g, :], idf, trash, None, ALU.add).then_inc(s_sx, 1)
                gg = gat[:, g * Q:(g + 1) * Q, :]
                for k in range(Q):
                    dve.wait_ge(s_ga[g * Q + k], it * 16 + 16 + 16 * IT)
                if is_reg(it):
                    dve.sem_inc(s_tick)
                note(V.tensor_tensor(qmu, ecol[:, bass.ds(it * U + g * Q, Q)], gg[:, :, H + GE], ALU.mult))
                link(V.tensor_tensor(uv, gg[:, :, H:H + GE], vse[g], ALU.mult))
                link(V.tensor_reduce(adp, uv, AX.X, ALU.add))
                dve.sem_inc(s_rs)
                dve.wait_ge(s_gt, n * 1 + 1)
                link(V.tensor_tensor(m1, psum[:, 4 + g, 0:Q * H].rearrange("p (k c) -> p k c", k=Q),
                                     adp.unsqueeze(2).to_broadcast([P, Q, H]), ALU.add))
                link(V.tensor_tensor(m2, m1, gg[:, :, 0:H], ALU.mult))
                note(V.tensor_copy(msg[g][:, :, H], gg[:, :, H + GE]))
                link(V.tensor_tensor(msg[g][:, :, 0:H], m2, qmu.unsqueeze(2).to_broadcast([P, Q, H]), ALU.mult))
                dve.sem_inc(s_ms)

            def body1(it):
                own.renew()
                group1(it, 0)
                group1(it, 1)
                own.renew()
            turns(dve, IT, body1)

            def chain1(q, s):
                c = q * 2 + s
                y, sq, sm = rows_[s], sqrs[s], sums[s]
                js = bass.ds(c * CH, CH)
                t = psum[:, 2 * s:2 * s + 2, 0:CH // 2 * C1].rearrange("p h (j c) -> p h j c", c=C1)

                def halves(v):
                    return v.rearrange("p (h j) -> p h j", h=2)
                dve.wait_ge(s_agg, c + 1)
                V.tensor_scalar(halves(sm[4]), t[:, :, :, H + 1], 1.0, None, ALU.max).then_inc(s_deg, 1)
                v = step(V.tensor_scalar(halves(sm[0]), t[:, :, :, H], 1e-8, None, ALU.max))
                yield
                need(v)
                v = step(V.reciprocal(sm[0], sm[0]))
                yield
                need(v)
                v = step(V.tensor_tensor(y.rearrange("p (h j c) -> p h j c", h=2, c=H), t[:, :, :, 0:H],
                                         halves(sm[0]).unsqueeze(3).to_broadcast([P, 2, CH // 2, H]), ALU.mult))
                yield
                need(v)
                dve.sem_inc(s_sum)
                v = step(V.tensor_tensor(v3(y), v3(y), X[:, js, :], ALU.add))
                yield
                dve.wait_ge(s_dst, c + 1)
                need(step(V.reciprocal(sm[5], sm[5])))
                need(v)
                yield from norm(y, sq, sm, v3(y), q * 4 + NC + s)
                v = step(V.tensor_tensor(v3(y), v3(y), vec(vecs[0]), ALU.mult))
                yield
                need(v)
                v = step(V.tensor_tensor(v3(y), v3(y), vec(vecs[1]), ALU.add))
                yield
                need(v)
                v = step(V.tensor_tensor(v3(y), v3(y), X[:, js, :], ALU.add))
                yield
                need(v)
                yield from norm(y, sq, sm, X[:, js, :], q * 4 + NC + 2 + s)
                V.tensor_tensor(v3(y), X[:, js, :], bc(sm[5]), ALU.mult).then_inc(s_pa, 1)
                yield
                dve.wait_ge(s_pb, c + 1)
                V.tensor_tensor(v3(y), v3(y), stg[s][:, :, 0, :], ALU.subtract).then_inc(s_pc, 1)
                yield
                dve.wait_ge(s_pd, c + 1)
                V.tensor_tensor(stg[s][:, :, 2, :], v3(y), stg[s][:, :, 1, :], ALU.subtract).then_inc(s_n1, 1)

            def nodes1(q):
                own.renew()
                together(chain1(q, 0), chain1(q, 1))
                own.renew()
            turns(dve, NC // 2, nodes1)
            link(V.memset(ACC[:, :], 0.0))
            for s in range(2):
                dve.wait_ge(s_t2[s], 16 * (NC // 2))

            def edges(layer):
                def produce(it, g, W):
                    n = it * 2 + g
                    if is_reg(it) or it > 0:
                        dve.wait_ge(s_mm2[layer], n * 1 - 1)
                    for k in range(Q):
                        i = it * U + g * Q + k
                        V.tensor_scalar(oneh[:, g * Q + k, 0:W * P], iota[:, 0:W * P], relc[:, bass.ds(i, 1)], None,
                                        ALU.is_equal).then_inc(s_oh2[layer], 1)

                def combine(it, g, W, js):
                    n = it * 2 + g
                    dve.wait_ge(s_mm2[layer], n * 1 + 1)
                    for k in range(Q):
                        C = C0 if layer == 0 else H
                        a = acc0[:, bass.ds(js[k], W), 0:C]
                        at = (k % 2) * W * C0
                        ps = psum[:, 2 * g + k // 2, at:at + W * C0].rearrange("p (w c) -> p w c", c=C0)[:, :, 0:C]
                        link(V.tensor_tensor(a, a, ps, ALU.add))
                    dve.sem_inc(s_cm2[layer])

                def body(it, w, after):
                    own.renew()
                    produce(it, 1, w)
                    js = bases(it * U, U)
                    combine(it, 0, w, js[0:Q])
                    if after is not None:
                        produce(it + 1, 0, after)
                    combine(it, 1, w, js[Q:U])
                    own.renew()
                produce(0, 0, SEGS[0][2])
                segments(dve, body)
                residual(1 + layer)

            edges(0)

            note(V.memset(hT, 1.0))
            note(V.memset(hT2, 1.0))
            sync()
            ask(V.tensor_scalar(tbuf[:, 0:T], acc0[:, 0:T, H], 1.0, None, ALU.max))
            link(V.reciprocal(cj, cj))
            ask(V.tensor_scalar(tbuf[:, 0:T], acc0[:, 0:T, H], 1.0, None, ALU.add))
            link(V.reciprocal(smax[:, 0:T], smax[:, 0:T]))
            ans.base, ans.k = ans.base + ans.k, 0

            def rows2(j):
                js = bass.ds(j * U, U)
                y, z = v3(r2buf, U), v3(zbuf2, U)
                v = step(V.tensor_scalar(sums[1][7][:, 0:U], acc0[:, js, H], 0.0, None, ALU.is_equal))
                yield
                need(v)
                v = step(V.tensor_tensor(z, X[:, js, :], bc(sums[1][7], U), ALU.mult))
                yield
                wait(dve, s_ntp, j)
                tick(j)
                need(step(V.tensor_tensor(y, acc[:, js, :], bc(cj[:, js], U), ALU.mult)))
                yield
                need(v)
                need(step(V.tensor_tensor(y, y, z, ALU.add)))
                dve.sem_inc(s_na)

            def table3(j):
                js = bass.ds(j * U, U)
                dve.wait_ge(s_nmm2, j + 1)
                ps = psum[:, 5, 0:U * H].rearrange("p (k c) -> p k c", k=U)
                v = step(V.tensor_tensor(acc[:, js, :], ps, bc(smax[:, js], U), ALU.mult))
                yield
                need(v)
                dve.sem_inc(s_nrd2)
                dve.sem_inc(s_pa)
                dve.wait_ge(s_pb, j + NC + 1)
                tick(j)
                V.tensor_tensor(v3(pbuf, U), acc[:, js, :], stg[0][:, 0:U, 0, :], ALU.subtract).then_inc(s_pc, 1)
                yield
                dve.wait_ge(s_pd, j + NC + 1)
                V.tensor_tensor(stg[0][:, 0:U, 2, :], v3(pbuf, U), stg[0][:, 0:U, 1, :], ALU.subtract).then_inc(s_n2, 1)

            def norm2(j):
                js = bass.ds(j * U, U)
                dve.wait_ge(s_nmm, j + 1)
                wait(dve, s_nx, j)
                tick(j)
                ps = psum[:, 4, 0:U * H].rearrange("p (k c) -> p k c", k=U)
                v = step(V.scalar_tensor_tensor(v3(n2buf, U), ps, 0.0, X[:, js, :], ALU.max, ALU.add))
                yield
                need(v)
                dve.sem_inc(s_nrd)
                yield from norm(n2buf, sbuf_, sums[0], v3(x2buf, U), j + 3 * NC, U,
                                free=lambda: wait(dve, s_ntp2, j))
                dve.sem_inc(s_na2)

            def nodes2(i):
                together(*([norm2(i)] if in2(i) else []), *([table3(i - 2)] if in2(i - 2) else []),
                         *([rows2(i + 2)] if in2(i + 2) else []))
                own.renew()
            own.renew()
            pipeline(dve, nodes2)
            dve.wait_ge(s_t3, 16 * IT)

            edges(1)

            def zero3(c, v):
                need(v)
                if not is_reg(c) and c == NC - 1:
                    note(V.tensor_scalar(acc[:, FULL, :], acc[:, FULL, :], valid, None, ALU.mult))
                    link(V.memset(acc[:, FULL + 1:T, :], 0.0))
                dve.sem_inc(s_bs)

            def scale3(c):
                a = acc[:, bass.ds(c * CH, CH), :]
                v = step(V.tensor_tensor(a, a, bc(smax[:, bass.ds(c * CH, CH)]), ALU.mult))
                yield
                need(v)
                v = step(V.tensor_tensor(a, a, vec(vecs[2]), ALU.add))
                yield
                zero3(c, v)

            def center3(c):
                a = acc[:, bass.ds(c * CH, CH), :]
                v = step(V.tensor_tensor(a, a, vec(mean3), ALU.subtract))
                yield
                zero3(c, v)

            def pairs3(chain):
                own.renew()
                with dve.Fori(0, NC // 2 - 1) as q:
                    together(chain(q * 2), chain(q * 2 + 1))
                    own.renew()
                together(chain(NC - 2), chain(NC - 1))
            pairs3(scale3)
            dve.wait_ge(s_bm, NC)
            link(V.tensor_reduce(mean3, psum[:, 0, 0:NCOL // 2].rearrange("p (j c) -> p c j", c=H), AX.X, ALU.add))
            link(V.tensor_scalar(mean3, mean3, 1.0 / N, None, ALU.mult))
            pairs3(center3)
            dve.wait_ge(s_bm, 2 * NC)
            ask(V.tensor_reduce(tbuf[:, 0:H], psum[:, 1, 0:NCOL // 2].rearrange("p (j c) -> p c j", c=H), AX.X, ALU.add))
            link(V.reciprocal(ubuf[:, 0:H], ybuf[:, 0:H]))
            link(V.tensor_tensor(vecs[3], vecs[3], ubuf[:, 0:H], ALU.mult))

            def chain3(c, s):
                js = bass.ds(c * CH, CH)
                y = v3(rows_[s])
                v = step(V.tensor_tensor(y, acc[:, js, :], vec(vecs[3]), ALU.mult))
                yield
                need(v)
                v = step(V.tensor_tensor(y, y, vec(vecs[4]), ALU.add))
                yield
                need(v)
                tick(c)
                v = step(V.scalar_tensor_tensor(y, y, 0.0, X[:, js, :], ALU.max, ALU.add))
                yield
                need(v)
                yield from norm(rows_[s], sqrs[s], sums[s], X[:, js, :], c + 3 * NC + IT)
                dve.sem_inc(s_n3)

            def nodes3(q):
                own.renew()
                together(chain3(q * 2, 0), chain3(q * 2 + 1, 1))
                own.renew()
            turns(dve, NC // 2, nodes3)


_INS = ['x', 'src', 'dst', 'edge_attr_40', 'edge_weight', 'edge_weight1', 'node_type_119', 'node_vec',
        'L1_gnn_W1', 'L1_gnn_b1', 'L1_gnn_W2', 'L1_gnn_b2', 'L1_gnn_emb', 'L1_gnn_adaptW', 'L1_gnn_gamma',
        'L1_gnn_beta', 'L2_gnn_W', 'L2_gnn_b', 'L3_gnn_W', 'L3_gnn_b', 'L3_gnn_gamma', 'L3_gnn_beta']


def kernel(**inputs):
    import numpy as _np
    import concourse.bacc as _bacc
    from concourse import mybir as _mybir
    from concourse.bass_utils import run_bass_kernel_spmd as _run

    nc = _bacc.Bacc("TRN2", target_bir_lowering=False, num_devices=1)
    arrays, args = {}, []
    for name in _INS:
        a = _np.ascontiguousarray(inputs[name])
        arrays[f"in_{name}_dram"] = a
        args.append(nc.dram_tensor(f"in_{name}_dram", a.shape, _mybir.dt.from_np(a.dtype), kind="ExternalInput").ap())
    args.append(nc.dram_tensor("out_0_dram", (N, H), F32, kind="ExternalOutput").ap())
    build(nc, *args)
    r = _run(nc, [arrays], core_ids=[0])
    return r.results[0]["out_0_dram"]
```
